# Optimizing a Trainium2 kernel written in Bass

```python
import numpy as np
import jax
import jax.numpy as jnp

def _softmax(x, axis=-1):
    return jax.nn.softmax(x, axis=axis)

def _gelu(x):
    return jax.nn.gelu(x, approximate=True)

def _silu(x):
    return jax.nn.silu(x)

def _sigmoid(x):
    return jax.nn.sigmoid(x)

def _layernorm(x, axis=-1, eps=1e-05):
    m = jnp.mean(x, axis=axis, keepdims=True)
    v = jnp.var(x, axis=axis, keepdims=True)
    return (x - m) / jnp.sqrt(v + eps)

def _scatter_add(tgt, idx, src, axis=0):
    return tgt.at[idx].add(src)

def _segment_sum(src, seg, n):
    return jax.ops.segment_sum(src, seg, n)
kernel_name = 'mk_hybrid_d1_jaxref_r8_64d692'

def setup_inputs(seed: int=0):
    np.random.seed(seed)
    _w = jnp.asarray

    def _L0_attn_a_setup():
        import jax, jax.numpy as jnp
        import numpy as np
        B, T, D, H = (4, 256, 128, 16)
        HD = D // H
        NEG = -np.finfo(np.float32).max
        key = jax.random.key(seed)
        ks = jax.random.split(key, 9)
        s = 1.0 / np.sqrt(D)
        return {'x': jax.random.normal(ks[0], (B, T, D), jnp.float32), 'wq': jax.random.normal(ks[1], (D, D), jnp.float32) * s, 'bq': jax.random.normal(ks[2], (D,), jnp.float32) * 0.02, 'wk': jax.random.normal(ks[3], (D, D), jnp.float32) * s, 'bk': jax.random.normal(ks[4], (D,), jnp.float32) * 0.02, 'wv': jax.random.normal(ks[5], (D, D), jnp.float32) * s, 'bv': jax.random.normal(ks[6], (D,), jnp.float32) * 0.02, 'wo': jax.random.normal(ks[7], (D, D), jnp.float32) * s, 'bo': jax.random.normal(ks[8], (D,), jnp.float32) * 0.02}
    _L0_attn_a_in = _L0_attn_a_setup()

    def _L0_attn_b_setup():
        import jax, jax.numpy as jnp
        import numpy as np
        ALPHA = 1.0
        N_HEADS = 16
        key = jax.random.key(seed)
        ks = jax.random.split(key, 3)
        B, N, D = (2, 256, 128)
        x = jax.random.normal(ks[0], (B, N, D), dtype=jnp.float32)
        W_qkv = jax.random.normal(ks[1], (D, 3 * D), dtype=jnp.float32) * D ** (-0.5)
        b_qkv = jnp.zeros((3 * D,), dtype=jnp.float32)
        W_proj = jax.random.normal(ks[2], (D, D), dtype=jnp.float32) * D ** (-0.5)
        b_proj = jnp.zeros((D,), dtype=jnp.float32)
        return {'x': x, 'W_qkv': W_qkv, 'b_qkv': b_qkv, 'W_proj': W_proj, 'b_proj': b_proj}
    _L0_attn_b_in = _L0_attn_b_setup()

    def _L0_ffn_setup():
        import jax, jax.numpy as jnp
        import numpy as np
        D_MODEL = 128
        HIDDEN = 512
        NUM_EXPERTS = 8
        TOP_K = 2
        DEPTH = 12
        DEPTH_SCALE = 1.0 / np.sqrt(DEPTH)
        key = jax.random.key(seed)
        k_x, k_r, k_g, k_u, k_d = jax.random.split(key, 5)
        s_in = 1.0 / np.sqrt(D_MODEL)
        s_hid = 1.0 / np.sqrt(HIDDEN)
        return {'x': jax.random.normal(k_x, (2, 256, D_MODEL), dtype=jnp.float32), 'Wr': jax.random.normal(k_r, (D_MODEL, NUM_EXPERTS), dtype=jnp.float32) * s_in, 'Wg': jax.random.normal(k_g, (NUM_EXPERTS, D_MODEL, HIDDEN), dtype=jnp.float32) * s_in, 'Wu': jax.random.normal(k_u, (NUM_EXPERTS, D_MODEL, HIDDEN), dtype=jnp.float32) * s_in, 'Wd': jax.random.normal(k_d, (NUM_EXPERTS, HIDDEN, D_MODEL), dtype=jnp.float32) * s_hid}
    _L0_ffn_in = _L0_ffn_setup()
    _d = {'L0_attn_a_x': _L0_attn_a_in['x'], 'L0_attn_a_wq': _L0_attn_a_in['wq'], 'L0_attn_a_bq': _L0_attn_a_in['bq'], 'L0_attn_a_wk': _L0_attn_a_in['wk'], 'L0_attn_a_bk': _L0_attn_a_in['bk'], 'L0_attn_a_wv': _L0_attn_a_in['wv'], 'L0_attn_a_bv': _L0_attn_a_in['bv'], 'L0_attn_a_wo': _L0_attn_a_in['wo'], 'L0_attn_a_bo': _L0_attn_a_in['bo'], 'L0_attn_b_W_qkv': _L0_attn_b_in['W_qkv'], 'L0_attn_b_b_qkv': _L0_attn_b_in['b_qkv'], 'L0_attn_b_W_proj': _L0_attn_b_in['W_proj'], 'L0_attn_b_b_proj': _L0_attn_b_in['b_proj'], 'L0_ffn_Wr': _L0_ffn_in['Wr'], 'L0_ffn_Wg': _L0_ffn_in['Wg'], 'L0_ffn_Wu': _L0_ffn_in['Wu'], 'L0_ffn_Wd': _L0_ffn_in['Wd']}
    _x0 = _d['L0_attn_a_x']
    _d['L0_attn_a_x'] = jax.random.normal(jax.random.fold_in(jax.random.key(seed), 1), (16, 256, 128), dtype=_x0.dtype)
    del _x0
    return _d

def reference(L0_attn_a_x, L0_attn_a_wq, L0_attn_a_bq, L0_attn_a_wk, L0_attn_a_bk, L0_attn_a_wv, L0_attn_a_bv, L0_attn_a_wo, L0_attn_a_bo, L0_attn_b_W_qkv, L0_attn_b_b_qkv, L0_attn_b_W_proj, L0_attn_b_b_proj, L0_ffn_Wr, L0_ffn_Wg, L0_ffn_Wu, L0_ffn_Wd):

    def _L0_attn_a_ref(x, wq, bq, wk, bk, wv, bv, wo, bo):
        import jax, jax.numpy as jnp
        import numpy as np
        B, T, D, H = (4, 256, 128, 16)
        HD = D // H
        NEG = -np.finfo(np.float32).max
        b, t, d = x.shape

        def proj(w, bias):
            y = x @ w + bias
            return y.reshape(b, t, H, HD).transpose(0, 2, 1, 3)
        q = proj(wq, bq)
        k = proj(wk, bk)
        v = proj(wv, bv)
        scale = 1.0 / np.sqrt(HD).astype(np.float32)
        scores = jnp.einsum('bhqd,bhkd->bhqk', q, k) * scale
        mask = jnp.triu(jnp.full((t, t), NEG, jnp.float32), k=1)
        attn = jax.nn.softmax(scores + mask, axis=-1)
        out = jnp.einsum('bhqk,bhkd->bhqd', attn, v)
        out = out.transpose(0, 2, 1, 3).reshape(b, t, d)
        return out @ wo + bo

    def _L0_attn_b_ref(x, W_qkv, b_qkv, W_proj, b_proj):
        import jax, jax.numpy as jnp
        import numpy as np
        ALPHA = 1.0
        N_HEADS = 16
        B, N, D = x.shape
        H = N_HEADS
        hd = D // H
        qkv = (x @ W_qkv + b_qkv).reshape(B, N, 3, H, hd).transpose(2, 0, 3, 1, 4)
        q, k, v = (qkv[0], qkv[1], qkv[2])
        q_row_2 = jnp.max(jnp.sum(jnp.abs(q), axis=-1), axis=-1) ** 2
        k_col_2 = jnp.max(jnp.sum(jnp.abs(k), axis=-2), axis=-1) ** 2
        fro_q = jnp.sqrt(jnp.sum(q * q, axis=(-2, -1)))
        inf_xt = jnp.max(jnp.sum(jnp.abs(x), axis=-2), axis=-1)
        denom = fro_q * inf_xt[:, None]
        qk = jnp.einsum('bhnd,bhmd->bhnm', q, k)
        sim = -ALPHA * (q_row_2[:, :, None, None] - 2.0 * qk + k_col_2[:, :, None, None]) / denom[:, :, None, None]
        attn = jax.nn.softmax(sim, axis=-1)
        weighted = jnp.einsum('bhnm,bhmd->bhnd', attn, v)
        weighted = weighted.transpose(0, 2, 1, 3).reshape(B, N, D)
        return weighted @ W_proj + b_proj

    def _L0_ffn_ref(x, Wr, Wg, Wu, Wd):
        import jax, jax.numpy as jnp
        import numpy as np
        D_MODEL = 128
        HIDDEN = 512
        NUM_EXPERTS = 8
        TOP_K = 2
        DEPTH = 12
        DEPTH_SCALE = 1.0 / np.sqrt(DEPTH)
        B, T, C = x.shape
        flat_x = x.reshape(-1, C)
        logits = flat_x @ Wr
        top_vals, top_idx = jax.lax.top_k(logits, TOP_K)
        rw = jax.nn.softmax(top_vals.astype(jnp.float32), axis=-1).astype(x.dtype)
        combine = jnp.sum(rw[..., None] * jax.nn.one_hot(top_idx, NUM_EXPERTS, dtype=x.dtype), axis=1)
        g = jnp.einsum('nc,ech->neh', flat_x, Wg)
        u = jnp.einsum('nc,ech->neh', flat_x, Wu)
        h = jax.nn.silu(g) * u
        eo = jnp.einsum('neh,ehc->nec', h, Wd) * DEPTH_SCALE
        out = jnp.einsum('ne,nec->nc', combine, eo)
        return out.reshape(B, T, C)
    x = L0_attn_a_x
    x = x + _L0_attn_a_ref(_layernorm(x, axis=-1), L0_attn_a_wq, L0_attn_a_bq, L0_attn_a_wk, L0_attn_a_bk, L0_attn_a_wv, L0_attn_a_bv, L0_attn_a_wo, L0_attn_a_bo)
    x = x + _L0_ffn_ref(_layernorm(x, axis=-1), L0_ffn_Wr, L0_ffn_Wg, L0_ffn_Wu, L0_ffn_Wd)
    x = x + _L0_attn_b_ref(_layernorm(x, axis=-1), L0_attn_b_W_qkv, L0_attn_b_b_qkv, L0_attn_b_W_proj, L0_attn_b_b_proj)
    x = x + _L0_ffn_ref(_layernorm(x, axis=-1), L0_ffn_Wr, L0_ffn_Wg, L0_ffn_Wu, L0_ffn_Wd)
    return x

_drawn_inputs = setup_inputs


def setup_inputs(seed=0):
    import zlib

    import numpy as np

    out = dict(_drawn_inputs(seed))
    spreads = {'L0_attn_b_b_qkv': (0.0, 0.1), 'L0_attn_b_b_proj': (0.0, 0.1)}
    factors = {'L0_attn_a_bq': 6.517, 'L0_attn_a_bk': 8.0}
    for name, (base, spread) in spreads.items():
        noise = np.random.default_rng([zlib.crc32(name.encode()), seed]).standard_normal(out[name].shape)
        drawn = base * np.exp(spread * noise) if base else spread * noise
        out[name] = jnp.asarray(drawn.astype(out[name].dtype))
    for name, factor in factors.items():
        out[name] = (out[name] * factor).astype(out[name].dtype)
    return out
```

```python
from contextlib import ExitStack

import concourse.bass as bass
from concourse import mybir

F32 = mybir.dt.float32
BF16 = mybir.dt.bfloat16
I32 = mybir.dt.int32
ALU = mybir.AluOpType
ACT = mybir.ActivationFunctionType
AX_X = mybir.AxisListType.X

P = 128
B, T, D = 16, 256, 128
H, HD = 16, 8
NBLK = B * T // P
TERMS = 6
ROWS = TERMS * HD
E, HID = 8, 512
HB = HID // P
G = 2
GBLK = NBLK // G
NT = 2 * GBLK + E
CST_DESC, CST_TILE, CST_HEAD, CST_TRIU = 0, E, E + NT, E + NT + P
CST_COLS = CST_TRIU + P
EPS = 1e-5
NEG = -3.0e38
DEPTH_SCALE = float(12.0 ** -0.5)
PCH = 23
POS = [8 * (h // 8) + 4 * (h % 2) + (h % 8) // 2 for h in range(H)]
RING = 3
RSQRT_MAGIC = float(0x5F3759DF)


def after(eng, sem, value):
    if isinstance(value, int) and value <= 0:
        return
    eng.wait_ge(sem, value)


def fixed(eng, value):
    if not isinstance(value, int):
        eng.compute_val(value)
    return value


class Layer:
    pass


def build(nc, A, out):
    with ExitStack() as ctx:
        def sb(name, shape, dt=F32):
            return ctx.enter_context(nc.sbuf_tensor(name, shape, dt))

        def psum(name):
            return ctx.enter_context(nc.psum_tensor(name, [P, 512], F32))

        def sem(name):
            return ctx.enter_context(nc.semaphore(name))

        def dram(name, shape, dt=F32):
            return nc.dram_tensor(name, shape, dt, kind="Internal").ap()

        psS = [psum("psS0"), psum("psS1")]
        psT = [psum("psT0"), psum("psT1")]
        psO = [psum("psO0"), psum("psO1")]
        psM = psum("psM")
        psN = psum("psN")

        x = sb("x", [P, NBLK, D])
        cst = sb("cst", [P, CST_COLS])
        mean_rstd = sb("mean_rstd", [P, NBLK, 2])
        bn6 = sb("bn6", [P, NBLK, 6])
        nwt = sb("nwt", [P, 3, NBLK])
        ident = sb("ident", [P, P])
        identb = sb("identb", [P, P], BF16)
        trib = sb("trib", [P, P], BF16)
        tick = sb("tick", [1, 2])
        ones_row = sb("ones_row", [1, T])
        xs = sb("xs", [P, 2, D])
        xT = [sb(f"xT{r}", [P, T]) for r in range(RING)]
        qk = sb("qk", [P, 2, T])
        rest = sb("rest", [P, 2, T])
        part = sb("part", [P, 2, 3, T], BF16)
        qst = [sb(f"qst{r}", [P, 8, T], BF16) for r in range(RING)]
        kst = [sb(f"kst{r}", [P, 8, T], BF16) for r in range(RING)]
        vp = [sb(f"vp{r}", [P, 2, H, 32]) for r in range(RING)]
        mx3 = sb("mx3", [P, 2, 3, 8])
        mxu = sb("mxu", [P, 2, 2, 8])
        mrow = sb("mrow", [8, 2, T], BF16)
        pT = sb("pT", [P, 8, 512])
        oT = sb("oT", [P, 4, T])
        rden = sb("rden", [P, H])
        on = sb("on", [P, D])
        onT = sb("onT", [P, D])

        head_ones = cst[:, CST_HEAD:CST_HEAD + P]
        absq = sb("absq", [P, T])
        junk = sb("junk", [P, 3, T])
        st = sb("st", [P, 4])
        row = sb("row", [1, 56])
        prow = sb("prow", [1, 8, H])
        half = sb("half", [1, 2, H])
        scb = [sb(f"scb{r}", [P, 2, H]) for r in range(RING)]
        neg_shift = [sb(f"neg_shift{r}", [8, 2]) for r in range(RING)]

        wg = sb("wg", [P, E * HID])
        wu = sb("wu", [P, E * HID])
        wd = sb("wd", [P, E * HID])
        wr = sb("wr", [P, E])
        xn = sb("xn", [P, NBLK, D])
        gb = [pT[:].rearrange("p a (b c) -> p (a b) c", c=D), xn[:]]
        triu = sb("triu", [P, P], BF16)
        onesb = sb("onesb", [P, P], BF16)
        zero = sb("zero", [P, D])
        xnT = [sb(f"xnT{i}", [P, 4 * P]) for i in range(2)]
        lg = sb("lg", [P, GBLK, E])
        ea = sb("ea", [P, GBLK, E])
        eb = sb("eb", [P, GBLK, E])
        pick = [sb(f"pick{i}", [P, GBLK, E]) for i in range(2)]
        pickb = sb("pickb", [P, GBLK, E], BF16)
        v12 = sb("v12", [P, 3, GBLK])
        e1 = sb("e1", [P, GBLK])
        slotf = sb("slotf", [P, 2, GBLK])
        slot = [sb(f"slot{g}", [P, 2, GBLK], I32) for g in range(G)]
        wgt = [sb(f"wgt{g}", [P, 2, GBLK]) for g in range(G)]
        pc = sb("pc", [P, 4, E])
        pci = sb("pci", [P, 2, E], I32)
        cmpt = sb("cmpt", [1, NT, E])
        tef = sb("tef", [1, NT])
        te = [sb(f"te{g}", [1, NT], I32) for g in range(G)]
        xin = [sb(f"xin{i}", [P, D]) for i in range(2)]
        xTt = [sb(f"xTt{i}", [P, P]) for i in range(2)]
        sg = [sb(f"sg{i}", [P, HID]) for i in range(2)]
        hh = [sb(f"hh{i}", [P, HID]) for i in range(2)]
        hT = [sb(f"hT{i}", [P, HB, P]) for i in range(2)]
        ysb = [sb(f"ysb{i}", [P, D]) for i in range(2)]

        xg = [dram(f"xg{g}", (NT * P, D)) for g in range(G)]
        eo = [dram(f"eo{g}", (NT * P, D)) for g in range(G)]
        scr_part = dram("scr_part", (2, P, TERMS, T), BF16)
        scr_m = dram("scr_m", (2, 8, 2, T), BF16)

        x_dram = A["L0_attn_a_x"].rearrange("b (k p) d -> p (b k) d", p=P)
        out_dram = out.rearrange("b (k p) d -> p (b k) d", p=P)

        s_xin = sem("s_xin")
        s_const = sem("s_const")
        s_const_dve = sem("s_const_dve")
        s_chain = sem("s_chain")
        s_ln = [sem("s_ln0"), sem("s_ln1"), sem("s_ln2"), sem("s_ln3")]
        s_out = sem("s_out")
        s_mset = sem("s_mset")
        s_cst = sem("s_cst")
        s_half = sem("s_half")
        s_lnB = sem("s_lnB")
        s_wffn = sem("s_wffn")
        s_zero = sem("s_zero")
        s_zfill = sem("s_zfill")
        r_sem = {n: sem("R_" + n) for n in ["xn", "T_ps", "T", "lg_ps", "lg", "d12", "e12", "pickb", "cnt_ps",
                                            "slots", "x"]}
        r_scat = [sem(f"R_scat{g}") for g in range(G)]
        r_gat = [[sem(f"R_gat{g}{q}") for q in range(4)] for g in range(G)]
        f_sem = {n: sem("F_" + n) for n in ["T_ps", "xT", "gu", "silu", "h", "hT_ps", "hTa", "hTb", "y_ps", "y"]}
        f_ld = [sem(f"F_ld{i}") for i in range(2)]
        f_st = [sem(f"F_st{i}") for i in range(2)]
        chain = [0]

        def link(ins):
            chain[0] += 1
            ins.then_inc(s_chain, 1)
            nc.vector.wait_ge(s_chain, chain[0])

        SEMS = ["w", "wp", "bcol_ps", "bcol", "xs", "xT_ps", "xT", "qk_ps", "qk", "split", "scr_w", "stack",
                "S", "mx", "mxu", "mT", "m1", "m2", "mscr", "mrow", "ST", "exp", "pT", "PV", "oT", "tO_ps",
                "rden", "on", "onT_ps", "onT", "y", "x1", "v_ps", "v",
                "col", "qsum_ps", "qsum", "row_ps", "row", "pool", "bc_ps", "bc", "seed"]

        def layer(tag, causal):
            L = Layer()
            L.tag, L.causal = tag, causal
            L.s = {n: sem(f"{tag}_{n}") for n in SEMS}
            L.w_in = sb(f"w_in{tag}", [P, 4, D])
            L.w_perm = sb(f"w_perm{tag}", [P, 2, D])
            L.b_in = sb(f"b_in{tag}", [1, 4, D])
            L.b_perm = sb(f"b_perm{tag}", [1, 2, D])
            L.b_col = sb(f"b_col{tag}", [P, 2])
            return L

        LA = layer("A", True)
        LB = layer("B", False)
        LB.s["pT"] = LB.s["exp"]

        def kcols(L):
            return 384 if L.causal else 512

        def pe_setup(pe, L):
            s = L.s
            pe.wait_ge(s["wp"], 4)
            pe.wait_ge(s_const_dve, 3)
            for o in range(2):
                last = nc.tensor.matmul(psM[:, o:o + 1], L.b_perm[0:1, o, :], ones_row[0:1, 0:1],
                                        start=(o == 0), stop=True, skip_group_check=True)
            last.then_inc(s["bcol_ps"], 1)

        def pe_step(pe, L, j, c, P_, V_, S_, T_, O_):
            s = L.s
            bS, bT, bO = j - 2, j - 3, j - 4
            rP, rS, rT, rO = c % 3, (c - 2) % 3, (c - 3) % 3, (c - 4) % 3
            cols = kcols(L)
            C_ = not L.causal and (not isinstance(j, int) or 0 <= j - 1 < B)

            def pv_quad(b, r, q):
                after(pe, s["pT"], 16 * b + 4 * q + 4)
                if q % 2 == 0:
                    after(pe, s["oT"], 2 * (b - 1) + q // 2 + 1)
                for kb in range(2):
                    for i in range(4):
                        h = 4 * q + i
                        if kb == 0:
                            dst, src = (0, T), (0, T)
                        elif L.causal:
                            dst, src = (P, T), (T, T + P)
                        else:
                            dst, src = (0, T), (T, 2 * T)
                        o0 = (q % 2) * T
                        last = nc.tensor.matmul(psO[q // 2][32 * i:32 * i + 32, o0 + dst[0]:o0 + dst[1]],
                                                vp[r][:, kb, h, :], pT[:, h % 8, src[0]:src[1]],
                                                start=(kb == 0), stop=(kb == 1), skip_group_check=True)
                last.then_inc(s["PV"], 1)

            def out_transposes(qb):
                for q in range(4):
                    last = nc.tensor.transpose(psN[:, q * P:(q + 1) * P], oT[:, q, qb * P:(qb + 1) * P], ident[:])
                last.then_inc(s["tO_ps"], 1)

            def out_transpose_on(qb):
                after(pe, s["on"], 2 * bO + qb + 1)
                nc.tensor.transpose(psN[:, 0:P], on[:], ident[:]).then_inc(s["onT_ps"], 1)

            def out_project(qb):
                after(pe, s["onT"], 2 * bO + qb + 1)
                nc.tensor.matmul(psN[:, P:2 * P], onT[:], L.w_in[:, 3, :], start=True, stop=False)
                nc.tensor.matmul(psN[:, P:2 * P], ones_row[0:1, 0:P], L.b_in[0:1, 3, :],
                                 start=False, stop=True).then_inc(s["y"], 1)

            def max_transposes(b, u):
                for qb in range(2):
                    src = mxu if L.causal else mx3
                    last = nc.tensor.transpose(psN[0:8, qb * P:(qb + 1) * P], src[:, u, qb, :], ident[:])
                last.then_inc(s["mT"], 1)

            for h in range(H):
                par, t = h % 2, h // 2
                r64 = slice(64 * par, 64 * par + ROWS)
                m64 = slice(64 * par, 64 * par + ROWS + 2)
                if S_:
                    if h == 0:
                        after(pe, s["stack"], 64 * (bS + 1))
                    after(pe, s["mx"], 16 * bS + h - 1)
                    ps, q_, k_ = psS[h % 2], qst[rS], kst[rS]
                    if L.causal:
                        for c0, k in ((0, 0), (P, 1)):
                            nc.tensor.matmul(ps[:, c0:c0 + P], q_[r64, t, k * P:(k + 1) * P],
                                             k_[r64, t, k * P:(k + 1) * P],
                                             start=True, stop=False, skip_group_check=True)
                            nc.tensor.matmul(ps[:, c0:c0 + P], identb[:], trib[:],
                                             start=False, stop=True, skip_group_check=True)
                        nc.tensor.matmul(ps[:, 2 * P:3 * P], q_[r64, t, P:T], k_[r64, t, 0:P],
                                         start=True, stop=True, skip_group_check=True).then_inc(s["S"], 1)
                    else:
                        nc.tensor.matmul(ps[:, 0:T], q_[r64, t, 0:P], k_[r64, t, :],
                                         start=True, stop=True, skip_group_check=True)
                        nc.tensor.matmul(ps[:, T:2 * T], q_[r64, t, P:T], k_[r64, t, :],
                                         start=True, stop=True, skip_group_check=True).then_inc(s["S"], 1)
                if T_:
                    if h % 8 == 0:
                        after(pe, s["mrow"], 32 * (2 * bT + h // 8 + 1))
                    after(pe, s["exp"], 16 * bT + h - 1)
                    ps, q_, k_ = psT[h % 2], qst[rT], kst[rT]
                    nc.tensor.matmul(ps[:, 0:T], k_[m64, t, 0:P], q_[m64, t, :],
                                     start=True, stop=True, skip_group_check=True)
                    q0 = P if L.causal else 0
                    nc.tensor.matmul(ps[:, T:cols], k_[m64, t, P:T], q_[m64, t, q0:T],
                                     start=True, stop=True, skip_group_check=True).then_inc(s["ST"], 1)
                if T_ and h in (5, 9, 13):
                    pv_quad(bT, rT, (h - 5) // 4)
                if h == 1:
                    if O_:
                        pv_quad(bO, rO, 3)
                    if T_:
                        after(pe, s["mxu"] if L.causal else s["mx"], (2 if L.causal else 16) * (bT + 1))
                        after(pe, s["x1"], 2 * bO)
                        max_transposes(bT, 1)
                if h == 2 and P_:
                    after(pe, s["xs"], j + 1)
                    if not L.causal:
                        after(pe, s["row"], 4 * j)
                    after(pe, s["v"], j - 2)
                    after(pe, s["qk"], 2 * j)
                    after(pe, s["bcol"], 1)
                    after(pe, s["v_ps"], j - 4)
                    for k in range(2):
                        last = nc.tensor.transpose(psM[:, k * P:(k + 1) * P], xs[:, k, :], ident[:])
                    last.then_inc(s["xT_ps"], 1)
                if h == 5 and P_:
                    after(pe, s["xT"], j + 1)
                    for o in range(2):
                        last = nc.tensor.matmul(psM[:, o * T:(o + 1) * T], L.w_perm[:, o, :], xT[rP][:],
                                                start=(o == 0), stop=True, skip_group_check=True)
                    last.then_inc(s["qk_ps"], 1)
                if h == 8 and C_:
                    after(pe, s["pool"], PCH * j)
                    after(pe, s["qk"], 2 * (j + 1) if P_ else 2 * B)
                    after(pe, s["row"], 4 * j)
                    nc.tensor.matmul(psM[:, 0:2 * H], ones_row[0:1, 0:P],
                                     prow[0:1, 0:2, :].rearrange("p a h -> p (a h)"),
                                     start=True, stop=True, skip_group_check=True)
                    for u in range(2):
                        last = nc.tensor.matmul(psM[0:8, 2 * H + u:2 * H + u + 1],
                                                prow[0:1, 2, 8 * u:8 * u + 8], ones_row[0:1, 0:1],
                                                start=False, stop=True, skip_group_check=True)
                    last.then_inc(s["bc_ps"], 1)
                if h == 10 and V_:
                    if not L.causal:
                        after(pe, s["bc"], 2 * j if C_ else 2 * B)
                    if P_:
                        after(pe, s["qk"], 2 * (j + 1))
                    else:
                        after(pe, s["qk"], 2 * B)
                    after(pe, s["v"], bS)
                    for k in range(2):
                        nc.tensor.matmul(psM[:, k * P:(k + 1) * P], xT[rS][:, k * P:(k + 1) * P], L.w_in[:, 2, :],
                                         start=(k == 0), stop=False, skip_group_check=True)
                        last = nc.tensor.matmul(psM[:, k * P:(k + 1) * P], ones_row[0:1, 0:P], L.b_in[0:1, 2, :],
                                                start=False, stop=True, skip_group_check=True)
                    last.then_inc(s["v_ps"], 1)
                if h == 12 and P_ and not L.causal:
                    after(pe, s["col"], 4 * j + 1)
                    after(pe, s["v"], bS + 1)
                    after(pe, s["bc"], 2 * j)
                    nc.tensor.matmul(psM[:, 0:T], head_ones, absq[:],
                                     start=True, stop=True, skip_group_check=True).then_inc(s["qsum_ps"], 1)
                if h == 14 and P_ and not L.causal:
                    after(pe, s["col"], 4 * j + 4)
                    after(pe, s["qsum"], j + 1)
                    for i in range(4):
                        last = nc.tensor.transpose(psM[0:1, i * P:(i + 1) * P], st[:, i:i + 1], ident[:])
                    last.then_inc(s["row_ps"], 1)
                if h == 4 and O_:
                    after(pe, s["oT"], 2 * bO + 2)
                    if T_:
                        after(pe, s["m2"], 2 * (bT + 1))
                    else:
                        after(pe, s["x1"], 2 * bO)
                    out_transposes(0)
                if h == 6 and O_:
                    out_transpose_on(0)
                if h == 7 and O_:
                    out_project(0)
                if h == 9 and S_:
                    after(pe, s["mxu"] if L.causal else s["mx"], 2 * bS + 1 if L.causal else 16 * bS + 8)
                    after(pe, s["x1"], 2 * bO + 1)
                    max_transposes(bS, 0)
                if h == 11 and O_:
                    if S_:
                        after(pe, s["m2"], 2 * bS + 1)
                    after(pe, s["x1"], 2 * bO + 1)
                    out_transposes(1)
                if h == 13 and O_:
                    out_transpose_on(1)
                if h == 14 and O_:
                    out_project(1)

        def act_setup(act, L):
            act.wait_ge(L.s["bcol_ps"], 1)
            nc.scalar.activation(L.b_col[:], psM[:, 0:2], ACT.Copy).then_inc(L.s["bcol"], 1)
            act.wait_ge(L.s["bcol"], 1)

        def act_step(act, L, j, c, P_, V_, S_, T_, O_):
            s = L.s
            bS, bT, bO = j - 2, j - 3, j - 4
            rP = c % 3
            cols = kcols(L)

            def high_max(b, u, ring):
                after(act, s["mT"], 2 * b + u + 1)
                after(act, s["mscr"], 16 * (2 * b + u))
                if L.causal:
                    nc.scalar.activation(mrow[0:8, 0, :], psN[0:8, 0:T], ACT.Copy).then_inc(s["m1"], 1)
                else:
                    after(act, s["bc"], 2 * (b + 1))
                    nc.scalar.activation(mrow[0:8, 0, :], psN[0:8, 0:T], ACT.Identity,
                                         bias=neg_shift[ring][0:8, u:u + 1]).then_inc(s["m1"], 1)

            def evac_oT(b, half):
                after(act, s["PV"], 4 * b + 2 * half + 2)
                after(act, s["tO_ps"], 2 * b)
                nc.scalar.activation(oT[:, 2 * half:2 * half + 2, :], psO[half][:].rearrange("p (a t) -> p a t", a=2),
                                     ACT.Copy).then_inc(s["oT"], 1)

            def evac_onT(qb):
                after(act, s["onT_ps"], 2 * bO + qb + 1)
                after(act, s["y"], 2 * bO + qb)
                nc.scalar.activation(onT[:], psN[:, 0:P], ACT.Copy).then_inc(s["onT"], 1)

            for h in range(H):
                if T_:
                    after(act, s["ST"], 16 * bT + h + 1)
                    after(act, s["PV"], 4 * bT + h // 4 - 1)
                    if L.causal:
                        nc.scalar.activation(pT[:, h % 8, 0:cols], psT[h % 2][:, 0:cols], ACT.Exp,
                                             scale=float(HD) ** -0.5).then_inc(s["exp"], 1)
                    else:
                        i = POS[h]
                        r = (c - 3) % 3
                        nc.scalar.activation(pT[:, h % 8, 0:cols], psT[h % 2][:, 0:cols], ACT.Exp,
                                             scale=scb[r][:, 0, i:i + 1],
                                             bias=scb[r][:, 1, i:i + 1]).then_inc(s["exp"], 1)
                if h == 1 and T_:
                    high_max(bT, 1, (c - 3) % 3)
                if h == 2 and O_:
                    evac_oT(bO, 1)
                if h == 3 and P_:
                    after(act, s["xT_ps"], j + 1)
                    after(act, s["v_ps"], j - 2)
                    nc.scalar.activation(xT[rP][:], psM[:, 0:T], ACT.Copy).then_inc(s["xT"], 1)
                if h == 6 and P_:
                    after(act, s["qk_ps"], j + 1)
                    after(act, s["split"], 4 * j)
                    if not L.causal:
                        after(act, s["col"], 4 * j)
                    for o in range(2):
                        nc.scalar.activation(qk[:, o, :], psM[:, o * T:(o + 1) * T], ACT.Identity,
                                             bias=L.b_col[:, o:o + 1]).then_inc(s["qk"], 1)
                if h == 7 and O_:
                    evac_onT(0)
                if h == 8 and P_ and not L.causal:
                    after(act, s["qk"], 2 * j + 2)
                    after(act, s["qsum_ps"], j)
                    nc.scalar.activation(absq[:], qk[:, 0, :], ACT.Abs).then_inc(s["col"], 1)
                if h in (9, 10, 11) and P_ and not L.causal:
                    i = h - 8
                    after(act, s["row_ps"], j)
                    after(act, s["col"], 4 * j)
                    src = (qk[:, 0, :], qk[:, 1, :], xT[rP][:])[i - 1]
                    if i == 3:
                        after(act, s["xT"], j + 1)
                    nc.scalar.activation(junk[:, i - 1, :], src, ACT.Square if i == 1 else ACT.Abs,
                                         accum_out=st[:, i:i + 1]).then_inc(s["col"], 1)
                if h == 13 and T_:
                    evac_oT(bT, 0)
                if h == 10 and S_:
                    high_max(bS, 0, (c - 2) % 3)
                if h == 14 and O_:
                    evac_onT(1)

        def dve_setup(dve, L):
            s = L.s
            dve.wait_ge(s["w"], 16 * 8)
            for o in range(2):
                nc.vector.tensor_copy(L.w_perm[:, o, :].rearrange("p (a t i) -> p a t i", a=2, t=8),
                                      L.w_in[:, o, :].rearrange("p (t a i) -> p a t i", a=2, t=8)).then_inc(s["wp"], 1)
                nc.vector.tensor_copy(L.b_perm[:, o, :].rearrange("p (a t i) -> p a t i", a=2, t=8),
                                      L.b_in[:, o, :].rearrange("p (t a i) -> p a t i", a=2, t=8)).then_inc(s["wp"], 1)

        def split_step(eng, ncx, L, b):
            s = L.s
            after(eng, s["qk"], 2 * (b + 1))
            after(eng, s["scr_w"], 96 * b)
            ncx.tensor_copy(part[:, :, 0, :], qk[:]).then_inc(s["split"], 1)
            after(eng, s["split"], 4 * b + 1)
            ncx.tensor_tensor(out=rest[:], in0=qk[:], in1=part[:, :, 0, :], op=ALU.subtract).then_inc(s["split"], 1)
            after(eng, s["split"], 4 * b + 2)
            ncx.tensor_copy(part[:, :, 1, :], rest[:]).then_inc(s["split"], 1)
            after(eng, s["split"], 4 * b + 3)
            ncx.tensor_tensor(out=part[:, :, 2, :], in0=rest[:], in1=part[:, :, 1, :],
                              op=ALU.subtract).then_inc(s["split"], 1)

        def dve_step(dve, L, j, c, P_, V_, S_, T_, O_):
            s = L.s
            bS, bT, bO = j - 2, j - 3, j - 4
            rS = (c - 2) % 3
            C_ = not L.causal and (not isinstance(j, int) or 0 <= j - 1 < B)

            def low_max(b, u, ring):
                after(dve, s["m1"], 2 * b + u + 1)
                shift = 0.0 if L.causal else neg_shift[ring][0:8, u:u + 1]
                nc.vector.scalar_tensor_tensor(out=mrow[0:8, 1, :], in0=psN[0:8, 0:T], scalar=shift,
                                               in1=mrow[0:8, 0, :], op0=ALU.add,
                                               op1=ALU.subtract).then_inc(s["m2"], 1)

            def normalise(qb):
                after(dve, s["tO_ps"], 2 * bO + qb + 1)
                after(dve, s["onT_ps"], 2 * bO + qb)
                o4 = psN[:].rearrange("p (h c) -> p h c", c=32)
                nc.vector.reciprocal(rden[:], o4[:, :, HD]).then_inc(s["rden"], 1)
                after(dve, s["rden"], 2 * bO + qb + 1)
                nc.vector.tensor_tensor(out=on[:].rearrange("p (h c) -> p h c", c=HD), in0=o4[:, :, 0:HD],
                                        in1=rden[:].unsqueeze(2).to_broadcast([P, H, HD]),
                                        op=ALU.mult).then_inc(s["on"], 1)

            def residual(qb):
                after(dve, s["y"], 2 * bO + qb + 1)
                blk = x[:, bass.ds(2 * bO + qb, 1), :]
                nc.vector.tensor_tensor(out=blk, in0=blk, in1=psN[:, P:2 * P].unsqueeze(1),
                                        op=ALU.add).then_inc(s["x1"], 1)

            for h in range(H):
                if L.causal and ((h == 8 and S_) or (h == 0 and T_)):
                    b, u = (bS, 0) if h == 8 else (bT, 1)
                    after(dve, s["mx"], 16 * b + 8 * u + 8)
                    after(dve, s["mT"], 2 * b + u - 1)
                    nc.vector.tensor_tensor(out=mxu[:, u], in0=mx3[:, u, 0:2, :], in1=mx3[:, u, 0:3:2, :],
                                            op=ALU.max).then_inc(s["mxu"], 1)
                if S_:
                    u = h // 8
                    pos = (h % 2) * 4 + (h % 8) // 2
                    after(dve, s["S"], 16 * bS + h + 1)
                    if h % 8 == 0:
                        if L.causal:
                            after(dve, s["mxu"], 2 * bS + u - 1)
                        else:
                            after(dve, s["mT"], 2 * bS + u - 1)
                    n = 3 if L.causal else 2
                    nc.vector.tensor_reduce(mx3[:, u, 0:n, pos:pos + 1].rearrange("p a b -> p (a b)"),
                                            psS[h % 2][:, 0:kcols(L)].rearrange("p (a k) -> p a k", a=n),
                                            AX_X, ALU.max).then_inc(s["mx"], 1)
                if h == 0 and P_:
                    after(dve, s["xT_ps"], j)
                    for k in range(2):
                        blk = 2 * j + k
                        ins = nc.vector.tensor_scalar(xs[:, k, :].unsqueeze(1), x[:, bass.ds(blk, 1), :],
                                                      mean_rstd[:, bass.ds(blk, 1), 0:1].rearrange("p a b -> p (a b)"),
                                                      mean_rstd[:, bass.ds(blk, 1), 1:2].rearrange("p a b -> p (a b)"),
                                                      ALU.subtract, ALU.mult)
                    ins.then_inc(s["xs"], 1)
                if h == 2 and T_:
                    low_max(bT, 1, (c - 3) % 3)
                if h == 5 and O_:
                    normalise(0)
                if h == 8 and O_:
                    residual(0)
                if h == 3 and C_:
                    after(dve, s["pool"], PCH * (j - 1) + 2)
                    nc.vector.tensor_scalar(prow[0:1, 6, :].bitcast(I32), prow[0:1, 4, :].bitcast(I32), 1, None,
                                            ALU.logical_shift_right).then_inc(s["seed"], 1)
                    after(dve, s["seed"], 2 * j - 1)
                    nc.vector.tensor_scalar(prow[0:1, 7, :].bitcast(I32), prow[0:1, 6, :].bitcast(I32), -1.0,
                                            RSQRT_MAGIC, ALU.mult, ALU.add).then_inc(s["seed"], 1)
                if h == 9 and C_:
                    r = (c - 1) % 3
                    after(dve, s["bc_ps"], j)
                    after(dve, s["exp"], 16 * (j - 4) + 16)
                    nc.vector.tensor_copy(scb[r][:].rearrange("p a h -> p (a h)"),
                                          psM[:, 0:2 * H]).then_inc(s["bc"], 1)
                    nc.vector.tensor_copy(neg_shift[r][:], psM[0:8, 2 * H:2 * H + 2]).then_inc(s["bc"], 1)
                if h == 13 and P_ and not L.causal:
                    after(dve, s["qsum_ps"], j + 1)
                    after(dve, s["row_ps"], j)
                    nc.vector.tensor_reduce(st[:, 0:1], psM[:, 0:T], AX_X, ALU.max).then_inc(s["qsum"], 1)
                if h == 15 and P_ and not L.causal:
                    after(dve, s["row_ps"], j + 1)
                    after(dve, s["pool"], PCH * j)
                    for i, op in enumerate((ALU.max, ALU.add, ALU.max)):
                        for u in range(2):
                            src = psM[0:1, i * P:(i + 1) * P].rearrange("p (a u t i) -> p u a t i", a=2, u=2, i=HD)
                            ins = nc.vector.tensor_reduce(
                                row[0:1, 16 * i + 8 * u:16 * i + 8 * u + 8].rearrange("p (a t) -> p a t", a=2),
                                src[:, u], AX_X, op)
                        ins.then_inc(s["row"], 1)
                    nc.vector.tensor_reduce(row[0:1, 48:49], psM[0:1, 3 * P:4 * P], AX_X,
                                            ALU.max).then_inc(s["row"], 1)
                if h == 9 and P_:
                    split_step(dve, nc.vector, L, j)
                if h == 10 and S_:
                    low_max(bS, 0, (c - 2) % 3)
                if h == 11 and V_:
                    after(dve, s["v_ps"], bS + 1)
                    after(dve, s["PV"], 4 * (bS - 2))
                    nc.vector.tensor_copy(vp[rS][:, :, :, 0:HD],
                                          psM[:, 0:T].rearrange("p (k h c) -> p k h c", k=2, c=HD)).then_inc(s["v"], 1)
                if h == 12 and O_:
                    normalise(1)
                if h == 15 and O_:
                    residual(1)

        def pool_step(pool, L, j, c, P_, V_, S_, T_, O_):
            s = L.s
            bT = j - 3
            if not L.causal and (not isinstance(j, int) or 0 <= j - 1 < B):
                S2, C, NC, KK, V, W, SH, Y = (prow[0:1, i, :] for i in range(8))
                q_row, fro, k_col = (row[0:1, 16 * i:16 * i + 16] for i in range(3))
                inf_x = row[0:1, 48:49].to_broadcast([1, H])
                m05, p15 = half[0:1, 0, :], half[0:1, 1, :]
                mul, add = ALU.mult, ALU.add
                ops = [(W, fro, inf_x, mul), (V, W, inf_x, mul)]
                ops += [(NC, q_row, q_row, mul), (KK, k_col, k_col, mul), (NC, NC, KK, add), (NC, NC, m05, mul)]
                for it in range(3):
                    src = Y if it == 0 else S2
                    ops += [(W, src, src, mul), (W, W, V, mul), (W, W, m05, mul), (W, W, p15, add), (S2, src, W, mul)]
                ops += [(S2, S2, S2, add), (C, NC, S2, mul)]
                assert len(ops) == PCH
                after(pool, s["row"], 4 * j)
                after(pool, s["bc_ps"], j - 1)
                for n, (o, a, b_, op) in enumerate(ops):
                    if n > 0:
                        after(pool, s["pool"], PCH * (j - 1) + n)
                    if n == 6:
                        after(pool, s["seed"], 2 * j)
                    nc.gpsimd.tensor_tensor(out=o, in0=a, in1=b_, op=op).then_inc(s["pool"], 1)
            if L.causal and T_:
                fixed(pool, 16 * bT + 1)
                for h in range(H):
                    after(pool, s["exp"], 16 * bT + h + 1)
                    if h < H - 1:
                        fixed(pool, 16 * bT + h + 2)
                    else:
                        nc.gpsimd.tensor_tensor(out=tick[:, 0:1], in0=tick[:, 1:2], in1=tick[:, 1:2], op=ALU.add)
                    d = pT[:, h % 8, 0:384].rearrange("p (a k) -> p a k", a=3)[:, 0:3:2, :]
                    nc.gpsimd.affine_select(out=d, in_=d, compare_op=ALU.is_ge, fill=0.0, base=0,
                                            pattern=[[0, 2], [1, P]], channel_multiplier=-1).then_inc(s["pT"], 1)

        def sp_step(sp, L, j, c, P_, V_, S_, T_, O_):
            s = L.s
            bS, bT = j - 2, j - 3

            def max_rows(b, u, r):
                ready, read, written = (fixed(sp, v) for v in (2 * b + u + 1, 32 * (2 * b + u), 16 * (2 * b + u + 1)))
                after(sp, s["m2"], ready)
                after(sp, s["mrow"], read)
                sp.dma_start(scr_m[u], mrow[:]).then_inc(s["mscr"], 16)
                after(sp, s["mscr"], written)
                for par in range(2):
                    sp.dma_start(qst[r][64 * par + ROWS:64 * par + ROWS + 2, 4 * u:4 * u + 4, :],
                                 scr_m[u, 4 * par:4 * par + 4].rearrange("t k q -> k t q")).then_inc(s["mrow"], 16)

            if T_:
                max_rows(bT, 1, (c - 3) % 3)
            if not isinstance(j, int) or 0 <= j - 1 < B:
                b, r = j - 1, (c - 1) % 3
                ready, read, written, scored = (fixed(sp, v) for v in (4 * (b + 1), 64 * b, 96 * (b + 1), 16 * (b - 2)))
                after(sp, s["split"], ready)
                after(sp, s["stack"], read)
                q3 = part[:, 0, :, :]
                k3 = part[:, 1, :, :]
                sp.dma_start(scr_part[0, :, 0:3, :], q3).then_inc(s["scr_w"], 16)
                sp.dma_start(scr_part[0, :, 3:5, :], q3[:, 0:2, :]).then_inc(s["scr_w"], 16)
                sp.dma_start(scr_part[0, :, 5:6, :], q3[:, 0:1, :]).then_inc(s["scr_w"], 16)
                sp.dma_start(scr_part[1, :, 0:3:2, :], k3[:, 0:1, :].to_broadcast([P, 2, T])).then_inc(s["scr_w"], 16)
                sp.dma_start(scr_part[1, :, 1:4:2, :], k3[:, 0:2, :]).then_inc(s["scr_w"], 16)
                sp.dma_start(scr_part[1, :, 4:6, :], k3[:, 1:3, :]).then_inc(s["scr_w"], 16)
                after(sp, s["scr_w"], written)
                after(sp, s["ST"], scored)
                after(sp, s_mset, 1)
                for o, st in enumerate((qst, kst)):
                    for par in range(2):
                        sp.dma_start(st[r][64 * par:64 * par + ROWS, :, :],
                                     scr_part[o, 64 * par:64 * par + 64].rearrange("(t i) r q -> (i r) t q", t=8)
                                     ).then_inc(s["stack"], 16)
            if S_:
                max_rows(bS, 0, (c - 2) % 3)

        def pipeline(step, eng, L):
            def flags(j):
                return [0 <= j < B] + [0 <= j - d < B for d in (2, 2, 3, 4)]

            for j in range(7):
                step(eng, L, j, j % 3, *flags(j))
            with eng.Fori(7, B - 2, 3) as j:
                for d in range(3):
                    step(eng, L, j + d, (7 + d) % 3, True, True, True, True, True)
            for j in range(B, B + 4):
                step(eng, L, j, j % 3, *flags(j))

        def dve_ln_stats(dve, lo, hi, done):
            for k in range(lo, hi):
                ins = nc.vector.bn_stats(bn6[:, k, :], x[:, k, :])
            link(ins)
            for k in range(lo, hi):
                ins = nc.vector.bn_aggr(mean_rstd[:, k, :], bn6[:, k, :])
            link(ins)
            ve, y, a = (nwt[:, i, lo:hi] for i in range(3))
            link(nc.vector.tensor_scalar(ve, mean_rstd[:, lo:hi, 1], EPS, None, ALU.add))
            rsqrt(ve, y, a)
            nc.vector.tensor_copy(mean_rstd[:, lo:hi, 1], y).then_inc(done, 1)

        def rsqrt(v, y, a):
            link(nc.vector.tensor_scalar(a.bitcast(I32), v.bitcast(I32), 1, None, ALU.logical_shift_right))
            link(nc.vector.tensor_scalar(y.bitcast(I32), a.bitcast(I32), -1.0, RSQRT_MAGIC, ALU.mult, ALU.add))
            for _ in range(4):
                link(nc.vector.scalar_tensor_tensor(out=a, in0=y, scalar=-0.5, in1=y, op0=ALU.mult, op1=ALU.mult))
                link(nc.vector.tensor_tensor(out=a, in0=a, in1=v, op=ALU.mult))
                link(nc.vector.scalar_tensor_tensor(out=y, in0=a, scalar=1.5, in1=y, op0=ALU.add, op1=ALU.mult))

        def ffn_over(eng, n):
            eng.wait_ge(f_sem["y"], NT * (n + 1))
            for i in range(2):
                eng.wait_ge(f_st[i], 16 * (NT // 2) * (n + 1))

        def layer_over(eng, L):
            s = L.s
            for name, count in (("x1", 2 * B), ("y", 2 * B), ("exp", 16 * B), ("PV", 4 * B), ("oT", 2 * B),
                                ("onT", 2 * B), ("stack", 64 * B), ("mrow", 64 * B), ("v", B), ("split", 4 * B),
                                ("pT", 16 * B)):
                eng.wait_ge(s[name], count)

        def dve_route_in(dve, n):
            g = n % G
            lo = g * GBLK
            dve_ln_stats(dve, lo, lo + GBLK, s_ln[n])
            dve.wait_ge(s_ln[n], 1)
            if n >= G:
                for q in range(4):
                    dve.wait_ge(r_gat[1][q], 16 * 8 * (n // G))
                dve.wait_ge(r_sem["x"], NBLK * 2)
            for k in range(lo, lo + GBLK):
                nc.vector.tensor_scalar(xn[:, k, :], x[:, k, :], mean_rstd[:, k, 0:1], mean_rstd[:, k, 1:2],
                                        ALU.subtract, ALU.mult).then_inc(r_sem["xn"], 1)

        def pe_route(pe, n):
            g = n % G
            lo = g * GBLK
            r = r_sem

            def transposes(i):
                pe.wait_ge(r["xn"], GBLK * n + 4 * i + 4)
                after(pe, r["T"], 4 * n + i)
                for m in range(4):
                    last = nc.tensor.transpose(psM[:, m * P:(m + 1) * P], xn[:, lo + 4 * i + m, :], ident[:])
                last.then_inc(r["T_ps"], 1)

            after(pe, r["lg"], n)
            transposes(0)
            for i in range(4):
                pe.wait_ge(r["T"], 4 * n + i + 1)
                if i < 3:
                    transposes(i + 1)
                for m in range(4):
                    k = 4 * i + m
                    last = nc.tensor.matmul(psS[0][:, E * k:E * k + E], xnT[i % 2][:, m * P:(m + 1) * P], wr[:],
                                            start=True, stop=True, skip_group_check=True)
                last.then_inc(r["lg_ps"], 1)
            pe.wait_ge(r["pickb"], n + 1)
            after(pe, r["slots"], n)
            rhs = pickb[:].rearrange("p k e -> p (k e)")
            nc.tensor.matmul(psS[1][:, 0:P], triu[:], rhs, start=True, stop=True, skip_group_check=True)
            nc.tensor.matmul(psS[1][:, P:2 * P], onesb[:], rhs, start=True, stop=True,
                             skip_group_check=True).then_inc(r["cnt_ps"], 1)

        def act_route(act, n):
            r = r_sem
            for i in range(4):
                act.wait_ge(r["T_ps"], 4 * n + i + 1)
                after(act, r["lg_ps"], 4 * n + i - 1)
                nc.scalar.activation(xnT[i % 2][:], psM[:], ACT.Copy).then_inc(r["T"], 1)
            act.wait_ge(r["d12"], n + 1)
            nc.scalar.activation(e1[:], v12[:, 2, :], ACT.Exp).then_inc(r["e12"], 1)

        def dve_route(dve, n):
            g = n % G
            r = r_sem
            shape = [P, GBLK, E]
            desc = cst[:, CST_DESC:CST_DESC + E].unsqueeze(1).to_broadcast(shape)

            def wide(a):
                return a.unsqueeze(2).to_broadcast(shape)

            dve.wait_ge(r["lg_ps"], 4 * (n + 1))
            ins = nc.vector.tensor_copy(lg[:].rearrange("p k e -> p (k e)"), psS[0][:, 0:P])
            ins.then_inc(r["lg"], 1)
            dve.wait_ge(r["lg"], n + 1)
            for i in range(2):
                link(nc.vector.tensor_reduce(v12[:, i, :], lg[:], AX_X, ALU.max))
                link(nc.vector.tensor_tensor(out=ea[:], in0=lg[:], in1=wide(v12[:, i, :]), op=ALU.is_equal))
                link(nc.vector.tensor_tensor(out=ea[:], in0=ea[:], in1=desc, op=ALU.mult))
                link(nc.vector.tensor_reduce(slotf[:, 0, :], ea[:], AX_X, ALU.max))
                link(nc.vector.tensor_tensor(out=pick[i][:], in0=desc, in1=wide(slotf[:, 0, :]), op=ALU.is_equal))
                if i == 0:
                    link(nc.vector.scalar_tensor_tensor(out=lg[:], in0=pick[0][:], scalar=-1e38, in1=lg[:],
                                                        op0=ALU.mult, op1=ALU.add))
            nc.vector.tensor_tensor(out=v12[:, 2, :], in0=v12[:, 1, :], in1=v12[:, 0, :],
                                    op=ALU.subtract).then_inc(r["d12"], 1)
            nc.vector.tensor_tensor(out=pickb[:], in0=pick[0][:], in1=pick[1][:], op=ALU.add).then_inc(r["pickb"], 1)
            dve.wait_ge(r["e12"], n + 1)
            w = wgt[g]
            link(nc.vector.tensor_scalar(slotf[:, 0, :], e1[:], 1.0, None, ALU.add))
            link(nc.vector.reciprocal(slotf[:, 1, :], slotf[:, 0, :]))
            link(nc.vector.tensor_scalar(w[:, 0, :], slotf[:, 1, :], DEPTH_SCALE, None, ALU.mult))
            link(nc.vector.tensor_tensor(out=w[:, 1, :], in0=w[:, 0, :], in1=e1[:], op=ALU.mult))
            dve.wait_ge(r["cnt_ps"], n + 1)
            cnt = psS[1][:, P:2 * P].rearrange("p (k e) -> p k e", e=E)
            pre = psS[1][:, 0:P].rearrange("p (k e) -> p k e", e=E)
            link(nc.vector.tensor_copy(ea[:], cnt))
            a, b = ea, eb
            for sh in (1, 2, 4, 8):
                nc.vector.tensor_copy(b[:, 0:sh, :], a[:, 0:sh, :])
                link(nc.vector.tensor_tensor(out=b[:, sh:, :], in0=a[:, sh:, :], in1=a[:, :GBLK - sh, :], op=ALU.add))
                a, b = b, a
            link(nc.vector.tensor_scalar(pc[:, 0, :], a[:, GBLK - 1, :], float(P - 1), None, ALU.add))
            link(nc.vector.tensor_copy(pci[:, 0, :], pc[:, 0, :]))
            link(nc.vector.tensor_scalar(pci[:, 1, :], pci[:, 0, :], 7, None, ALU.logical_shift_right))
            link(nc.vector.tensor_scalar(pci[:, 0, :], pci[:, 1, :], 7, None, ALU.logical_shift_left))
            link(nc.vector.tensor_copy(pc[:, 0, :], pci[:, 0, :]))
            c, d = 0, 1
            for sh in (1, 2, 4):
                nc.vector.tensor_copy(pc[:, d, 0:sh], pc[:, c, 0:sh])
                link(nc.vector.tensor_tensor(out=pc[:, d, sh:], in0=pc[:, c, sh:], in1=pc[:, c, :E - sh], op=ALU.add))
                c, d = d, (2 if d == 1 else 1)
            end = pc[:, c, :]
            link(nc.vector.tensor_tensor(out=pc[:, 3, :], in0=end, in1=pc[:, 0, :], op=ALU.subtract))
            link(nc.vector.tensor_tensor(out=b[:], in0=a[:], in1=cnt, op=ALU.subtract))
            link(nc.vector.tensor_tensor(out=a[:], in0=b[:], in1=pre, op=ALU.add))
            link(nc.vector.tensor_tensor(out=b[:], in0=a[:], in1=pc[:, 3, :].unsqueeze(1).to_broadcast(shape),
                                         op=ALU.add))
            for i in range(2):
                link(nc.vector.tensor_tensor(out=a[:], in0=b[:], in1=pick[i][:], op=ALU.mult))
                link(nc.vector.tensor_reduce(slotf[:, i, :], a[:], AX_X, ALU.add))
            tile0 = cst[0:1, CST_TILE:CST_TILE + NT]
            link(nc.vector.tensor_tensor(out=cmpt[:], in0=pc[0:1, c, :].unsqueeze(1).to_broadcast([1, NT, E]),
                                         in1=tile0.unsqueeze(2).to_broadcast([1, NT, E]), op=ALU.is_le))
            link(nc.vector.tensor_reduce(tef[:], cmpt[:], AX_X, ALU.add))
            link(nc.vector.tensor_scalar(tef[:], tef[:], float(E - 1), float(HID), ALU.min, ALU.mult))
            nc.vector.tensor_copy(te[g][:], tef[:]).then_inc(r["slots"], 1)
            nc.vector.tensor_copy(slot[g][:], slotf[:]).then_inc(r["slots"], 1)

        def pool_scatter(pool, n):
            g = n % G
            pool.wait_ge(r_sem["slots"], 2 * (n + 1))
            for i in range(2):
                for k in range(GBLK):
                    nc.gpsimd.indirect_dma_start(
                        xg[g], bass.IndirectOffsetOnAxis(ap=slot[g][:, i, k:k + 1], axis=0),
                        xn[:, g * GBLK + k, :], None).then_inc(r_scat[g], 16)

        def pool_gather(pool, n):
            g = n % G
            for i in range(2):
                pool.wait_ge(f_st[i], 16 * (NT // 2) * (n + 1))
            if g == 1:
                pool.wait_ge(r_scat[0], 16 * 2 * GBLK * (n // G + 1))
                pool.wait_ge(r_scat[1], 16 * 2 * GBLK * (n // G + 1))
            for k in range(GBLK):
                for i in range(2):
                    nc.gpsimd.indirect_dma_start(
                        gb[g][:, 2 * k + i, :], None, eo[g],
                        bass.IndirectOffsetOnAxis(ap=slot[g][:, i, k:k + 1], axis=0)).then_inc(r_gat[g][k // 4], 16)

        def dve_combine(dve, n):
            g = n % G
            r = r_sem
            for i in range(2):
                for k in range(GBLK):
                    blk = x[:, g * GBLK + k, :]
                    if k % 4 == 0:
                        dve.wait_ge(r_gat[g][k // 4], 16 * 8 * (n // G + 1))
                    if i == 1:
                        dve.wait_ge(r["x"], 2 * GBLK * n + k + 1)
                    nc.vector.scalar_tensor_tensor(out=blk, in0=gb[g][:, 2 * k + i, :], scalar=wgt[g][:, i, k:k + 1],
                                                   in1=blk, op0=ALU.mult, op1=ALU.add).then_inc(r["x"], 1)
            dve.wait_ge(r["x"], 2 * GBLK * (n + 1))

        def tile_loop(step, eng, n):
            for k in range(4):
                step(eng, n, k, k % 2)
            with eng.Fori(4, NT - 3, 2) as k:
                step(eng, n, k, 0)
                step(eng, n, k + 1, 1)
            for k in range(NT - 2, NT + 2):
                step(eng, n, k, k % 2)

        def live(k, d):
            return not isinstance(k, int) or 0 <= k + d < NT

        def pe_tile(pe, n, k, p):
            f, n0, g = f_sem, n * NT, n % G

            def tokens(t, p):
                after(pe, f_ld[p], 16 * (n * NT // 2) + 8 * (t - p) + 16)
                after(pe, f["xT"], n0 + t)
                nc.tensor.transpose(psM[:, 0:P], xin[p][:], ident[:]).then_inc(f["T_ps"], 1)

            if isinstance(k, int) and k == 0:
                tokens(0, 0)
            if live(k, 0):
                e = pe.value_load(te[g][0:1, bass.ds(k, 1)], min_val=0, max_val=(E - 1) * HID)
                after(pe, f["xT"], n0 + k + 1)
                after(pe, f["silu"], n0 + k - 1)
                after(pe, f["h"], n0 + k - 1)
                nc.tensor.matmul(psS[p][:], xTt[p][:], wg[:, bass.ds(e, HID)], start=True, stop=True)
                nc.tensor.matmul(psT[p][:], xTt[p][:], wu[:, bass.ds(e, HID)],
                                 start=True, stop=True).then_inc(f["gu"], 1)
            if live(k, 1):
                tokens(k + 1, 1 - p)
            if live(k, -1):
                after(pe, f["h"], n0 + k)
                for half_, done in ((0, "hTa"), (1, "hTb")):
                    after(pe, f[done], n0 + k - 1)
                    for m in range(2):
                        hb = 2 * half_ + m
                        last = nc.tensor.transpose(psO[half_][:, m * P:(m + 1) * P],
                                                   hh[1 - p][:, hb * P:(hb + 1) * P], ident[:])
                    last.then_inc(f["hT_ps"], 1)
            if live(k, -2):
                e = pe.value_load(te[g][0:1, bass.ds(k - 2, 1)], min_val=0, max_val=(E - 1) * HID)
                after(pe, f["hTa"], n0 + k - 1)
                after(pe, f["hTb"], n0 + k - 1)
                after(pe, f["y"], n0 + k - 2)
                for hb in range(HB):
                    last = nc.tensor.matmul(psN[:, 0:P], hT[p][:, hb, :], wd[:, bass.ds(e + hb * P, P)],
                                            start=(hb == 0), stop=(hb == HB - 1))
                last.then_inc(f["y_ps"], 1)

        def act_tile(act, n, k, p):
            f, n0 = f_sem, n * NT

            def tokens(t, p):
                after(act, f["T_ps"], n0 + t + 1)
                after(act, f["gu"], n0 + t - 1)
                nc.scalar.activation(xTt[p][:], psM[:, 0:P], ACT.Copy).then_inc(f["xT"], 1)

            if isinstance(k, int) and k == 0:
                tokens(0, 0)
            if live(k, 1):
                tokens(k + 1, 1 - p)
            if live(k, 0):
                after(act, f["gu"], n0 + k + 1)
                after(act, f["h"], n0 + k - 1)
                nc.scalar.activation(sg[p][:], psS[p][:], ACT.Silu).then_inc(f["silu"], 1)
            if live(k, -1):
                after(act, f["hT_ps"], 2 * (n0 + k) - 1)
                after(act, f["y_ps"], n0 + k - 2)
                nc.scalar.activation(hT[1 - p][:, 0:2, :], psO[0][:, 0:2 * P].rearrange("p (a c) -> p a c", a=2),
                                     ACT.Copy).then_inc(f["hTa"], 1)

        def dve_tile(dve, n, k, p):
            f, n0 = f_sem, n * NT
            if live(k, -1):
                after(dve, f["hT_ps"], 2 * (n0 + k))
                after(dve, f["y_ps"], n0 + k - 2)
                nc.vector.tensor_copy(hT[1 - p][:, 2:4, :],
                                      psO[1][:, 0:2 * P].rearrange("p (a c) -> p a c", a=2)).then_inc(f["hTb"], 1)
            if live(k, 0):
                after(dve, f["silu"], n0 + k + 1)
                after(dve, f["hT_ps"], 2 * (n0 + k - 1))
                nc.vector.tensor_tensor(out=hh[p][:], in0=sg[p][:], in1=psT[p][:], op=ALU.mult).then_inc(f["h"], 1)
            if live(k, -2):
                after(dve, f["y_ps"], n0 + k - 1)
                after(dve, f_st[p], 16 * (n * NT // 2) + 8 * (k - 2 - p))
                nc.vector.tensor_copy(ysb[p][:], psN[:, 0:P]).then_inc(f["y"], 1)

        def sp_tile(sp, n, k, p):
            f, n0, g = f_sem, n * NT, n % G

            def load(t, p, row0):
                sp.dma_start(xin[p][:], xg[g][bass.ds(row0, P), :]).then_inc(f_ld[p], 16)

            if isinstance(k, int) and k == 0:
                for t in range(2):
                    after(sp, f["T_ps"], n0)
                    load(t, t, t * P)
            if live(k, 2):
                used, row0 = fixed(sp, n0 + k + 1), fixed(sp, (k + 2) * P)
                after(sp, f["T_ps"], used)
                load(k + 2, p, row0)
            if live(k, -2):
                ready, row0 = fixed(sp, n0 + k - 1), fixed(sp, (k - 2) * P)
                after(sp, f["y"], ready)
                sp.dma_start(eo[g][bass.ds(row0, P), :], ysb[p][:]).then_inc(f_st[p], 16)

        block = ctx.enter_context(nc.Block())

        def load_layer(sp, L, weights, biases):
            for i, w in enumerate(weights):
                sp.dma_start(L.w_in[:, i, :], w).then_inc(L.s["w"], 16)
            for i, b in enumerate(biases):
                sp.dma_start(L.b_in[0:1, i, :], b.rearrange("(a n) -> a n", a=1)).then_inc(L.s["w"], 16)

        def sp_ffn(sp, l):
            for g in range(G):
                n = 2 * l + g
                sp.wait_ge(r_scat[g], 16 * 2 * GBLK * (l + 1))
                if l > 0:
                    for q in range(4):
                        sp.wait_ge(r_gat[g][q], 16 * 8 * l)
                tile_loop(sp_tile, sp, n)

        @block.sync
        def _(sp):
            sp.dma_start(x[:], x_dram).then_inc(s_xin, 16)
            load_layer(sp, LA, [A["L0_attn_a_w" + c] for c in "qkvo"], [A["L0_attn_a_b" + c] for c in "qkvo"])
            sp.dma_start(cst[:], A["const"]).then_inc(s_cst, 16)
            pipeline(sp_step, sp, LA)
            sp_ffn(sp, 0)
            pipeline(sp_step, sp, LB)
            sp_ffn(sp, 1)
            sp.wait_ge(r_sem["x"], 2 * GBLK * 4)
            sp.dma_start(out_dram, x[:]).then_inc(s_out, 16)
            sp.wait_ge(s_out, 16)

        @block.gpsimd
        def _(pool):
            nc.gpsimd.memset(ident[:], 0.0).then_inc(s_const, 1)
            nc.gpsimd.memset(trib[:], 0.0).then_inc(s_const, 1)
            nc.gpsimd.memset(tick[:], 0.0).then_inc(s_const, 1)
            pool.wait_ge(s_const, 3)
            nc.gpsimd.affine_select(out=ident[:], in_=ident[:], compare_op=ALU.not_equal, fill=1.0, base=0,
                                    pattern=[[-1, P]], channel_multiplier=1).then_inc(s_const, 1)
            nc.gpsimd.affine_select(out=trib[:], in_=trib[:], compare_op=ALU.is_ge, fill=NEG, base=0,
                                    pattern=[[-1, P]], channel_multiplier=1).then_inc(s_const, 1)
            for r in range(RING):
                ins = nc.gpsimd.memset(kst[r][:], -1.0)
            ins.then_inc(s_mset, 1)
            load = pool.dma_start
            nc.gpsimd.memset(zero[:], 0.0).then_inc(s_zero, 1)
            pool.wait_ge(s_zero, 1)
            for g in range(G):
                load(xg[g].rearrange("(t p) d -> p t d", p=P),
                     zero[:].unsqueeze(1).to_broadcast([P, NT, D])).then_inc(s_zfill, 16)
            load(wr[:], A["L0_ffn_Wr"]).then_inc(s_wffn, 16)
            load(wg[:].rearrange("p (e h) -> p e h", e=E), A["L0_ffn_Wg"].rearrange("e c h -> c e h")).then_inc(s_wffn, 16)
            load(wu[:].rearrange("p (e h) -> p e h", e=E), A["L0_ffn_Wu"].rearrange("e c h -> c e h")).then_inc(s_wffn, 16)
            load(wd[:].rearrange("p (e k d) -> p e k d", e=E, k=HB),
                 A["L0_ffn_Wd"].rearrange("e (k p) d -> p e k d", p=P)).then_inc(s_wffn, 16)
            for i in range(3):
                load(LB.w_in[:, i, :], A["L0_attn_b_W_qkv"][:, i * D:(i + 1) * D]).then_inc(LB.s["w"], 16)
                load(LB.b_in[0:1, i, :],
                     A["L0_attn_b_b_qkv"][i * D:(i + 1) * D].rearrange("(a n) -> a n", a=1)).then_inc(LB.s["w"], 16)
            load(LB.w_in[:, 3, :], A["L0_attn_b_W_proj"]).then_inc(LB.s["w"], 16)
            load(LB.b_in[0:1, 3, :], A["L0_attn_b_b_proj"].rearrange("(a n) -> a n", a=1)).then_inc(LB.s["w"], 16)
            pipeline(pool_step, pool, LA)
            for l in range(2):
                pool.wait_ge(s_zfill, 32)
                pool_scatter(pool, 2 * l)
                pool_scatter(pool, 2 * l + 1)
                pool_gather(pool, 2 * l)
                pool_gather(pool, 2 * l + 1)
                if l == 0:
                    pool.wait_ge(s_half, 2)
                    pipeline(pool_step, pool, LB)

        @block.scalar
        def _(act):
            act_setup(act, LA)
            pipeline(act_step, act, LA)
            for l in range(2):
                layer_over(act, (LA, LB)[l])
                act_route(act, 2 * l)
                act_route(act, 2 * l + 1)
                tile_loop(act_tile, act, 2 * l)
                tile_loop(act_tile, act, 2 * l + 1)
                if l == 0:
                    ffn_over(act, 1)
                    act_setup(act, LB)
                    act.wait_ge(r_sem["x"], 4 * GBLK)
                    pipeline(act_step, act, LB)

        @block.vector
        def _(dve):
            for r in range(RING):
                link(nc.vector.memset(vp[r][:], 0.0))
                nc.vector.memset(vp[r][:, :, :, HD:HD + 1], 1.0)
            nc.vector.memset(ones_row[:], 1.0).then_inc(s_const_dve, 1)
            dve.wait_ge(s_const, 5)
            nc.vector.tensor_copy(identb[:], ident[:]).then_inc(s_const_dve, 1)
            dve_setup(dve, LA)
            dve.wait_ge(s_xin, 16)
            dve_ln_stats(dve, 0, NBLK, s_const_dve)
            nc.vector.memset(half[0:1, 0, :], -0.5).then_inc(s_half, 1)
            nc.vector.memset(half[0:1, 1, :], 1.5).then_inc(s_half, 1)
            dve.wait_ge(s_cst, 16)
            nc.vector.memset(onesb[:], 1.0).then_inc(s_half, 1)
            nc.vector.tensor_copy(triu[:], cst[:, CST_TRIU:CST_TRIU + P]).then_inc(s_half, 1)
            dve.wait_ge(s_const_dve, 3)
            pipeline(dve_step, dve, LA)
            for l in range(2):
                layer_over(dve, (LA, LB)[l])
                for g in range(G):
                    dve_route_in(dve, 2 * l + g)
                    dve_route(dve, 2 * l + g)
                tile_loop(dve_tile, dve, 2 * l)
                tile_loop(dve_tile, dve, 2 * l + 1)
                dve_combine(dve, 2 * l)
                dve_combine(dve, 2 * l + 1)
                if l == 0:
                    dve_setup(dve, LB)
                    dve_ln_stats(dve, 0, NBLK, s_lnB)
                    dve.wait_ge(s_lnB, 1)
                    pipeline(dve_step, dve, LB)

        @block.tensor
        def _(pe):
            pe.wait_ge(s_const, 5)
            pe_setup(pe, LA)
            pipeline(pe_step, pe, LA)
            for l in range(2):
                layer_over(pe, (LA, LB)[l])
                pe.wait_ge(s_wffn, 16 * 4)
                pe.wait_ge(s_half, 4)
                pe_route(pe, 2 * l)
                pe_route(pe, 2 * l + 1)
                pe.wait_ge(r_sem["slots"], 2 * (2 * l + 2))
                tile_loop(pe_tile, pe, 2 * l)
                tile_loop(pe_tile, pe, 2 * l + 1)
                if l == 0:
                    ffn_over(pe, 1)
                    pe_setup(pe, LB)
                    pipeline(pe_step, pe, LB)


def constants():
    import numpy as np
    c = np.zeros((P, CST_COLS), np.float32)
    c[:, CST_DESC:CST_DESC + E] = E - np.arange(E)
    c[:, CST_TILE:CST_TILE + NT] = P * np.arange(NT)
    p = np.arange(P)
    c[:, CST_HEAD:CST_HEAD + P] = p[:, None] // HD == p[None, :] // HD
    c[:, CST_TRIU:CST_TRIU + P] = p[:, None] < p[None, :]
    return c


_INS = ['L0_attn_a_x', 'L0_attn_a_wq', 'L0_attn_a_bq', 'L0_attn_a_wk', 'L0_attn_a_bk', 'L0_attn_a_wv',
        'L0_attn_a_bv', 'L0_attn_a_wo', 'L0_attn_a_bo', 'L0_attn_b_W_qkv', 'L0_attn_b_b_qkv',
        'L0_attn_b_W_proj', 'L0_attn_b_b_proj', 'L0_ffn_Wr', 'L0_ffn_Wg', 'L0_ffn_Wu', 'L0_ffn_Wd']
_OUTS = [((16, 256, 128), 'float32')]


def kernel(**inputs):
    import numpy as _np
    import concourse.bacc as _bacc
    from concourse import mybir as _mybir
    from concourse.bass_utils import run_bass_kernel_spmd as _run

    nc = _bacc.Bacc("TRN2", target_bir_lowering=False, num_devices=1)
    arrays, args = {}, {}
    for name in _INS:
        a = _np.ascontiguousarray(inputs[name])
        arrays[f"in_{name}"] = a
        args[name] = nc.dram_tensor(f"in_{name}", a.shape, _mybir.dt.from_np(a.dtype), kind="ExternalInput").ap()
    arrays["in_const"] = constants()
    args["const"] = nc.dram_tensor("in_const", (P, CST_COLS), F32, kind="ExternalInput").ap()
    shape, dtype = _OUTS[0]
    out = nc.dram_tensor("out_0", shape, _mybir.dt.from_np(_np.dtype(dtype)), kind="ExternalOutput").ap()
    build(nc, args, out)
    r = _run(nc, [arrays], core_ids=[0])
    return r.results[0]["out_0"]
```

```python
from contextlib import ExitStack

import concourse.bass as bass
from concourse import mybir

F32 = mybir.dt.float32
BF16 = mybir.dt.bfloat16
I32 = mybir.dt.int32
ALU = mybir.AluOpType
ACT = mybir.ActivationFunctionType
AX_X = mybir.AxisListType.X

P = 128
B, T, D = 16, 256, 128
H, HD = 16, 8
NBLK = B * T // P
TERMS = 6
ROWS = TERMS * HD
E, HID = 8, 512
HB = HID // P
G = 2
GBLK = NBLK // G
NT = 2 * GBLK + E - 1
CST_DESC, CST_TILE, CST_HEAD, CST_TRIU = 0, E, E + NT, E + NT + P
CST_COLS = CST_TRIU + P
EPS = 1e-5
NEG = -3.0e38
DEPTH_SCALE = float(12.0 ** -0.5)
PCH = 23
POS = [8 * (h // 8) + 4 * (h % 2) + (h % 8) // 2 for h in range(H)]
RING = 3
RSQRT_MAGIC = float(0x5F3759DF)


def after(eng, sem, value):
    if isinstance(value, int) and value <= 0:
        return
    eng.wait_ge(sem, value)


def fixed(eng, value):
    if not isinstance(value, int):
        eng.compute_val(value)
    return value


class Layer:
    pass


def build(nc, A, out):
    with ExitStack() as ctx:
        def sb(name, shape, dt=F32):
            return ctx.enter_context(nc.sbuf_tensor(name, shape, dt))

        def psum(name):
            return ctx.enter_context(nc.psum_tensor(name, [P, 512], F32))

        def sem(name):
            return ctx.enter_context(nc.semaphore(name))

        def dram(name, shape, dt=F32):
            return nc.dram_tensor(name, shape, dt, kind="Internal").ap()

        psS = [psum("psS0"), psum("psS1")]
        psT = [psum("psT0"), psum("psT1")]
        psO = [psum("psO0"), psum("psO1")]
        psM = psum("psM")
        psN = psum("psN")

        x = sb("x", [P, NBLK, D])
        cst = sb("cst", [P, CST_COLS])
        mean_rstd = sb("mean_rstd", [P, NBLK, 2])
        bn6 = sb("bn6", [P, NBLK, 6])
        nwt = sb("nwt", [P, 3, NBLK])
        ident = sb("ident", [P, P])
        identb = sb("identb", [P, P], BF16)
        trib = sb("trib", [P, P], BF16)
        tick = sb("tick", [1, 2])
        ones_row = sb("ones_row", [1, T])
        xs = sb("xs", [P, 2, D])
        xT = [sb(f"xT{r}", [P, T]) for r in range(RING)]
        qk = sb("qk", [P, 2, T])
        rest = sb("rest", [P, 2, T])
        part = sb("part", [P, 2, 3, T], BF16)
        qst = [sb(f"qst{r}", [P, 8, T], BF16) for r in range(RING)]
        kst = [sb(f"kst{r}", [P, 8, T], BF16) for r in range(RING)]
        vp = [sb(f"vp{r}", [P, 2, H, 32]) for r in range(RING)]
        mx3 = sb("mx3", [P, 2, 3, 8])
        mxu = sb("mxu", [P, 2, 2, 8])
        mrow = sb("mrow", [8, 2, T], BF16)
        pT = sb("pT", [P, 8, 512])
        oT = sb("oT", [P, 4, T])
        rden = sb("rden", [P, H])
        on = sb("on", [P, D])
        onT = sb("onT", [P, D])

        head_ones = cst[:, CST_HEAD:CST_HEAD + P]
        absq = sb("absq", [P, T])
        junk = sb("junk", [P, 3, T])
        st = sb("st", [P, 4])
        row = sb("row", [1, 56])
        prow = sb("prow", [1, 8, H])
        half = sb("half", [1, 2, H])
        scb = [sb(f"scb{r}", [P, 2, H]) for r in range(RING)]
        neg_shift = [sb(f"neg_shift{r}", [8, 2]) for r in range(RING)]

        wg = sb("wg", [P, E * HID])
        wu = sb("wu", [P, E * HID])
        wd = sb("wd", [P, E * HID])
        wr = sb("wr", [P, E])
        xn = sb("xn", [P, NBLK, D])
        gb = [pT[:].rearrange("p a (b c) -> p (a b) c", c=D), xn[:]]
        triu = sb("triu", [P, P], BF16)
        onesb = sb("onesb", [P, P], BF16)
        zero = sb("zero", [P, D])
        xnT = [sb(f"xnT{i}", [P, 4 * P]) for i in range(4)]
        lg = sb("lg", [P, GBLK, E])
        ea = sb("ea", [P, GBLK, E])
        eb = sb("eb", [P, GBLK, E])
        pick = [sb(f"pick{i}", [P, GBLK, E]) for i in range(2)]
        pickb = sb("pickb", [P, GBLK, E], BF16)
        v12 = sb("v12", [P, 3, GBLK])
        e1 = sb("e1", [P, GBLK])
        slotf = sb("slotf", [P, 2, GBLK])
        slot = [sb(f"slot{g}", [P, 2, GBLK], I32) for g in range(G)]
        wgt = [sb(f"wgt{g}", [P, 2, GBLK]) for g in range(G)]
        pc = sb("pc", [P, 4, E])
        pci = sb("pci", [P, 2, E], I32)
        cmpt = sb("cmpt", [1, NT, E])
        tef = sb("tef", [1, NT])
        te = [sb(f"te{g}", [1, NT], I32) for g in range(G)]
        xin = [sb(f"xin{i}", [P, D]) for i in range(2)]
        xTt = [sb(f"xTt{i}", [P, P]) for i in range(2)]
        sg = [sb(f"sg{i}", [P, HID]) for i in range(2)]
        hh = [sb(f"hh{i}", [P, HID]) for i in range(2)]
        hT = [sb(f"hT{i}", [P, HB, P]) for i in range(2)]
        ysb = [sb(f"ysb{i}", [P, D]) for i in range(2)]

        xg = [dram(f"xg{g}", (NT * P, D)) for g in range(G)]
        eo = [dram(f"eo{g}", (NT * P, D)) for g in range(G)]
        scr_part = dram("scr_part", (2, P, TERMS, T), BF16)
        scr_m = dram("scr_m", (2, 8, 2, T), BF16)

        x_dram = A["L0_attn_a_x"].rearrange("b (k p) d -> p (b k) d", p=P)
        out_dram = out.rearrange("b (k p) d -> p (b k) d", p=P)

        s_xin = sem("s_xin")
        s_xrest = sem("s_xrest")
        s_lnA = sem("s_lnA")
        s_const = sem("s_const")
        s_const_dve = sem("s_const_dve")
        s_chain = sem("s_chain")
        s_ln = [sem("s_ln0"), sem("s_ln1"), sem("s_ln2"), sem("s_ln3")]
        s_out = sem("s_out")
        s_mset = sem("s_mset")
        s_cst = sem("s_cst")
        s_half = sem("s_half")
        s_lnB = sem("s_lnB")
        s_wffn = sem("s_wffn")
        s_zero = sem("s_zero")
        s_zfill = sem("s_zfill")
        r_sem = {n: sem("R_" + n) for n in ["xn", "T_ps", "T", "lg_ps", "lg", "d12", "e12", "pickb", "cnt_ps",
                                            "slots", "x"]}
        r_scat = [sem(f"R_scat{g}") for g in range(G)]
        r_gat = [[sem(f"R_gat{g}{q}") for q in range(4)] for g in range(G)]
        f_sem = {n: sem("F_" + n) for n in ["T_ps", "xT", "gu", "silu", "h", "hT_ps", "hTa", "hTb", "y_ps", "y"]}
        f_ld = [sem(f"F_ld{i}") for i in range(2)]
        f_st = [sem(f"F_st{i}") for i in range(2)]
        chain = [0]

        def link(ins):
            chain[0] += 1
            ins.then_inc(s_chain, 1)
            nc.vector.wait_ge(s_chain, chain[0])

        SEMS = ["w", "w_vo", "wp", "bcol_ps", "bcol", "xs", "xT_ps", "xT", "qk_ps", "qk", "split", "scr_w", "stack",
                "S", "mx", "mxu", "mT", "m1", "m2", "mscr", "mrow", "ST", "exp", "pT", "PV", "oT", "tO_ps",
                "rden", "on", "onT_ps", "onT", "y", "x1", "v_ps", "v",
                "col", "qsum_ps", "qsum", "row_ps", "row", "pool", "bc_ps", "bc", "seed"]

        def layer(tag, causal):
            L = Layer()
            L.tag, L.causal = tag, causal
            L.s = {n: sem(f"{tag}_{n}") for n in SEMS}
            L.w_in = sb(f"w_in{tag}", [P, 4, D])
            L.w_perm = sb(f"w_perm{tag}", [P, 2, D])
            L.b_in = sb(f"b_in{tag}", [1, 4, D])
            L.b_perm = sb(f"b_perm{tag}", [1, 2, D])
            L.b_col = sb(f"b_col{tag}", [P, 2])
            L.pe_hook = L.act_hook = L.dve_hook = L.pool_hook = L.sp_hook = None
            return L

        LA = layer("A", True)
        LB = layer("B", False)
        LB.s["pT"] = LB.s["exp"]

        def kcols(L):
            return 384 if L.causal else 512

        def pe_setup(pe, L):
            s = L.s
            pe.wait_ge(s["wp"], 4)
            pe.wait_ge(s_const_dve, 2)
            for o in range(2):
                last = nc.tensor.matmul(psM[:, o:o + 1], L.b_perm[0:1, o, :], ones_row[0:1, 0:1],
                                        start=(o == 0), stop=True, skip_group_check=True)
            last.then_inc(s["bcol_ps"], 1)

        def pe_step(pe, L, j, c, P_, V_, S_, T_, O_):
            s = L.s
            bS, bT, bO = j - 2, j - 3, j - 4
            rP, rS, rT, rO = c % 3, (c - 2) % 3, (c - 3) % 3, (c - 4) % 3
            cols = kcols(L)

            def pv_quad(b, r, q):
                after(pe, s["pT"], 16 * b + 4 * q + 4)
                if q % 2 == 0:
                    after(pe, s["oT"], 2 * (b - 1) + q // 2 + 1)
                for kb in range(2):
                    for i in range(4):
                        h = 4 * q + i
                        if kb == 0:
                            dst, src = (0, T), (0, T)
                        elif L.causal:
                            dst, src = (P, T), (T, T + P)
                        else:
                            dst, src = (0, T), (T, 2 * T)
                        o0 = (q % 2) * T
                        last = nc.tensor.matmul(psO[q // 2][32 * i:32 * i + 32, o0 + dst[0]:o0 + dst[1]],
                                                vp[r][:, kb, h, :], pT[:, h % 8, src[0]:src[1]],
                                                start=(kb == 0), stop=(kb == 1), skip_group_check=True)
                last.then_inc(s["PV"], 1)

            def out_transposes(qb):
                for q in range(4):
                    last = nc.tensor.transpose(psN[:, q * P:(q + 1) * P], oT[:, q, qb * P:(qb + 1) * P], ident[:])
                last.then_inc(s["tO_ps"], 1)

            def out_transpose_on(qb):
                after(pe, s["on"], 2 * bO + qb + 1)
                nc.tensor.transpose(psN[:, 0:P], on[:], ident[:]).then_inc(s["onT_ps"], 1)

            def out_project(qb):
                after(pe, s["onT"], 2 * bO + qb + 1)
                nc.tensor.matmul(psN[:, P:2 * P], onT[:], L.w_in[:, 3, :], start=True, stop=False)
                nc.tensor.matmul(psN[:, P:2 * P], ones_row[0:1, 0:P], L.b_in[0:1, 3, :],
                                 start=False, stop=True).then_inc(s["y"], 1)

            def max_transposes(b, u):
                for qb in range(2):
                    src = mxu if L.causal else mx3
                    last = nc.tensor.transpose((psM, psN)[u][0:8, qb * P:(qb + 1) * P], src[:, u, qb, :], ident[:])
                last.then_inc(s["mT"], 1)

            for h in range(H):
                par, t = h % 2, h // 2
                r64 = slice(64 * par, 64 * par + ROWS)
                m64 = slice(64 * par, 64 * par + ROWS + 2)
                if S_:
                    if h == 0:
                        after(pe, s["stack"], 64 * (bS + 1))
                    after(pe, s["mx"], 16 * bS + h - 1)
                    ps, q_, k_ = psS[h % 2], qst[rS], kst[rS]
                    if L.causal:
                        for c0, k in ((0, 0), (P, 1)):
                            nc.tensor.matmul(ps[:, c0:c0 + P], q_[r64, t, k * P:(k + 1) * P],
                                             k_[r64, t, k * P:(k + 1) * P],
                                             start=True, stop=False, skip_group_check=True)
                            nc.tensor.matmul(ps[:, c0:c0 + P], identb[:], trib[:],
                                             start=False, stop=True, skip_group_check=True)
                        nc.tensor.matmul(ps[:, 2 * P:3 * P], q_[r64, t, P:T], k_[r64, t, 0:P],
                                         start=True, stop=True, skip_group_check=True).then_inc(s["S"], 1)
                    else:
                        nc.tensor.matmul(ps[:, 0:T], q_[r64, t, 0:P], k_[r64, t, :],
                                         start=True, stop=True, skip_group_check=True)
                        nc.tensor.matmul(ps[:, T:2 * T], q_[r64, t, P:T], k_[r64, t, :],
                                         start=True, stop=True, skip_group_check=True).then_inc(s["S"], 1)
                if T_:
                    if h % 8 == 0:
                        after(pe, s["mrow"], 32 * (2 * bT + h // 8 + 1))
                    after(pe, s["exp"], 16 * bT + h - 1)
                    ps, q_, k_ = psT[h % 2], qst[rT], kst[rT]
                    nc.tensor.matmul(ps[:, 0:T], k_[m64, t, 0:P], q_[m64, t, :],
                                     start=True, stop=True, skip_group_check=True)
                    q0 = P if L.causal else 0
                    nc.tensor.matmul(ps[:, T:cols], k_[m64, t, P:T], q_[m64, t, q0:T],
                                     start=True, stop=True, skip_group_check=True).then_inc(s["ST"], 1)
                if T_ and h in (5, 9, 13):
                    pv_quad(bT, rT, (h - 5) // 4)
                if h == 1:
                    if O_:
                        pv_quad(bO, rO, 3)
                    if T_:
                        after(pe, s["mxu"] if L.causal else s["mx"], (2 if L.causal else 16) * (bT + 1))
                        after(pe, s["x1"], 2 * bO)
                        max_transposes(bT, 1)
                if h == 1 and S_ and not L.causal:
                    after(pe, s["pool"], PCH * (j - 1))
                    after(pe, s["v"], bS)
                    after(pe, s["row"], 4 * j if P_ else 4 * min(j, B))
                    nc.tensor.matmul(psM[:, 0:2 * H], ones_row[0:1, 0:P],
                                     prow[0:1, 0:2, :].rearrange("p a h -> p (a h)"),
                                     start=True, stop=True, skip_group_check=True)
                    for u in range(2):
                        last = nc.tensor.matmul(psM[0:8, 2 * H + u:2 * H + u + 1],
                                                prow[0:1, 2, 8 * u:8 * u + 8], ones_row[0:1, 0:1],
                                                start=False, stop=True, skip_group_check=True)
                    last.then_inc(s["bc_ps"], 1)
                if h == (2 if L.causal else 3) and P_:
                    after(pe, s["xs"], j + 1)
                    if not L.causal:
                        after(pe, s["bc"], 2 * (j - 1))
                        after(pe, s["row"], 4 * j)
                    after(pe, s["v"], j - 2)
                    after(pe, s["qk"], 2 * j)
                    after(pe, s["bcol"], 1)
                    after(pe, s["v_ps"], j - 4)
                    for k in range(2):
                        last = nc.tensor.transpose(psM[:, k * P:(k + 1) * P], xs[:, k, :], ident[:])
                    last.then_inc(s["xT_ps"], 1)
                if h == 5 and P_:
                    after(pe, s["xT"], j + 1)
                    for o in range(2):
                        last = nc.tensor.matmul(psM[:, o * T:(o + 1) * T], L.w_perm[:, o, :], xT[rP][:],
                                                start=(o == 0), stop=True, skip_group_check=True)
                    last.then_inc(s["qk_ps"], 1)
                if h == 12 and V_:
                    if not L.causal:
                        after(pe, s["bc"], 2 * (j - 1))
                    after(pe, s["m2"], 2 * bS + 1)
                    if P_:
                        after(pe, s["qk"], 2 * (j + 1))
                    else:
                        after(pe, s["qk"], 2 * B)
                    after(pe, s["v"], bS)
                    for k in range(2):
                        nc.tensor.matmul(psM[:, k * P:(k + 1) * P], xT[rS][:, k * P:(k + 1) * P], L.w_in[:, 2, :],
                                         start=(k == 0), stop=False, skip_group_check=True)
                        last = nc.tensor.matmul(psM[:, k * P:(k + 1) * P], ones_row[0:1, 0:P], L.b_in[0:1, 2, :],
                                                start=False, stop=True, skip_group_check=True)
                    last.then_inc(s["v_ps"], 1)
                if h == 14 and P_ and not L.causal:
                    after(pe, s["col"], 4 * j + 2)
                    after(pe, s["v"], bS + 1)
                    after(pe, s["bc"], 2 * (j - 1))
                    nc.tensor.matmul(psM[:, 0:T], head_ones, absq[:],
                                     start=True, stop=True, skip_group_check=True).then_inc(s["qsum_ps"], 1)
                if h == 15 and P_ and not L.causal:
                    after(pe, s["col"], 4 * j + 4)
                    after(pe, s["qsum"], j + 1)
                    for i in range(4):
                        last = nc.tensor.transpose(psM[0:1, i * P:(i + 1) * P], st[:, i:i + 1], ident[:])
                    last.then_inc(s["row_ps"], 1)
                if h == 4 and O_:
                    after(pe, s["oT"], 2 * bO + 2)
                    if T_:
                        after(pe, s["m2"], 2 * (bT + 1))
                    else:
                        after(pe, s["x1"], 2 * bO)
                    out_transposes(0)
                if h == 6 and O_:
                    out_transpose_on(0)
                if h == 8 and O_:
                    out_project(0)
                if h == 9 and S_:
                    after(pe, s["mxu"] if L.causal else s["mx"], 2 * bS + 1 if L.causal else 16 * bS + 8)
                    after(pe, s["qk"], 2 * (j + 1) if P_ else 2 * B)
                    after(pe, s["v"], bS)
                    if not L.causal:
                        after(pe, s["bc"], 2 * (j - 1))
                    max_transposes(bS, 0)
                if h == 11 and O_:
                    after(pe, s["x1"], 2 * bO + 1)
                    out_transposes(1)
                if h == 13 and O_:
                    out_transpose_on(1)
                if h == 14 and O_:
                    out_project(1)
                if L.pe_hook and isinstance(j, int):
                    L.pe_hook(pe, j, h)

        def act_setup(act, L):
            act.wait_ge(L.s["bcol_ps"], 1)
            nc.scalar.activation(L.b_col[:], psM[:, 0:2], ACT.Copy).then_inc(L.s["bcol"], 1)
            act.wait_ge(L.s["bcol"], 1)

        def act_step(act, L, j, c, P_, V_, S_, T_, O_):
            s = L.s
            bS, bT, bO = j - 2, j - 3, j - 4
            rP = c % 3
            cols = kcols(L)

            def split_copy(i):
                after(act, s["qk"], 2 * (j + 1))
                after(act, s["scr_w"], 96 * j)
                after(act, s["split"], 4 * j + 2 * i)
                src = qk if i == 0 else rest
                nc.scalar.activation(part[:, :, i, :], src[:], ACT.Copy).then_inc(s["split"], 1)

            def high_max(b, u, ring):
                after(act, s["mT"], 2 * b + u + 1)
                after(act, s["mscr"], 16 * (2 * b + u))
                if L.causal:
                    nc.scalar.activation(mrow[0:8, 0, :], (psM, psN)[u][0:8, 0:T], ACT.Copy).then_inc(s["m1"], 1)
                else:
                    after(act, s["bc"], 2 * (b + 1))
                    nc.scalar.activation(mrow[0:8, 0, :], (psM, psN)[u][0:8, 0:T], ACT.Identity,
                                         bias=neg_shift[ring][0:8, u:u + 1]).then_inc(s["m1"], 1)

            def evac_oT(b, half):
                after(act, s["PV"], 4 * b + 2 * half + 2)
                after(act, s["tO_ps"], 2 * b)
                nc.scalar.activation(oT[:, 2 * half:2 * half + 2, :], psO[half][:].rearrange("p (a t) -> p a t", a=2),
                                     ACT.Copy).then_inc(s["oT"], 1)

            def evac_onT(qb):
                after(act, s["onT_ps"], 2 * bO + qb + 1)
                after(act, s["y"], 2 * bO + qb)
                nc.scalar.activation(onT[:], psN[:, 0:P], ACT.Copy).then_inc(s["onT"], 1)

            for h in range(H):
                if h == 1 and T_:
                    high_max(bT, 1, (c - 3) % 3)
                if h == 2 and O_:
                    evac_oT(bO, 1)
                if h == (3 if L.causal else 4) and P_:
                    after(act, s["xT_ps"], j + 1)
                    after(act, s["v_ps"], j - 2)
                    nc.scalar.activation(xT[rP][:], psM[:, 0:T], ACT.Copy).then_inc(s["xT"], 1)
                if h in (6, 7) and P_:
                    after(act, s["qk_ps"], j + 1)
                    after(act, s["split"], 4 * j)
                    if not L.causal:
                        after(act, s["col"], 4 * j)
                    for o in (h - 6,):
                        nc.scalar.activation(qk[:, o, :], psM[:, o * T:(o + 1) * T], ACT.Identity,
                                             bias=L.b_col[:, o:o + 1]).then_inc(s["qk"], 1)
                if h == 7 and O_:
                    evac_onT(0)
                if h == 10 and S_:
                    high_max(bS, 0, (c - 2) % 3)
                if h == 14 and O_:
                    evac_onT(1)
                if L.act_hook and isinstance(j, int):
                    L.act_hook(act, j, h)
                if T_:
                    after(act, s["ST"], 16 * bT + h + 1)
                    after(act, s["PV"], 4 * bT + h // 4 - 1)
                    if L.causal:
                        nc.scalar.activation(pT[:, h % 8, 0:cols], psT[h % 2][:, 0:cols], ACT.Exp,
                                             scale=float(HD) ** -0.5).then_inc(s["exp"], 1)
                    else:
                        i = POS[h]
                        r = (c - 3) % 3
                        nc.scalar.activation(pT[:, h % 8, 0:cols], psT[h % 2][:, 0:cols], ACT.Exp,
                                             scale=scb[r][:, 0, i:i + 1],
                                             bias=scb[r][:, 1, i:i + 1]).then_inc(s["exp"], 1)
                if h in (9, 12) and P_:
                    split_copy(h // 12)
                if h == 8 and P_ and not L.causal:
                    after(act, s["qk"], 2 * j + 2)
                    after(act, s["qsum_ps"], j)
                    nc.scalar.activation(absq[:], qk[:, 0, :], ACT.Abs).then_inc(s["col"], 1)
                if h in (4, 10, 11) and P_ and not L.causal:
                    i = {4: 3, 10: 1, 11: 2}[h]
                    after(act, s["row_ps"], j)
                    after(act, s["col"], 4 * j)
                    src = (qk[:, 0, :], qk[:, 1, :], xT[rP][:])[i - 1]
                    if i == 3:
                        after(act, s["xT"], j + 1)
                    nc.scalar.activation(junk[:, i - 1, :], src, ACT.Square if i == 1 else ACT.Abs,
                                         accum_out=st[:, i:i + 1]).then_inc(s["col"], 1)
                if h == 13 and T_:
                    evac_oT(bT, 0)

        def dve_setup(dve, L):
            s = L.s
            dve.wait_ge(s["w"], 16 * 4)
            for o in range(2):
                nc.vector.tensor_copy(L.w_perm[:, o, :].rearrange("p (a t i) -> p a t i", a=2, t=8),
                                      L.w_in[:, o, :].rearrange("p (t a i) -> p a t i", a=2, t=8)).then_inc(s["wp"], 1)
                nc.vector.tensor_copy(L.b_perm[:, o, :].rearrange("p (a t i) -> p a t i", a=2, t=8),
                                      L.b_in[:, o, :].rearrange("p (t a i) -> p a t i", a=2, t=8)).then_inc(s["wp"], 1)

        def dve_step(dve, L, j, c, P_, V_, S_, T_, O_):
            s = L.s
            bS, bT, bO = j - 2, j - 3, j - 4
            rS = (c - 2) % 3
            C_ = not L.causal and (not isinstance(j, int) or 0 <= j - 1 < B)

            def split_rest(i):
                after(dve, s["qk"], 2 * (j + 1))
                after(dve, s["split"], 4 * j + 2 * i + 1)
                o = part[:, :, 2, :] if i else rest[:]
                nc.vector.tensor_tensor(out=o, in0=rest[:] if i else qk[:], in1=part[:, :, i, :],
                                        op=ALU.subtract).then_inc(s["split"], 1)

            def low_max(b, u, ring):
                after(dve, s["m1"], 2 * b + u + 1)
                shift = 0.0 if L.causal else neg_shift[ring][0:8, u:u + 1]
                nc.vector.scalar_tensor_tensor(out=mrow[0:8, 1, :], in0=(psM, psN)[u][0:8, 0:T], scalar=shift,
                                               in1=mrow[0:8, 0, :], op0=ALU.add,
                                               op1=ALU.subtract).then_inc(s["m2"], 1)

            def normalise(qb):
                after(dve, s["tO_ps"], 2 * bO + qb + 1)
                after(dve, s["onT_ps"], 2 * bO + qb)
                o4 = psN[:].rearrange("p (h c) -> p h c", c=32)
                nc.vector.reciprocal(rden[:], o4[:, :, HD]).then_inc(s["rden"], 1)
                after(dve, s["rden"], 2 * bO + qb + 1)
                nc.vector.tensor_tensor(out=on[:].rearrange("p (h c) -> p h c", c=HD), in0=o4[:, :, 0:HD],
                                        in1=rden[:].unsqueeze(2).to_broadcast([P, H, HD]),
                                        op=ALU.mult).then_inc(s["on"], 1)

            def residual(qb):
                after(dve, s["y"], 2 * bO + qb + 1)
                blk = x[:, bass.ds(2 * bO + qb, 1), :]
                nc.vector.tensor_tensor(out=blk, in0=blk, in1=psN[:, P:2 * P].unsqueeze(1),
                                        op=ALU.add).then_inc(s["x1"], 1)

            for h in range(H):
                if L.causal and ((h == 8 and S_) or (h == 0 and T_)):
                    b, u = (bS, 0) if h == 8 else (bT, 1)
                    after(dve, s["mx"], 16 * b + 8 * u + 8)
                    after(dve, s["mT"], 2 * b + u - 1)
                    nc.vector.tensor_tensor(out=mxu[:, u], in0=mx3[:, u, 0:2, :], in1=mx3[:, u, 0:3:2, :],
                                            op=ALU.max).then_inc(s["mxu"], 1)
                if S_:
                    u = h // 8
                    pos = (h % 2) * 4 + (h % 8) // 2
                    after(dve, s["S"], 16 * bS + h + 1)
                    if h % 8 == 0:
                        if L.causal:
                            after(dve, s["mxu"], 2 * bS + u - 1)
                        else:
                            after(dve, s["mT"], 2 * bS + u - 1)
                    n = 3 if L.causal else 2
                    nc.vector.tensor_reduce(mx3[:, u, 0:n, pos:pos + 1].rearrange("p a b -> p (a b)"),
                                            psS[h % 2][:, 0:kcols(L)].rearrange("p (a k) -> p a k", a=n),
                                            AX_X, ALU.max).then_inc(s["mx"], 1)
                if h == 0 and P_:
                    after(dve, s["xT_ps"], j)
                    for k in range(2):
                        blk = 2 * j + k
                        ins = nc.vector.tensor_scalar(xs[:, k, :].unsqueeze(1), x[:, bass.ds(blk, 1), :],
                                                      mean_rstd[:, bass.ds(blk, 1), 0:1].rearrange("p a b -> p (a b)"),
                                                      mean_rstd[:, bass.ds(blk, 1), 1:2].rearrange("p a b -> p (a b)"),
                                                      ALU.subtract, ALU.mult)
                    ins.then_inc(s["xs"], 1)
                if h == 2 and T_:
                    low_max(bT, 1, (c - 3) % 3)
                if h == 5 and O_:
                    normalise(0)
                if h == 9 and O_:
                    residual(0)
                if h == 3 and C_:
                    after(dve, s["pool"], PCH * (j - 1) + 2)
                    nc.vector.tensor_scalar(prow[0:1, 6, :].bitcast(I32), prow[0:1, 4, :].bitcast(I32), 1, None,
                                            ALU.logical_shift_right).then_inc(s["seed"], 1)
                    after(dve, s["seed"], 2 * j - 1)
                    nc.vector.tensor_scalar(prow[0:1, 7, :].bitcast(I32), prow[0:1, 6, :].bitcast(I32), -1.0,
                                            RSQRT_MAGIC, ALU.mult, ALU.add).then_inc(s["seed"], 1)
                if h == 1 and S_ and not L.causal:
                    r = (c - 2) % 3
                    after(dve, s["bc_ps"], j - 1)
                    after(dve, s["exp"], 16 * (j - 5) + 16)
                    nc.vector.tensor_copy(scb[r][:].rearrange("p a h -> p (a h)"),
                                          psM[:, 0:2 * H]).then_inc(s["bc"], 1)
                    nc.vector.tensor_copy(neg_shift[r][:], psM[0:8, 2 * H:2 * H + 2]).then_inc(s["bc"], 1)
                if h == 14 and P_ and not L.causal:
                    after(dve, s["qsum_ps"], j + 1)
                    after(dve, s["row_ps"], j)
                    nc.vector.tensor_reduce(st[:, 0:1], psM[:, 0:T], AX_X, ALU.max).then_inc(s["qsum"], 1)
                if h == 15 and P_ and not L.causal:
                    after(dve, s["row_ps"], j + 1)
                    after(dve, s["pool"], PCH * j)
                    for i, op in enumerate((ALU.max, ALU.add, ALU.max)):
                        for u in range(2):
                            src = psM[0:1, i * P:(i + 1) * P].rearrange("p (a u t i) -> p u a t i", a=2, u=2, i=HD)
                            ins = nc.vector.tensor_reduce(
                                row[0:1, 16 * i + 8 * u:16 * i + 8 * u + 8].rearrange("p (a t) -> p a t", a=2),
                                src[:, u], AX_X, op)
                        ins.then_inc(s["row"], 1)
                    nc.vector.tensor_reduce(row[0:1, 48:49], psM[0:1, 3 * P:4 * P], AX_X,
                                            ALU.max).then_inc(s["row"], 1)
                if h == 11 and P_:
                    split_rest(0)
                if h == 10 and S_:
                    low_max(bS, 0, (c - 2) % 3)
                if h == 13 and V_:
                    after(dve, s["v_ps"], bS + 1)
                    after(dve, s["PV"], 4 * (bS - 2))
                    nc.vector.tensor_copy(vp[rS][:, :, :, 0:HD],
                                          psM[:, 0:T].rearrange("p (k h c) -> p k h c", k=2, c=HD)).then_inc(s["v"], 1)
                if h == 12 and O_:
                    normalise(1)
                if h == 14 and P_:
                    split_rest(1)
                if h == 15 and O_:
                    residual(1)
                if L.dve_hook and isinstance(j, int):
                    L.dve_hook(dve, j, h)

        def pool_step(pool, L, j, c, P_, V_, S_, T_, O_):
            s = L.s
            bT = j - 3
            if L.pool_hook and isinstance(j, int):
                L.pool_hook(pool, j, 0)
            if not L.causal and (not isinstance(j, int) or 0 <= j - 1 < B):
                S2, C, NC, KK, V, W, SH, Y = (prow[0:1, i, :] for i in range(8))
                q_row, fro, k_col = (row[0:1, 16 * i:16 * i + 16] for i in range(3))
                inf_x = row[0:1, 48:49].to_broadcast([1, H])
                m05, p15 = half[0:1, 0, :], half[0:1, 1, :]
                mul, add = ALU.mult, ALU.add
                ops = [(W, fro, inf_x, mul), (V, W, inf_x, mul)]
                ops += [(NC, q_row, q_row, mul), (KK, k_col, k_col, mul), (NC, NC, KK, add), (NC, NC, m05, mul)]
                for it in range(3):
                    src = Y if it == 0 else S2
                    ops += [(W, src, src, mul), (W, W, V, mul), (W, W, m05, mul), (W, W, p15, add), (S2, src, W, mul)]
                ops += [(S2, S2, S2, add), (C, NC, S2, mul)]
                assert len(ops) == PCH
                after(pool, s["row"], 4 * j)
                after(pool, s["bc_ps"], j - 1)
                for n, (o, a, b_, op) in enumerate(ops):
                    if n > 0:
                        after(pool, s["pool"], PCH * (j - 1) + n)
                    if n == 6:
                        after(pool, s["seed"], 2 * j)
                    nc.gpsimd.tensor_tensor(out=o, in0=a, in1=b_, op=op).then_inc(s["pool"], 1)
            if L.causal and T_:
                fixed(pool, 16 * bT + 1)
                for h in range(H):
                    after(pool, s["exp"], 16 * bT + h + 1)
                    if h < H - 1:
                        fixed(pool, 16 * bT + h + 2)
                    else:
                        nc.gpsimd.tensor_tensor(out=tick[:, 0:1], in0=tick[:, 1:2], in1=tick[:, 1:2], op=ALU.add)
                    d = pT[:, h % 8, 0:384].rearrange("p (a k) -> p a k", a=3)[:, 0:3:2, :]
                    nc.gpsimd.affine_select(out=d, in_=d, compare_op=ALU.is_ge, fill=0.0, base=0,
                                            pattern=[[0, 2], [1, P]], channel_multiplier=-1).then_inc(s["pT"], 1)
                    if L.pool_hook and isinstance(j, int):
                        L.pool_hook(pool, j, h + 1)

        def sp_step(sp, L, j, c, P_, V_, S_, T_, O_):
            s = L.s
            bS, bT = j - 2, j - 3

            def max_rows(b, u, r):
                ready, read, written = (fixed(sp, v) for v in (2 * b + u + 1, 32 * (2 * b + u), 16 * (2 * b + u + 1)))
                after(sp, s["m2"], ready)
                after(sp, s["mrow"], read)
                sp.dma_start(scr_m[u], mrow[:]).then_inc(s["mscr"], 16)
                after(sp, s["mscr"], written)
                for par in range(2):
                    sp.dma_start(qst[r][64 * par + ROWS:64 * par + ROWS + 2, 4 * u:4 * u + 4, :],
                                 scr_m[u, 4 * par:4 * par + 4].rearrange("t k q -> k t q")).then_inc(s["mrow"], 16)

            def beside(point):
                if L.sp_hook and isinstance(j, int):
                    L.sp_hook(sp, j, point)

            if T_:
                max_rows(bT, 1, (c - 3) % 3)
            beside(0)
            if not isinstance(j, int) or 0 <= j - 1 < B:
                b, r = j - 1, (c - 1) % 3
                ready, read, written, scored = (fixed(sp, v) for v in (4 * (b + 1), 64 * b, 96 * (b + 1), 16 * (b - 2)))
                after(sp, s["split"], ready)
                after(sp, s["stack"], read)
                q3 = part[:, 0, :, :]
                k3 = part[:, 1, :, :]
                sp.dma_start(scr_part[0, :, 0:3, :], q3).then_inc(s["scr_w"], 16)
                sp.dma_start(scr_part[0, :, 3:5, :], q3[:, 0:2, :]).then_inc(s["scr_w"], 16)
                sp.dma_start(scr_part[0, :, 5:6, :], q3[:, 0:1, :]).then_inc(s["scr_w"], 16)
                sp.dma_start(scr_part[1, :, 0:3:2, :], k3[:, 0:1, :].to_broadcast([P, 2, T])).then_inc(s["scr_w"], 16)
                sp.dma_start(scr_part[1, :, 1:4:2, :], k3[:, 0:2, :]).then_inc(s["scr_w"], 16)
                sp.dma_start(scr_part[1, :, 4:6, :], k3[:, 1:3, :]).then_inc(s["scr_w"], 16)
                after(sp, s["scr_w"], written)
                after(sp, s["ST"], scored)
                after(sp, s_mset, 2 * RING)
                for o, st in enumerate((qst, kst)):
                    for par in range(2):
                        sp.dma_start(st[r][64 * par:64 * par + ROWS, :, :],
                                     scr_part[o, 64 * par:64 * par + 64].rearrange("(t i) r q -> (i r) t q", t=8)
                                     ).then_inc(s["stack"], 16)
            beside(1)
            if S_:
                max_rows(bS, 0, (c - 2) % 3)
            beside(2)
            beside(3)

        def pipeline(step, eng, L):
            def flags(j):
                return [0 <= j < B] + [0 <= j - d < B for d in (2, 2, 3, 4)]

            for j in range(7):
                step(eng, L, j, j % 3, *flags(j))
            with eng.Fori(7, B - 2, 3) as j:
                for d in range(3):
                    step(eng, L, j + d, (7 + d) % 3, True, True, True, True, True)
            for j in range(B, B + 4):
                step(eng, L, j, j % 3, *flags(j))

        def dve_ln_stats(dve, lo, hi, done):
            for k in range(lo, hi):
                ins = nc.vector.bn_stats(bn6[:, k, :], x[:, k, :])
            link(ins)
            for k in range(lo, hi):
                ins = nc.vector.bn_aggr(mean_rstd[:, k, :], bn6[:, k, :])
            link(ins)
            dve_ln_root(lo, hi, done)

        def dve_ln_root(lo, hi, done):
            ve, y, a = (nwt[:, i, lo:hi] for i in range(3))
            link(nc.vector.tensor_scalar(ve, mean_rstd[:, lo:hi, 1], EPS, None, ALU.add))
            rsqrt(ve, y, a)
            nc.vector.tensor_copy(mean_rstd[:, lo:hi, 1], y).then_inc(done, 1)

        def rsqrt(v, y, a):
            link(nc.vector.tensor_scalar(a.bitcast(I32), v.bitcast(I32), 1, None, ALU.logical_shift_right))
            link(nc.vector.tensor_scalar(y.bitcast(I32), a.bitcast(I32), -1.0, RSQRT_MAGIC, ALU.mult, ALU.add))
            for _ in range(4):
                link(nc.vector.scalar_tensor_tensor(out=a, in0=y, scalar=-0.5, in1=y, op0=ALU.mult, op1=ALU.mult))
                link(nc.vector.tensor_tensor(out=a, in0=a, in1=v, op=ALU.mult))
                link(nc.vector.scalar_tensor_tensor(out=y, in0=a, scalar=1.5, in1=y, op0=ALU.add, op1=ALU.mult))

        def tiles_done(p, count):
            return 16 * ((count + 1 - p) // 2)

        def ffn_over(eng, n):
            eng.wait_ge(f_sem["y"], NT * (n + 1))
            for i in range(2):
                eng.wait_ge(f_st[i], tiles_done(i, NT * (n + 1)))

        def layer_over(eng, L):
            s = L.s
            for name, count in (("x1", 2 * B), ("y", 2 * B), ("exp", 16 * B), ("PV", 4 * B), ("oT", 2 * B),
                                ("onT", 2 * B), ("stack", 64 * B), ("mrow", 64 * B), ("v", B), ("split", 4 * B),
                                ("pT", 16 * B)):
                eng.wait_ge(s[name], count)

        tokT_bank = [[psM, psM], [psM, psN]]
        logit_bank = [psM, psO[0]]
        count_bank = [psM, psO[1]]

        def dve_ln_at(dve, h, lo, done, times):
            if h < 8:
                for k in (lo + 2 * h, lo + 2 * h + 1):
                    ins = nc.vector.bn_stats(bn6[:, k, :], x[:, k, :])
                if h == 7:
                    link(ins)
            elif h < 10:
                for k in range(lo + 8 * (h - 8), lo + 8 * (h - 7)):
                    ins = nc.vector.bn_aggr(mean_rstd[:, k, :], bn6[:, k, :])
                link(ins)
            elif h == 10:
                dve_ln_root(lo, lo + GBLK, done)
                dve.wait_ge(done, times)

        def dve_tokens(dve, n, lo, hi):
            for k in range(lo, hi):
                nc.vector.tensor_scalar(xn[:, k, :], x[:, k, :], mean_rstd[:, k, 0:1], mean_rstd[:, k, 1:2],
                                        ALU.subtract, ALU.mult).then_inc(r_sem["xn"], 1)

        def pe_tokens(pe, n, i):
            g, r = n % G, r_sem
            pe.wait_ge(r["xn"], GBLK * n + 4 * i + 4)
            if i > 0:
                pe.wait_ge(r["T"], 4 * n + i - g)
            for m in range(4):
                last = nc.tensor.transpose(tokT_bank[g][i % 2][:, m * P:(m + 1) * P],
                                           xn[:, g * GBLK + 4 * i + m, :], ident[:])
            last.then_inc(r["T_ps"], 1)

        def pe_logits(pe, n, i):
            g, r = n % G, r_sem
            pe.wait_ge(r["T"], 4 * n + (4 if g == 0 else i + 1))
            for m in range(4):
                k = 4 * i + m
                last = nc.tensor.matmul(logit_bank[g][:, E * k:E * k + E], xnT[i][:, m * P:(m + 1) * P], wr[:],
                                        start=True, stop=True, skip_group_check=True)
            last.then_inc(r["lg_ps"], 1)

        def pe_counts(pe, n):
            g, r = n % G, r_sem
            pe.wait_ge(r["pickb"], n + 1)
            rhs = pickb[:].rearrange("p k e -> p (k e)")
            ps = count_bank[g]
            nc.tensor.matmul(ps[:, 0:P], triu[:], rhs, start=True, stop=True, skip_group_check=True)
            nc.tensor.matmul(ps[:, P:2 * P], onesb[:], rhs, start=True, stop=True,
                             skip_group_check=True).then_inc(r["cnt_ps"], 1)

        def pe_route(pe, n):
            for i in range(5):
                if i < 4:
                    pe_tokens(pe, n, i)
                if i > 0:
                    pe_logits(pe, n, i - 1)
            pe_counts(pe, n)

        def act_tokens(act, n, i):
            r = r_sem
            act.wait_ge(r["T_ps"], 4 * n + i + 1)
            after(act, r["lg_ps"], 4 * (n - 1) + i + 1)
            nc.scalar.activation(xnT[i][:], tokT_bank[n % G][i % 2][:], ACT.Copy).then_inc(r["T"], 1)

        def act_weights(act, n):
            r = r_sem
            act.wait_ge(r["d12"], n + 1)
            nc.scalar.activation(e1[:], v12[:, 2, :], ACT.Exp).then_inc(r["e12"], 1)

        def act_route(act, n):
            for i in range(4):
                act_tokens(act, n, i)
            act_weights(act, n)

        def dve_route(dve, n):
            for part_ in range(4):
                dve_route_part(dve, n, part_)

        def dve_route_part(dve, n, stage):
            g = n % G
            r = r_sem
            w = wgt[g]
            shape = [P, GBLK, E]
            desc = cst[:, CST_DESC:CST_DESC + E].unsqueeze(1).to_broadcast(shape)

            def wide(a):
                return a.unsqueeze(2).to_broadcast(shape)

            if stage == 0:
                dve.wait_ge(r["lg_ps"], 4 * (n + 1))
                nc.vector.tensor_copy(lg[:].rearrange("p k e -> p (k e)"), logit_bank[g][:, 0:P]).then_inc(r["lg"], 1)
                dve.wait_ge(r["lg"], n + 1)
            if stage < 2:
                i = stage
                link(nc.vector.tensor_reduce(v12[:, i, :], lg[:], AX_X, ALU.max))
                link(nc.vector.tensor_tensor(out=ea[:], in0=lg[:], in1=wide(v12[:, i, :]), op=ALU.is_equal))
                link(nc.vector.tensor_tensor(out=ea[:], in0=ea[:], in1=desc, op=ALU.mult))
                link(nc.vector.tensor_reduce(slotf[:, 0, :], ea[:], AX_X, ALU.max))
                link(nc.vector.tensor_tensor(out=pick[i][:], in0=desc, in1=wide(slotf[:, 0, :]), op=ALU.is_equal))
            if stage == 0:
                link(nc.vector.scalar_tensor_tensor(out=lg[:], in0=pick[0][:], scalar=-1e38, in1=lg[:],
                                                    op0=ALU.mult, op1=ALU.add))
            if stage == 1:
                nc.vector.tensor_tensor(out=v12[:, 2, :], in0=v12[:, 1, :], in1=v12[:, 0, :],
                                        op=ALU.subtract).then_inc(r["d12"], 1)
                nc.vector.tensor_tensor(out=pickb[:], in0=pick[0][:], in1=pick[1][:],
                                        op=ALU.add).then_inc(r["pickb"], 1)
            if stage == 2:
                dve.wait_ge(r["e12"], n + 1)
                link(nc.vector.tensor_scalar(slotf[:, 0, :], e1[:], 1.0, None, ALU.add))
                link(nc.vector.reciprocal(slotf[:, 1, :], slotf[:, 0, :]))
                link(nc.vector.tensor_scalar(w[:, 0, :], slotf[:, 1, :], DEPTH_SCALE, None, ALU.mult))
                link(nc.vector.tensor_tensor(out=w[:, 1, :], in0=w[:, 0, :], in1=e1[:], op=ALU.mult))
            if stage < 3:
                return
            dve.wait_ge(r["cnt_ps"], n + 1)
            cnt = count_bank[g][:, P:2 * P].rearrange("p (k e) -> p k e", e=E)
            pre = count_bank[g][:, 0:P].rearrange("p (k e) -> p k e", e=E)
            link(nc.vector.tensor_copy(ea[:], cnt))
            a, b = ea, eb
            for sh in (1, 2, 4, 8):
                nc.vector.tensor_copy(b[:, 0:sh, :], a[:, 0:sh, :])
                link(nc.vector.tensor_tensor(out=b[:, sh:, :], in0=a[:, sh:, :], in1=a[:, :GBLK - sh, :], op=ALU.add))
                a, b = b, a
            link(nc.vector.tensor_scalar(pc[:, 0, :], a[:, GBLK - 1, :], float(P - 1), None, ALU.add))
            link(nc.vector.tensor_copy(pci[:, 0, :], pc[:, 0, :]))
            link(nc.vector.tensor_scalar(pci[:, 1, :], pci[:, 0, :], 7, None, ALU.logical_shift_right))
            link(nc.vector.tensor_scalar(pci[:, 0, :], pci[:, 1, :], 7, None, ALU.logical_shift_left))
            link(nc.vector.tensor_copy(pc[:, 0, :], pci[:, 0, :]))
            c, d = 0, 1
            for sh in (1, 2, 4):
                nc.vector.tensor_copy(pc[:, d, 0:sh], pc[:, c, 0:sh])
                link(nc.vector.tensor_tensor(out=pc[:, d, sh:], in0=pc[:, c, sh:], in1=pc[:, c, :E - sh], op=ALU.add))
                c, d = d, (2 if d == 1 else 1)
            end = pc[:, c, :]
            link(nc.vector.tensor_tensor(out=pc[:, 3, :], in0=end, in1=pc[:, 0, :], op=ALU.subtract))
            link(nc.vector.tensor_tensor(out=b[:], in0=a[:], in1=cnt, op=ALU.subtract))
            link(nc.vector.tensor_tensor(out=a[:], in0=b[:], in1=pre, op=ALU.add))
            link(nc.vector.tensor_tensor(out=b[:], in0=a[:], in1=pc[:, 3, :].unsqueeze(1).to_broadcast(shape),
                                         op=ALU.add))
            for i in range(2):
                link(nc.vector.tensor_tensor(out=a[:], in0=b[:], in1=pick[i][:], op=ALU.mult))
                link(nc.vector.tensor_reduce(slotf[:, i, :], a[:], AX_X, ALU.add))
            tile0 = cst[0:1, CST_TILE:CST_TILE + NT]
            link(nc.vector.tensor_tensor(out=cmpt[:], in0=pc[0:1, c, :].unsqueeze(1).to_broadcast([1, NT, E]),
                                         in1=tile0.unsqueeze(2).to_broadcast([1, NT, E]), op=ALU.is_le))
            link(nc.vector.tensor_reduce(tef[:], cmpt[:], AX_X, ALU.add))
            link(nc.vector.tensor_scalar(tef[:], tef[:], float(E - 1), float(HID), ALU.min, ALU.mult))
            nc.vector.tensor_copy(te[g][:], tef[:]).then_inc(r["slots"], 1)
            nc.vector.tensor_copy(slot[g][:], slotf[:]).then_inc(r["slots"], 1)

        def pool_scatter(pool, n, blocks):
            g = n % G
            if blocks[0] == 0:
                pool.wait_ge(r_sem["slots"], 2 * (n + 1))
            for k in blocks:
                for i in range(2):
                    nc.gpsimd.indirect_dma_start(
                        xg[g], bass.IndirectOffsetOnAxis(ap=slot[g][:, i, k:k + 1], axis=0),
                        xn[:, g * GBLK + k, :], None).then_inc(r_scat[g], 16)

        def pool_gather(pool, n, quarters):
            g = n % G
            if quarters[0] == 0:
                for i in range(2):
                    pool.wait_ge(f_st[i], tiles_done(i, NT * (n + 1)))
                if g == 1:
                    pool.wait_ge(r_scat[0], 16 * 2 * GBLK * (n // G + 1))
                    pool.wait_ge(r_scat[1], 16 * 2 * GBLK * (n // G + 1))
            for k in range(4 * quarters[0], 4 * quarters[-1] + 4):
                for i in range(2):
                    nc.gpsimd.indirect_dma_start(
                        gb[g][:, 2 * k + i, :], None, eo[g],
                        bass.IndirectOffsetOnAxis(ap=slot[g][:, i, k:k + 1], axis=0)).then_inc(r_gat[g][k // 4], 16)

        def dve_add_expert(n, k, i):
            blk = x[:, bass.ds(k, 1), :]
            w = wgt[0][:, i, bass.ds(k, 1)]
            nc.vector.scalar_tensor_tensor(out=blk, in0=gb[0][:, bass.ds(2 * k + i, 1), :], scalar=w,
                                           in1=blk, op0=ALU.mult, op1=ALU.add).then_inc(r_sem["x"], 1)

        def dve_combine_0(dve, n, k):
            dve_add_expert(n, k, 0)
            dve.wait_ge(r_sem["x"], 2 * GBLK * (n - 1) + 2 * k + 1)
            dve_add_expert(n, k, 1)

        def dve_combine_1(dve, n, q):
            dve.wait_ge(r_gat[1][q], 16 * 8 * (n // G + 1))
            for i in range(2):
                for k in range(4 * q, 4 * q + 4):
                    blk = x[:, GBLK + k, :]
                    nc.vector.scalar_tensor_tensor(out=blk, in0=gb[1][:, 2 * k + i, :], scalar=wgt[1][:, i, k:k + 1],
                                                   in1=blk, op0=ALU.mult, op1=ALU.add).then_inc(r_sem["x"], 1)
                dve.wait_ge(r_sem["x"], 2 * GBLK * n + 8 * q + 4 * (i + 1))

        def tile_loop(step, eng, n, between=None, last=None):
            def parity(k):
                return (n * NT + k) % 2

            first = NT - 2 - GBLK
            for k in range(5):
                step(eng, n, k, parity(k))
            if between is None:
                with eng.Fori(5, NT - 5, 4) as k:
                    for d in range(4):
                        step(eng, n, k + d, parity(5 + d))
            else:
                with eng.Fori(5, first - 3, 4) as k:
                    for d in range(4):
                        step(eng, n, k + d, parity(5 + d))
                for q in range(4):
                    eng.wait_ge(r_gat[0][q], 16 * 8 * (n // G + 1))
                with eng.Fori(first, NT - 5, 4) as k:
                    for d in range(4):
                        step(eng, n, k + d, parity(5 + d))
                        between(eng, n, k + d - first)
            for k in range(NT - 2, NT + 2):
                step(eng, n, k, parity(k))
                if last is not None:
                    last(eng, n, k - NT + 2)

        def live(k, d):
            return not isinstance(k, int) or 0 <= k + d < NT

        def pe_tile(pe, n, k, p):
            f, n0, g = f_sem, n * NT, n % G

            def tokens(t, p):
                after(pe, f_ld[p], 8 * (n0 + t - p) + 16)
                after(pe, f["xT"], n0 + t)
                nc.tensor.transpose(psM[:, 0:P], xin[p][:], ident[:]).then_inc(f["T_ps"], 1)

            if isinstance(k, int) and k == 0:
                tokens(0, n0 % 2)
            if live(k, 0):
                e = pe.value_load(te[g][0:1, bass.ds(k, 1)], min_val=0, max_val=(E - 1) * HID)
                after(pe, f["xT"], n0 + k + 1)
                after(pe, f["silu"], n0 + k - 1)
                after(pe, f["h"], n0 + k - 1)
                nc.tensor.matmul(psS[p][:], xTt[p][:], wg[:, bass.ds(e, HID)], start=True, stop=True)
                nc.tensor.matmul(psT[p][:], xTt[p][:], wu[:, bass.ds(e, HID)],
                                 start=True, stop=True).then_inc(f["gu"], 1)
            if live(k, 1):
                tokens(k + 1, 1 - p)
            if live(k, -1):
                after(pe, f["h"], n0 + k)
                for half_, done in ((0, "hTa"), (1, "hTb")):
                    after(pe, f[done], n0 + k - 1)
                    for m in range(2):
                        hb = 2 * half_ + m
                        last = nc.tensor.transpose(psO[half_][:, m * P:(m + 1) * P],
                                                   hh[1 - p][:, hb * P:(hb + 1) * P], ident[:])
                    last.then_inc(f["hT_ps"], 1)
            if live(k, -2):
                e = pe.value_load(te[g][0:1, bass.ds(k - 2, 1)], min_val=0, max_val=(E - 1) * HID)
                after(pe, f["hTa"], n0 + k - 1)
                after(pe, f["hTb"], n0 + k - 1)
                after(pe, f["y"], n0 + k - 2)
                for hb in range(HB):
                    last = nc.tensor.matmul(psN[:, 0:P], hT[p][:, hb, :], wd[:, bass.ds(e + hb * P, P)],
                                            start=(hb == 0), stop=(hb == HB - 1))
                last.then_inc(f["y_ps"], 1)

        def act_tile(act, n, k, p):
            f, n0 = f_sem, n * NT

            def tokens(t, p):
                after(act, f["T_ps"], n0 + t + 1)
                after(act, f["gu"], n0 + t - 1)
                nc.scalar.activation(xTt[p][:], psM[:, 0:P], ACT.Copy).then_inc(f["xT"], 1)

            if isinstance(k, int) and k == 0:
                tokens(0, n0 % 2)
            if live(k, 1):
                tokens(k + 1, 1 - p)
            if live(k, 0):
                after(act, f["gu"], n0 + k + 1)
                after(act, f["h"], n0 + k - 1)
                nc.scalar.activation(sg[p][:], psS[p][:], ACT.Silu).then_inc(f["silu"], 1)
            if live(k, -1):
                after(act, f["hT_ps"], 2 * (n0 + k) - 1)
                after(act, f["y_ps"], n0 + k - 2)
                nc.scalar.activation(hT[1 - p][:, 0:2, :], psO[0][:, 0:2 * P].rearrange("p (a c) -> p a c", a=2),
                                     ACT.Copy).then_inc(f["hTa"], 1)

        def dve_tile(dve, n, k, p):
            f, n0 = f_sem, n * NT
            if live(k, -1):
                after(dve, f["hT_ps"], 2 * (n0 + k))
                after(dve, f["y_ps"], n0 + k - 2)
                nc.vector.tensor_copy(hT[1 - p][:, 2:4, :],
                                      psO[1][:, 0:2 * P].rearrange("p (a c) -> p a c", a=2)).then_inc(f["hTb"], 1)
            if live(k, 0):
                after(dve, f["silu"], n0 + k + 1)
                after(dve, f["hT_ps"], 2 * (n0 + k - 1))
                nc.vector.tensor_tensor(out=hh[p][:], in0=sg[p][:], in1=psT[p][:], op=ALU.mult).then_inc(f["h"], 1)
            if live(k, -2):
                after(dve, f["y_ps"], n0 + k - 1)
                after(dve, f_st[p], 8 * (n0 + k - 2 - p))
                nc.vector.tensor_copy(ysb[p][:], psN[:, 0:P]).then_inc(f["y"], 1)

        def sp_tile(sp, n, k, p):
            f, n0, g = f_sem, n * NT, n % G

            def load(t, p, row0):
                sp.dma_start(xin[p][:], xg[g][bass.ds(row0, P), :]).then_inc(f_ld[p], 16)

            if isinstance(k, int) and k == 0:
                for t in range(2):
                    after(sp, f["T_ps"], n0)
                    load(t, (n0 + t) % 2, t * P)
            if live(k, 2):
                used, row0 = fixed(sp, n0 + k + 1), fixed(sp, (k + 2) * P)
                after(sp, f["T_ps"], used)
                load(k + 2, p, row0)
            if live(k, -2):
                ready, row0 = fixed(sp, n0 + k - 1), fixed(sp, (k - 2) * P)
                after(sp, f["y"], ready)
                sp.dma_start(eo[g][bass.ds(row0, P), :], ysb[p][:]).then_inc(f_st[p], 16)

        block = ctx.enter_context(nc.Block())

        def load_layer(sp, L, weights, biases):
            for i, (w, b) in enumerate(zip(weights, biases)):
                done = L.s["w"] if i < 2 else L.s["w_vo"]
                sp.dma_start(L.w_in[:, i, :], w).then_inc(done, 16)
                sp.dma_start(L.b_in[0:1, i, :], b.rearrange("(a n) -> a n", a=1)).then_inc(done, 16)

        def sp_ffn(sp, l):
            for g in range(G):
                n = 2 * l + g
                sp.wait_ge(r_scat[g], 16 * 2 * GBLK * (l + 1))
                if l > 0:
                    for q in range(4):
                        sp.wait_ge(r_gat[g][q], 16 * 8 * l)
                tile_loop(sp_tile, sp, n)

        def pool_beside(l):
            def hook(pool, j, h):
                if l == 1 and j < 4 and h == 0:
                    pool_gather(pool, 1, range(j, j + 1))
                if j == 18 and l == 1 and h == 0:
                    pool_scatter(pool, 2, range(5))
            return hook

        def sp_beside(sp, j, point):
            experts = slice(2 * point, 2 * point + 2)
            if j in (3, 4):
                w, name = ((wg, "L0_ffn_Wg"), (wu, "L0_ffn_Wu"))[j - 3]
                sp.dma_start(w[:].rearrange("p (e h) -> p e h", e=E)[:, experts, :],
                             A[name].rearrange("e c h -> c e h")[:, experts, :]).then_inc(s_wffn, 16)
            if j == 5:
                for e in (2 * point, 2 * point + 1):
                    sp.dma_start(wd[:, e * HID:(e + 1) * HID].rearrange("p (k d) -> p k d", k=HB),
                                 A["L0_ffn_Wd"][e].rearrange("(k p) d -> p k d", p=P)).then_inc(s_wffn, 16)
            if j == 6:
                done = LB.s["w"] if point < 2 else LB.s["w_vo"]
                lo, hi = point * D, (point + 1) * D
                w = A["L0_attn_b_W_proj"] if point == 3 else A["L0_attn_b_W_qkv"][:, lo:hi]
                b = A["L0_attn_b_b_proj"] if point == 3 else A["L0_attn_b_b_qkv"][lo:hi]
                sp.dma_start(LB.w_in[:, point, :], w).then_inc(done, 16)
                sp.dma_start(LB.b_in[0:1, point, :], b.rearrange("(a n) -> a n", a=1)).then_inc(done, 16)
                if point == 0:
                    sp.dma_start(wr[:], A["L0_ffn_Wr"]).then_inc(s_wffn, 16)
            if j in (16, 17):
                sp.wait_ge(s_zero, 1)
                t0, t1 = (NT * point // 4, NT * (point + 1) // 4)
                sp.dma_start(xg[j - 16].rearrange("(t p) d -> p t d", p=P)[:, t0:t1, :],
                             zero[:].unsqueeze(1).to_broadcast([P, t1 - t0, D])).then_inc(s_zfill, 16)

        def pe_beside(l):
            L, n = (LA, LB)[l], 2 * l

            def hook(pe, j, h):
                if j == 1 and h == 15:
                    pe.wait_ge(L.s["w_vo"], 64)
                if j == 17 and 2 <= h < 6:
                    if h == 2:
                        pe.wait_ge(s_wffn, 16 * 17)
                        pe.wait_ge(s_half, 4)
                        pe.wait_ge(L.s["v"], B - 1)
                        if l == 1:
                            pe.wait_ge(L.s["bc"], 2 * B)
                    pe_tokens(pe, n, h - 2)
                if j == 17 and h == 7:
                    for i in range(4):
                        pe_logits(pe, n, i)
                if j == 17 and h == 8:
                    pe.wait_ge(r_sem["lg"], n + 1)
                if j == 17 and h == 15:
                    pe.wait_ge(L.s["v"], B)
                    pe_counts(pe, n)
                if l == 0 and j == 19 and h == 10:
                    pe.wait_ge(r_sem["slots"], 2)
                    pe_setup(pe, LB)
            return hook

        def act_beside(l):
            def hook(act, j, h):
                if j == 17 and 3 <= h < 7:
                    act_tokens(act, 2 * l, h - 3)
                if j == 17 and h == 11:
                    act_weights(act, 2 * l)
                if l == 0 and j == 19 and h == 14:
                    act_setup(act, LB)
            return hook

        def dve_beside(l):
            n = 2 * l

            def hook(dve, j, h):
                if l == 0 and 1 <= j < 5 and h == 15:
                    if j == 1:
                        dve.wait_ge(s_xrest, 16)
                    dve_ln_stats(dve, (4, 6, 12, 22)[j - 1], (6, 12, 22, NBLK)[j - 1], s_lnA)
                    dve.wait_ge(s_lnA, j + 1)
                if l == 0 and j == 1 and h == 15:
                    dve.wait_ge(s_mset, 2 * RING)
                    nc.vector.memset(half[0:1, 0, :], -0.5).then_inc(s_half, 1)
                    nc.vector.memset(half[0:1, 1, :], 1.5).then_inc(s_half, 1)
                    dve.wait_ge(s_cst, 16)
                    nc.vector.memset(onesb[:], 1.0).then_inc(s_half, 1)
                    nc.vector.tensor_copy(triu[:], cst[:, CST_TRIU:CST_TRIU + P]).then_inc(s_half, 1)
                if l == 1 and 2 <= j < 6 and h == 7:
                    dve_combine_1(dve, 1, j - 2)
                if l == 1 and j == 6:
                    dve_ln_at(dve, h, GBLK, s_lnB, 2)
                if j == 16:
                    if h == 0:
                        dve.wait_ge((LA, LB)[l].s["x1"], GBLK)
                    dve_ln_at(dve, h, 0, s_ln[n], 1)
                    if 11 <= h < 15:
                        dve_tokens(dve, n, 4 * (h - 11), 4 * (h - 10))
                if j == 17 and h in (8, 9):
                    dve_route_part(dve, n, h - 8)
                if j == 17 and h == 12:
                    dve_route_part(dve, n, 2)
                if j == 18 and h == 0:
                    dve_route_part(dve, n, 3)
                if l == 0 and j == 18 and h == 15:
                    dve_setup(dve, LB)
                if j == 19 and h == 2:
                    dve.wait_ge((LA, LB)[l].s["x1"], NBLK - 2)
                    dve_ln_stats(dve, GBLK, NBLK - 2, s_ln[n + 1])
                    dve.wait_ge(s_ln[n + 1], 1)
                if j == 19 and h == 8:
                    dve_tokens(dve, n + 1, GBLK, NBLK - 2)
            return hook

        LA.sp_hook = sp_beside
        for l, L in enumerate((LA, LB)):
            L.pe_hook, L.act_hook, L.dve_hook, L.pool_hook = pe_beside(l), act_beside(l), dve_beside(l), pool_beside(l)

        def dve_ln_tail(dve, n, i):
            if i == 0:
                dve.wait_ge(r_sem["x"], 2 * GBLK * n)
            if i < 3:
                for h in ((0, 1, 2, 3, 4), (5, 6, 7, 8), (9, 10))[i]:
                    dve_ln_at(dve, h, 0, s_lnB, 1)

        @block.sync
        def _(sp):
            sp.dma_start(x[:, 0:4, :], x_dram[:, 0:4, :]).then_inc(s_xin, 16)
            load_layer(sp, LA, [A["L0_attn_a_w" + c] for c in "qkvo"], [A["L0_attn_a_b" + c] for c in "qkvo"])
            sp.dma_start(x[:, 4:, :], x_dram[:, 4:, :]).then_inc(s_xrest, 16)
            sp.dma_start(cst[:], A["const"]).then_inc(s_cst, 16)
            pipeline(sp_step, sp, LA)
            sp_ffn(sp, 0)
            pipeline(sp_step, sp, LB)
            sp_ffn(sp, 1)
            sp.wait_ge(r_sem["x"], 2 * GBLK * 3)
            sp.dma_start(out_dram[:, 0:GBLK, :], x[:, 0:GBLK, :]).then_inc(s_out, 16)
            for q in range(4):
                lo = GBLK + 4 * q
                sp.wait_ge(r_sem["x"], 2 * GBLK * 3 + 8 * (q + 1))
                sp.dma_start(out_dram[:, lo:lo + 4, :], x[:, lo:lo + 4, :]).then_inc(s_out, 16)
            sp.wait_ge(s_out, 16 * 5)

        @block.gpsimd
        def _(pool):
            nc.gpsimd.memset(ident[:], 0.0).then_inc(s_const, 1)
            nc.gpsimd.memset(trib[:], 0.0).then_inc(s_const, 1)
            nc.gpsimd.memset(tick[:], 0.0).then_inc(s_const, 1)
            pool.wait_ge(s_const, 3)
            nc.gpsimd.affine_select(out=ident[:], in_=ident[:], compare_op=ALU.not_equal, fill=1.0, base=0,
                                    pattern=[[-1, P]], channel_multiplier=1).then_inc(s_const, 1)
            nc.gpsimd.affine_select(out=trib[:], in_=trib[:], compare_op=ALU.is_ge, fill=NEG, base=0,
                                    pattern=[[-1, P]], channel_multiplier=1).then_inc(s_const, 1)
            for r in range(RING):
                if r == 0:
                    nc.gpsimd.memset(zero[:], 0.0).then_inc(s_zero, 1)
                ins = nc.gpsimd.memset(kst[r][:], -1.0)
            for r in range(RING):
                nc.gpsimd.memset(vp[r][:], 0.0).then_inc(s_mset, 1)
            pool.wait_ge(s_mset, RING)
            for r in range(RING):
                nc.gpsimd.memset(vp[r][:, :, :, HD:HD + 1], 1.0).then_inc(s_mset, 1)
            pipeline(pool_step, pool, LA)
            pool.wait_ge(s_zfill, 16 * 8)
            pool_scatter(pool, 0, range(GBLK))
            pool_scatter(pool, 1, range(GBLK))
            pool_gather(pool, 0, range(4))
            pool.wait_ge(s_half, 2)
            pipeline(pool_step, pool, LB)
            pool_scatter(pool, 2, range(5, GBLK))
            pool_scatter(pool, 3, range(GBLK))
            pool_gather(pool, 2, range(4))
            pool_gather(pool, 3, range(4))

        @block.scalar
        def _(act):
            act_setup(act, LA)
            pipeline(act_step, act, LA)
            for l in range(2):
                layer_over(act, (LA, LB)[l])
                act_route(act, 2 * l + 1)
                tile_loop(act_tile, act, 2 * l)
                tile_loop(act_tile, act, 2 * l + 1)
                if l == 0:
                    ffn_over(act, 1)
                    act.wait_ge(r_sem["x"], 2 * GBLK)
                    pipeline(act_step, act, LB)

        @block.vector
        def _(dve):
            nc.vector.memset(ones_row[:], 1.0).then_inc(s_const_dve, 1)
            dve.wait_ge(s_xin, 16)
            dve_ln_stats(dve, 0, 4, s_lnA)
            dve.wait_ge(s_lnA, 1)
            dve.wait_ge(s_const, 5)
            nc.vector.tensor_copy(identb[:], ident[:]).then_inc(s_const_dve, 1)
            dve_setup(dve, LA)
            pipeline(dve_step, dve, LA)
            for l in range(2):
                layer_over(dve, (LA, LB)[l])
                n = 2 * l + 1
                dve_ln_stats(dve, NBLK - 2, NBLK, s_ln[n])
                dve.wait_ge(s_ln[n], 2)
                dve_tokens(dve, n, NBLK - 2, NBLK)
                dve_route(dve, n)
                tile_loop(dve_tile, dve, 2 * l)
                tile_loop(dve_tile, dve, n, dve_combine_0, dve_ln_tail if l == 0 else None)
                if l == 0:
                    pipeline(dve_step, dve, LB)
            for q in range(4):
                dve_combine_1(dve, 3, q)

        @block.tensor
        def _(pe):
            pe.wait_ge(s_const, 5)
            pe_setup(pe, LA)
            pipeline(pe_step, pe, LA)
            for l in range(2):
                layer_over(pe, (LA, LB)[l])
                pe.wait_ge(r_sem["slots"], 4 * l + 2)
                pe.wait_ge(LB.s["bcol"], 1)
                pe_route(pe, 2 * l + 1)
                tile_loop(pe_tile, pe, 2 * l)
                pe.wait_ge(r_sem["slots"], 4 * l + 4)
                tile_loop(pe_tile, pe, 2 * l + 1)
                if l == 0:
                    ffn_over(pe, 1)
                    pipeline(pe_step, pe, LB)


def constants():
    import numpy as np
    c = np.zeros((P, CST_COLS), np.float32)
    c[:, CST_DESC:CST_DESC + E] = E - np.arange(E)
    c[:, CST_TILE:CST_TILE + NT] = P * np.arange(NT)
    p = np.arange(P)
    c[:, CST_HEAD:CST_HEAD + P] = p[:, None] // HD == p[None, :] // HD
    c[:, CST_TRIU:CST_TRIU + P] = p[:, None] < p[None, :]
    return c


_INS = ['L0_attn_a_x', 'L0_attn_a_wq', 'L0_attn_a_bq', 'L0_attn_a_wk', 'L0_attn_a_bk', 'L0_attn_a_wv',
        'L0_attn_a_bv', 'L0_attn_a_wo', 'L0_attn_a_bo', 'L0_attn_b_W_qkv', 'L0_attn_b_b_qkv',
        'L0_attn_b_W_proj', 'L0_attn_b_b_proj', 'L0_ffn_Wr', 'L0_ffn_Wg', 'L0_ffn_Wu', 'L0_ffn_Wd']
_OUTS = [((16, 256, 128), 'float32')]


def kernel(**inputs):
    import numpy as _np
    import concourse.bacc as _bacc
    from concourse import mybir as _mybir
    from concourse.bass_utils import run_bass_kernel_spmd as _run

    nc = _bacc.Bacc("TRN2", target_bir_lowering=False, num_devices=1)
    arrays, args = {}, {}
    for name in _INS:
        a = _np.ascontiguousarray(inputs[name])
        arrays[f"in_{name}"] = a
        args[name] = nc.dram_tensor(f"in_{name}", a.shape, _mybir.dt.from_np(a.dtype), kind="ExternalInput").ap()
    arrays["in_const"] = constants()
    args["const"] = nc.dram_tensor("in_const", (P, CST_COLS), F32, kind="ExternalInput").ap()
    shape, dtype = _OUTS[0]
    out = nc.dram_tensor("out_0", shape, _mybir.dt.from_np(_np.dtype(dtype)), kind="ExternalOutput").ap()
    build(nc, args, out)
    r = _run(nc, [arrays], core_ids=[0])
    return r.results[0]["out_0"]
```

```python
from contextlib import ExitStack

import concourse.bass as bass
from concourse import mybir

F32 = mybir.dt.float32
BF16 = mybir.dt.bfloat16
I32 = mybir.dt.int32
ALU = mybir.AluOpType
ACT = mybir.ActivationFunctionType
AX_X = mybir.AxisListType.X

P = 128
B, T, D = 16, 256, 128
H, HD = 16, 8
NBLK = B * T // P
TERMS = 6
ROWS = TERMS * HD
E, HID = 8, 512
HB = HID // P
G = 2
GBLK = NBLK // G
NT = 2 * GBLK + E - 1
CST_DESC, CST_TILE, CST_HEAD, CST_TRIU = 0, E, E + NT, E + NT + P
CST_COLS = CST_TRIU + P
TILES = G * NT
EPS = 1e-5
NEG = -3.0e38
DEPTH_SCALE = float(12.0 ** -0.5)
PCH = 23
POS = [8 * (h // 8) + 4 * (h % 2) + (h % 8) // 2 for h in range(H)]
RING = 3
RSQRT_MAGIC = float(0x5F3759DF)


def after(eng, sem, value):
    if isinstance(value, int) and value <= 0:
        return
    eng.wait_ge(sem, value)


def fixed(eng, value):
    if not isinstance(value, int):
        eng.compute_val(value)
    return value


class Layer:
    pass


def build(nc, A, out):
    with ExitStack() as ctx:
        def sb(name, shape, dt=F32):
            return ctx.enter_context(nc.sbuf_tensor(name, shape, dt))

        def psum(name):
            return ctx.enter_context(nc.psum_tensor(name, [P, 512], F32))

        def sem(name):
            return ctx.enter_context(nc.semaphore(name))

        def dram(name, shape, dt=F32):
            return nc.dram_tensor(name, shape, dt, kind="Internal").ap()

        psS = [psum("psS0"), psum("psS1")]
        psT = [psum("psT0"), psum("psT1")]
        psO = [psum("psO0"), psum("psO1")]
        psM = psum("psM")
        psN = psum("psN")

        x = sb("x", [P, NBLK, D])
        cst = sb("cst", [P, CST_COLS])
        mean_rstd = sb("mean_rstd", [P, NBLK, 2])
        bn6 = sb("bn6", [P, NBLK, 6])
        nwt = sb("nwt", [P, 3, NBLK])
        ident = sb("ident", [P, P])
        identb = sb("identb", [P, P], BF16)
        trib = sb("trib", [P, P], BF16)
        tick = sb("tick", [1, 2])
        ones_row = sb("ones_row", [1, T])
        xs = sb("xs", [P, 2, D])
        xT = [sb(f"xT{r}", [P, T]) for r in range(RING)]
        qk = sb("qk", [P, 2, T])
        rest = sb("rest", [P, 2, T])
        part = sb("part", [P, 2, 3, T], BF16)
        qst = [sb(f"qst{r}", [P, 8, T], BF16) for r in range(RING)]
        kst = [sb(f"kst{r}", [P, 8, T], BF16) for r in range(RING)]
        vp = [sb(f"vp{r}", [P, 2, H, 32]) for r in range(RING)]
        mx3 = sb("mx3", [P, 2, 3, 8])
        mxu = sb("mxu", [P, 2, 2, 8])
        mrow = sb("mrow", [8, 2, T], BF16)
        pT = sb("pT", [P, 8, 512])
        oT = sb("oT", [P, 4, T])
        rden = sb("rden", [P, H])
        on = sb("on", [P, D])
        onT = sb("onT", [P, D])

        head_ones = cst[:, CST_HEAD:CST_HEAD + P]
        absq = sb("absq", [P, T])
        junk = sb("junk", [P, 3, T])
        st = sb("st", [P, 4])
        row = sb("row", [1, 56])
        prow = sb("prow", [1, 8, H])
        half = sb("half", [1, 2, H])
        scb = [sb(f"scb{r}", [P, 2, H]) for r in range(RING)]
        neg_shift = [sb(f"neg_shift{r}", [8, 2]) for r in range(RING)]

        wg = sb("wg", [P, E * HID])
        wu = sb("wu", [P, E * HID])
        wd = sb("wd", [P, E * HID])
        wr = sb("wr", [P, E])
        xn = sb("xn", [P, NBLK, D])
        gb = [pT[:].rearrange("p a (b c) -> p (a b) c", c=D), xn[:]]
        triu = sb("triu", [P, P], BF16)
        onesb = sb("onesb", [P, P], BF16)
        zero = sb("zero", [P, D])
        xnT = [sb(f"xnT{i}", [P, 4 * P]) for i in range(4)]
        lg = sb("lg", [P, GBLK, E])
        ea = sb("ea", [P, GBLK, E])
        eb = sb("eb", [P, GBLK, E])
        pick = [sb(f"pick{i}", [P, GBLK, E]) for i in range(2)]
        pickb = sb("pickb", [P, GBLK, E], BF16)
        counts = sb("counts", [P, 2 * P])
        v12 = sb("v12", [P, 3, GBLK])
        e1 = sb("e1", [P, GBLK])
        slotf = sb("slotf", [P, 2, GBLK])
        slot = [sb(f"slot{g}", [P, 2, GBLK], I32) for g in range(G)]
        wgt = [sb(f"wgt{g}", [P, 2, GBLK]) for g in range(G)]
        pc = sb("pc", [P, 4, E])
        pci = sb("pci", [P, 2, E], I32)
        cmpt = sb("cmpt", [1, NT, E])
        tef = sb("tef", [1, NT])
        te = sb("te", [1, TILES], I32)
        xin = [sb(f"xin{i}", [P, D]) for i in range(2)]
        xTt = [sb(f"xTt{i}", [P, P]) for i in range(2)]
        sg = [sb(f"sg{i}", [P, HID]) for i in range(2)]
        hh = [sb(f"hh{i}", [P, HID]) for i in range(2)]
        hT = [sb(f"hT{i}", [P, HB, P]) for i in range(2)]
        ysb = [sb(f"ysb{i}", [P, D]) for i in range(2)]

        xg = [dram(f"xg{g}", (NT * P, D)) for g in range(G)]
        eo = [dram(f"eo{g}", (NT * P, D)) for g in range(G)]
        scr_part = dram("scr_part", (2, P, TERMS, T), BF16)
        scr_m = dram("scr_m", (2, 8, 2, T), BF16)

        x_dram = A["L0_attn_a_x"].rearrange("b (k p) d -> p (b k) d", p=P)
        out_dram = out.rearrange("b (k p) d -> p (b k) d", p=P)

        s_xin = sem("s_xin")
        s_xrest = sem("s_xrest")
        s_lnA = sem("s_lnA")
        s_const = sem("s_const")
        s_const_dve = sem("s_const_dve")
        s_chain = sem("s_chain")
        s_ln = [sem("s_ln0"), sem("s_ln1"), sem("s_ln2"), sem("s_ln3")]
        s_out = sem("s_out")
        s_mset = sem("s_mset")
        s_cst = sem("s_cst")
        s_half = sem("s_half")
        s_lnB = sem("s_lnB")
        s_wffn = sem("s_wffn")
        s_zero = sem("s_zero")
        s_zfill = sem("s_zfill")
        r_sem = {n: sem("R_" + n) for n in ["xn", "T_ps", "T", "lg_ps", "lg", "d12", "e12", "pickb", "cnt_ps", "cnt",
                                            "slots", "x"]}
        r_scat = [sem(f"R_scat{g}") for g in range(G)]
        r_gat = [[sem(f"R_gat{g}{q}") for q in range(4)] for g in range(G)]
        f_sem = {n: sem("F_" + n) for n in ["T_ps", "xT", "gu", "silu", "h", "hT_ps", "hTa", "hTb", "y_ps", "y"]}
        f_ld = [sem(f"F_ld{i}") for i in range(2)]
        f_st = [sem(f"F_st{i}") for i in range(2)]
        chain = [0]

        def link(ins):
            chain[0] += 1
            ins.then_inc(s_chain, 1)
            nc.vector.wait_ge(s_chain, chain[0])

        SEMS = ["w", "w_vo", "wp", "bcol_ps", "bcol", "xs", "xT_ps", "xT", "qk_ps", "qk", "split", "scr_w", "stack",
                "S", "mx", "mxu", "mT", "m1", "m2", "mscr", "mrow", "ST", "exp", "pT", "PV", "oT", "tO_ps",
                "rden", "on", "onT_ps", "onT", "y", "x1", "v_ps", "v",
                "col", "qsum_ps", "qsum", "row_ps", "row", "pool", "bc_ps", "bc", "seed"]

        def layer(tag, causal):
            L = Layer()
            L.tag, L.causal = tag, causal
            L.s = {n: sem(f"{tag}_{n}") for n in SEMS}
            L.w_in = sb(f"w_in{tag}", [P, 4, D])
            L.w_perm = sb(f"w_perm{tag}", [P, 2, D])
            L.b_in = sb(f"b_in{tag}", [1, 4, D])
            L.b_perm = sb(f"b_perm{tag}", [1, 2, D])
            L.b_col = sb(f"b_col{tag}", [P, 2])
            L.pe_hook = L.act_hook = L.dve_hook = L.pool_hook = L.sp_hook = None
            return L

        LA = layer("A", True)
        LB = layer("B", False)
        LB.s["pT"] = LB.s["exp"]

        def kcols(L):
            return 384 if L.causal else 512

        def pe_setup(pe, L):
            s = L.s
            pe.wait_ge(s["wp"], 4)
            pe.wait_ge(s_const_dve, 2)
            for o in range(2):
                last = nc.tensor.matmul(psM[:, o:o + 1], L.b_perm[0:1, o, :], ones_row[0:1, 0:1],
                                        start=(o == 0), stop=True, skip_group_check=True)
            last.then_inc(s["bcol_ps"], 1)

        def pe_step(pe, L, j, c, P_, V_, S_, T_, O_):
            s = L.s
            bS, bT, bO = j - 2, j - 3, j - 4
            rP, rS, rT, rO = c % 3, (c - 2) % 3, (c - 3) % 3, (c - 4) % 3
            cols = kcols(L)

            def pv_quad(b, r, q):
                after(pe, s["pT"], 16 * b + 4 * q + 4)
                if q % 2 == 0:
                    after(pe, s["oT"], 2 * (b - 1) + q // 2 + 1)
                for kb in range(2):
                    for i in range(4):
                        h = 4 * q + i
                        if kb == 0:
                            dst, src = (0, T), (0, T)
                        elif L.causal:
                            dst, src = (P, T), (T, T + P)
                        else:
                            dst, src = (0, T), (T, 2 * T)
                        o0 = (q % 2) * T
                        last = nc.tensor.matmul(psO[q // 2][32 * i:32 * i + 32, o0 + dst[0]:o0 + dst[1]],
                                                vp[r][:, kb, h, :], pT[:, h % 8, src[0]:src[1]],
                                                start=(kb == 0), stop=(kb == 1), skip_group_check=True)
                last.then_inc(s["PV"], 1)

            def out_transposes(qb):
                for q in range(4):
                    last = nc.tensor.transpose(psN[:, q * P:(q + 1) * P], oT[:, q, qb * P:(qb + 1) * P], ident[:])
                last.then_inc(s["tO_ps"], 1)

            def out_transpose_on(qb):
                after(pe, s["on"], 2 * bO + qb + 1)
                nc.tensor.transpose(psN[:, 0:P], on[:], ident[:]).then_inc(s["onT_ps"], 1)

            def out_project(qb):
                after(pe, s["onT"], 2 * bO + qb + 1)
                nc.tensor.matmul(psN[:, P:2 * P], onT[:], L.w_in[:, 3, :], start=True, stop=False)
                nc.tensor.matmul(psN[:, P:2 * P], ones_row[0:1, 0:P], L.b_in[0:1, 3, :],
                                 start=False, stop=True).then_inc(s["y"], 1)

            def max_transposes(b, u):
                for qb in range(2):
                    src = mxu if L.causal else mx3
                    last = nc.tensor.transpose((psM, psN)[u][0:8, qb * P:(qb + 1) * P], src[:, u, qb, :], ident[:])
                last.then_inc(s["mT"], 1)

            for h in range(H):
                par, t = h % 2, h // 2
                r64 = slice(64 * par, 64 * par + ROWS)
                m64 = slice(64 * par, 64 * par + ROWS + 2)
                if S_:
                    if h == 0:
                        after(pe, s["stack"], 64 * (bS + 1))
                    after(pe, s["mx"], 16 * bS + h - 1)
                    ps, q_, k_ = psS[h % 2], qst[rS], kst[rS]
                    if L.causal:
                        for c0, k in ((0, 0), (P, 1)):
                            nc.tensor.matmul(ps[:, c0:c0 + P], q_[r64, t, k * P:(k + 1) * P],
                                             k_[r64, t, k * P:(k + 1) * P],
                                             start=True, stop=False, skip_group_check=True)
                            nc.tensor.matmul(ps[:, c0:c0 + P], identb[:], trib[:],
                                             start=False, stop=True, skip_group_check=True)
                        nc.tensor.matmul(ps[:, 2 * P:3 * P], q_[r64, t, P:T], k_[r64, t, 0:P],
                                         start=True, stop=True, skip_group_check=True).then_inc(s["S"], 1)
                    else:
                        nc.tensor.matmul(ps[:, 0:T], q_[r64, t, 0:P], k_[r64, t, :],
                                         start=True, stop=True, skip_group_check=True)
                        nc.tensor.matmul(ps[:, T:2 * T], q_[r64, t, P:T], k_[r64, t, :],
                                         start=True, stop=True, skip_group_check=True).then_inc(s["S"], 1)
                if T_:
                    if h % 8 == 0:
                        after(pe, s["mrow"], 32 * (2 * bT + h // 8 + 1))
                    after(pe, s["exp"], 16 * bT + h - 1)
                    ps, q_, k_ = psT[h % 2], qst[rT], kst[rT]
                    nc.tensor.matmul(ps[:, 0:T], k_[m64, t, 0:P], q_[m64, t, :],
                                     start=True, stop=True, skip_group_check=True)
                    q0 = P if L.causal else 0
                    nc.tensor.matmul(ps[:, T:cols], k_[m64, t, P:T], q_[m64, t, q0:T],
                                     start=True, stop=True, skip_group_check=True).then_inc(s["ST"], 1)
                if T_ and h in (5, 9, 13):
                    pv_quad(bT, rT, (h - 5) // 4)
                if h == 1:
                    if T_:
                        after(pe, s["mxu"] if L.causal else s["mx"], (2 if L.causal else 16) * (bT + 1))
                        after(pe, s["x1"], 2 * bO)
                        max_transposes(bT, 1)
                    if O_:
                        pv_quad(bO, rO, 3)
                if h == 1 and S_ and not L.causal:
                    after(pe, s["pool"], PCH * (j - 1))
                    after(pe, s["v"], bS)
                    after(pe, s["row"], 4 * j if P_ else 4 * min(j, B))
                    nc.tensor.matmul(psM[:, 0:2 * H], ones_row[0:1, 0:P],
                                     prow[0:1, 0:2, :].rearrange("p a h -> p (a h)"),
                                     start=True, stop=True, skip_group_check=True)
                    for u in range(2):
                        last = nc.tensor.matmul(psM[0:8, 2 * H + u:2 * H + u + 1],
                                                prow[0:1, 2, 8 * u:8 * u + 8], ones_row[0:1, 0:1],
                                                start=False, stop=True, skip_group_check=True)
                    last.then_inc(s["bc_ps"], 1)
                if h == (2 if L.causal else 3) and P_:
                    after(pe, s["xs"], j + 1)
                    if not L.causal:
                        after(pe, s["bc"], 2 * (j - 1))
                        after(pe, s["row"], 4 * j)
                    after(pe, s["v"], j - 2)
                    after(pe, s["qk"], 2 * j)
                    after(pe, s["bcol"], 1)
                    after(pe, s["v_ps"], j - 4)
                    for k in range(2):
                        last = nc.tensor.transpose(psM[:, k * P:(k + 1) * P], xs[:, k, :], ident[:])
                    last.then_inc(s["xT_ps"], 1)
                if h == 5 and P_:
                    after(pe, s["xT"], j + 1)
                    for o in range(2):
                        last = nc.tensor.matmul(psM[:, o * T:(o + 1) * T], L.w_perm[:, o, :], xT[rP][:],
                                                start=(o == 0), stop=True, skip_group_check=True)
                    last.then_inc(s["qk_ps"], 1)
                if h == 12 and V_:
                    if not L.causal:
                        after(pe, s["bc"], 2 * (j - 1))
                    after(pe, s["m2"], 2 * bS + 1)
                    if P_:
                        after(pe, s["qk"], 2 * (j + 1))
                    else:
                        after(pe, s["qk"], 2 * B)
                    after(pe, s["v"], bS)
                    for k in range(2):
                        nc.tensor.matmul(psM[:, k * P:(k + 1) * P], xT[rS][:, k * P:(k + 1) * P], L.w_in[:, 2, :],
                                         start=(k == 0), stop=False, skip_group_check=True)
                        last = nc.tensor.matmul(psM[:, k * P:(k + 1) * P], ones_row[0:1, 0:P], L.b_in[0:1, 2, :],
                                                start=False, stop=True, skip_group_check=True)
                    last.then_inc(s["v_ps"], 1)
                if h == 14 and P_ and not L.causal:
                    after(pe, s["col"], 4 * j + 2)
                    after(pe, s["v"], bS + 1)
                    after(pe, s["bc"], 2 * (j - 1))
                    nc.tensor.matmul(psM[:, 0:T], head_ones, absq[:],
                                     start=True, stop=True, skip_group_check=True).then_inc(s["qsum_ps"], 1)
                if h == 15 and P_ and not L.causal:
                    after(pe, s["col"], 4 * j + 4)
                    after(pe, s["qsum"], j + 1)
                    for i in range(4):
                        last = nc.tensor.transpose(psM[0:1, i * P:(i + 1) * P], st[:, i:i + 1], ident[:])
                    last.then_inc(s["row_ps"], 1)
                if h == 4 and O_:
                    after(pe, s["oT"], 2 * bO + 2)
                    if T_:
                        after(pe, s["m2"], 2 * (bT + 1))
                    else:
                        after(pe, s["x1"], 2 * bO)
                    out_transposes(0)
                if h == 6 and O_:
                    out_transpose_on(0)
                if h == 8 and O_:
                    out_project(0)
                if h == 9 and S_:
                    after(pe, s["mxu"] if L.causal else s["mx"], 2 * bS + 1 if L.causal else 16 * bS + 8)
                    after(pe, s["qk"], 2 * (j + 1) if P_ else 2 * B)
                    after(pe, s["v"], bS)
                    if not L.causal:
                        after(pe, s["bc"], 2 * (j - 1))
                    max_transposes(bS, 0)
                if h == 11 and O_:
                    after(pe, s["x1"], 2 * bO + 1)
                    out_transposes(1)
                if h == 13 and O_:
                    out_transpose_on(1)
                if h == 14 and O_:
                    out_project(1)
                if L.pe_hook and isinstance(j, int):
                    L.pe_hook(pe, j, h)

        def act_setup(act, L):
            act.wait_ge(L.s["bcol_ps"], 1)
            nc.scalar.activation(L.b_col[:], psM[:, 0:2], ACT.Copy).then_inc(L.s["bcol"], 1)
            act.wait_ge(L.s["bcol"], 1)

        def act_step(act, L, j, c, P_, V_, S_, T_, O_):
            s = L.s
            bS, bT, bO = j - 2, j - 3, j - 4
            rP = c % 3
            cols = kcols(L)

            def split_copy(i):
                after(act, s["qk"], 2 * (j + 1))
                after(act, s["scr_w"], 96 * j)
                after(act, s["split"], 4 * j + 2 * i)
                src = qk if i == 0 else rest
                nc.scalar.activation(part[:, :, i, :], src[:], ACT.Copy).then_inc(s["split"], 1)

            def high_max(b, u, ring):
                after(act, s["mT"], 2 * b + u + 1)
                after(act, s["mscr"], 16 * (2 * b + u))
                if L.causal:
                    nc.scalar.activation(mrow[0:8, 0, :], (psM, psN)[u][0:8, 0:T], ACT.Copy).then_inc(s["m1"], 1)
                else:
                    after(act, s["bc"], 2 * (b + 1))
                    nc.scalar.activation(mrow[0:8, 0, :], (psM, psN)[u][0:8, 0:T], ACT.Identity,
                                         bias=neg_shift[ring][0:8, u:u + 1]).then_inc(s["m1"], 1)

            def evac_oT(b, half):
                after(act, s["PV"], 4 * b + 2 * half + 2)
                after(act, s["tO_ps"], 2 * b)
                nc.scalar.activation(oT[:, 2 * half:2 * half + 2, :], psO[half][:].rearrange("p (a t) -> p a t", a=2),
                                     ACT.Copy).then_inc(s["oT"], 1)

            def evac_onT(qb):
                after(act, s["onT_ps"], 2 * bO + qb + 1)
                after(act, s["y"], 2 * bO + qb)
                nc.scalar.activation(onT[:], psN[:, 0:P], ACT.Copy).then_inc(s["onT"], 1)

            for h in range(H):
                if h == 1 and T_:
                    high_max(bT, 1, (c - 3) % 3)
                if h == 2 and O_:
                    evac_oT(bO, 1)
                if h == (3 if L.causal else 4) and P_:
                    after(act, s["xT_ps"], j + 1)
                    after(act, s["v_ps"], j - 2)
                    nc.scalar.activation(xT[rP][:], psM[:, 0:T], ACT.Copy).then_inc(s["xT"], 1)
                if h in (6, 7) and P_:
                    after(act, s["qk_ps"], j + 1)
                    after(act, s["split"], 4 * j)
                    if not L.causal:
                        after(act, s["col"], 4 * j)
                    for o in (h - 6,):
                        nc.scalar.activation(qk[:, o, :], psM[:, o * T:(o + 1) * T], ACT.Identity,
                                             bias=L.b_col[:, o:o + 1]).then_inc(s["qk"], 1)
                if h == 7 and O_:
                    evac_onT(0)
                if h == 10 and S_:
                    high_max(bS, 0, (c - 2) % 3)
                if h == 14 and O_:
                    evac_onT(1)
                if L.act_hook and isinstance(j, int):
                    L.act_hook(act, j, h)
                if T_:
                    after(act, s["ST"], 16 * bT + h + 1)
                    after(act, s["PV"], 4 * bT + h // 4 - 1)
                    if L.causal:
                        nc.scalar.activation(pT[:, h % 8, 0:cols], psT[h % 2][:, 0:cols], ACT.Exp,
                                             scale=float(HD) ** -0.5).then_inc(s["exp"], 1)
                    else:
                        i = POS[h]
                        r = (c - 3) % 3
                        nc.scalar.activation(pT[:, h % 8, 0:cols], psT[h % 2][:, 0:cols], ACT.Exp,
                                             scale=scb[r][:, 0, i:i + 1],
                                             bias=scb[r][:, 1, i:i + 1]).then_inc(s["exp"], 1)
                if h in (9, 12) and P_ and L.causal:
                    split_copy(h // 12)
                if h == 8 and P_ and not L.causal:
                    after(act, s["qk"], 2 * j + 2)
                    after(act, s["qsum_ps"], j)
                    nc.scalar.activation(absq[:], qk[:, 0, :], ACT.Abs).then_inc(s["col"], 1)
                if h in (4, 10, 11) and P_ and not L.causal:
                    i = {4: 3, 10: 1, 11: 2}[h]
                    after(act, s["row_ps"], j)
                    after(act, s["col"], 4 * j)
                    src = (qk[:, 0, :], qk[:, 1, :], xT[rP][:])[i - 1]
                    if i == 3:
                        after(act, s["xT"], j + 1)
                    nc.scalar.activation(junk[:, i - 1, :], src, ACT.Square if i == 1 else ACT.Abs,
                                         accum_out=st[:, i:i + 1]).then_inc(s["col"], 1)
                if h == 13 and T_:
                    evac_oT(bT, 0)

        def dve_setup(dve, L):
            s = L.s
            dve.wait_ge(s["w"], 16 * 4)
            for o in range(2):
                nc.vector.tensor_copy(L.w_perm[:, o, :].rearrange("p (a t i) -> p a t i", a=2, t=8),
                                      L.w_in[:, o, :].rearrange("p (t a i) -> p a t i", a=2, t=8)).then_inc(s["wp"], 1)
                nc.vector.tensor_copy(L.b_perm[:, o, :].rearrange("p (a t i) -> p a t i", a=2, t=8),
                                      L.b_in[:, o, :].rearrange("p (t a i) -> p a t i", a=2, t=8)).then_inc(s["wp"], 1)

        def dve_step(dve, L, j, c, P_, V_, S_, T_, O_):
            s = L.s
            bS, bT, bO = j - 2, j - 3, j - 4
            rS = (c - 2) % 3
            C_ = not L.causal and (not isinstance(j, int) or 0 <= j - 1 < B)

            def split_rest(i):
                after(dve, s["qk"], 2 * (j + 1))
                after(dve, s["split"], 4 * j + 2 * i + 1)
                o = part[:, :, 2, :] if i else rest[:]
                nc.vector.tensor_tensor(out=o, in0=rest[:] if i else qk[:], in1=part[:, :, i, :],
                                        op=ALU.subtract).then_inc(s["split"], 1)

            def low_max(b, u, ring):
                after(dve, s["m1"], 2 * b + u + 1)
                shift = 0.0 if L.causal else neg_shift[ring][0:8, u:u + 1]
                nc.vector.scalar_tensor_tensor(out=mrow[0:8, 1, :], in0=(psM, psN)[u][0:8, 0:T], scalar=shift,
                                               in1=mrow[0:8, 0, :], op0=ALU.add,
                                               op1=ALU.subtract).then_inc(s["m2"], 1)

            def normalise(qb):
                after(dve, s["tO_ps"], 2 * bO + qb + 1)
                after(dve, s["onT_ps"], 2 * bO + qb)
                o4 = psN[:].rearrange("p (h c) -> p h c", c=32)
                nc.vector.reciprocal(rden[:], o4[:, :, HD]).then_inc(s["rden"], 1)
                after(dve, s["rden"], 2 * bO + qb + 1)
                nc.vector.tensor_tensor(out=on[:].rearrange("p (h c) -> p h c", c=HD), in0=o4[:, :, 0:HD],
                                        in1=rden[:].unsqueeze(2).to_broadcast([P, H, HD]),
                                        op=ALU.mult).then_inc(s["on"], 1)

            def residual(qb):
                after(dve, s["y"], 2 * bO + qb + 1)
                blk = x[:, bass.ds(2 * bO + qb, 1), :]
                nc.vector.tensor_tensor(out=blk, in0=blk, in1=psN[:, P:2 * P].unsqueeze(1),
                                        op=ALU.add).then_inc(s["x1"], 1)

            for h in range(H):
                if L.causal and ((h == 8 and S_) or (h == 0 and T_)):
                    b, u = (bS, 0) if h == 8 else (bT, 1)
                    after(dve, s["mx"], 16 * b + 8 * u + 8)
                    after(dve, s["mT"], 2 * b + u - 1)
                    nc.vector.tensor_tensor(out=mxu[:, u], in0=mx3[:, u, 0:2, :], in1=mx3[:, u, 0:3:2, :],
                                            op=ALU.max).then_inc(s["mxu"], 1)
                if S_:
                    u = h // 8
                    pos = (h % 2) * 4 + (h % 8) // 2
                    after(dve, s["S"], 16 * bS + h + 1)
                    if h % 8 == 0:
                        if L.causal:
                            after(dve, s["mxu"], 2 * bS + u - 1)
                        else:
                            after(dve, s["mT"], 2 * bS + u - 1)
                    n = 3 if L.causal else 2
                    nc.vector.tensor_reduce(mx3[:, u, 0:n, pos:pos + 1].rearrange("p a b -> p (a b)"),
                                            psS[h % 2][:, 0:kcols(L)].rearrange("p (a k) -> p a k", a=n),
                                            AX_X, ALU.max).then_inc(s["mx"], 1)
                if h == 0 and P_:
                    after(dve, s["xT_ps"], j)
                    for k in range(2):
                        blk = 2 * j + k
                        ins = nc.vector.tensor_scalar(xs[:, k, :].unsqueeze(1), x[:, bass.ds(blk, 1), :],
                                                      mean_rstd[:, bass.ds(blk, 1), 0:1].rearrange("p a b -> p (a b)"),
                                                      mean_rstd[:, bass.ds(blk, 1), 1:2].rearrange("p a b -> p (a b)"),
                                                      ALU.subtract, ALU.mult)
                    ins.then_inc(s["xs"], 1)
                if h == 2 and T_:
                    low_max(bT, 1, (c - 3) % 3)
                if h == 5 and O_:
                    normalise(0)
                if h == 9 and O_:
                    residual(0)
                if h == 3 and C_:
                    after(dve, s["pool"], PCH * (j - 1) + 2)
                    nc.vector.tensor_scalar(prow[0:1, 6, :].bitcast(I32), prow[0:1, 4, :].bitcast(I32), 1, None,
                                            ALU.logical_shift_right).then_inc(s["seed"], 1)
                    after(dve, s["seed"], 2 * j - 1)
                    nc.vector.tensor_scalar(prow[0:1, 7, :].bitcast(I32), prow[0:1, 6, :].bitcast(I32), -1.0,
                                            RSQRT_MAGIC, ALU.mult, ALU.add).then_inc(s["seed"], 1)
                if h == 1 and S_ and not L.causal:
                    r = (c - 2) % 3
                    after(dve, s["bc_ps"], j - 1)
                    after(dve, s["exp"], 16 * (j - 5) + 16)
                    nc.vector.tensor_copy(scb[r][:].rearrange("p a h -> p (a h)"),
                                          psM[:, 0:2 * H]).then_inc(s["bc"], 1)
                    nc.vector.tensor_copy(neg_shift[r][:], psM[0:8, 2 * H:2 * H + 2]).then_inc(s["bc"], 1)
                if h == 14 and P_ and not L.causal:
                    after(dve, s["qsum_ps"], j + 1)
                    after(dve, s["row_ps"], j)
                    nc.vector.tensor_reduce(st[:, 0:1], psM[:, 0:T], AX_X, ALU.max).then_inc(s["qsum"], 1)
                if h == 15 and P_ and not L.causal:
                    after(dve, s["row_ps"], j + 1)
                    after(dve, s["pool"], PCH * j)
                    for i, op in enumerate((ALU.max, ALU.add, ALU.max)):
                        for u in range(2):
                            src = psM[0:1, i * P:(i + 1) * P].rearrange("p (a u t i) -> p u a t i", a=2, u=2, i=HD)
                            ins = nc.vector.tensor_reduce(
                                row[0:1, 16 * i + 8 * u:16 * i + 8 * u + 8].rearrange("p (a t) -> p a t", a=2),
                                src[:, u], AX_X, op)
                        ins.then_inc(s["row"], 1)
                    nc.vector.tensor_reduce(row[0:1, 48:49], psM[0:1, 3 * P:4 * P], AX_X,
                                            ALU.max).then_inc(s["row"], 1)
                if h == 11 and P_ and L.causal:
                    split_rest(0)
                if h == 10 and S_:
                    low_max(bS, 0, (c - 2) % 3)
                if h == 13 and V_:
                    after(dve, s["v_ps"], bS + 1)
                    after(dve, s["PV"], 4 * (bS - 2))
                    nc.vector.tensor_copy(vp[rS][:, :, :, 0:HD],
                                          psM[:, 0:T].rearrange("p (k h c) -> p k h c", k=2, c=HD)).then_inc(s["v"], 1)
                if h == 12 and O_:
                    normalise(1)
                if h == 14 and P_ and L.causal:
                    split_rest(1)
                if h == 15 and O_:
                    residual(1)
                if L.dve_hook and isinstance(j, int):
                    L.dve_hook(dve, j, h)

        def pool_step(pool, L, j, c, P_, V_, S_, T_, O_):
            s = L.s
            bT = j - 3
            if L.pool_hook and isinstance(j, int):
                L.pool_hook(pool, j, 0)
            if not L.causal and (not isinstance(j, int) or 0 <= j - 1 < B):
                S2, C, NC, KK, V, W, SH, Y = (prow[0:1, i, :] for i in range(8))
                q_row, fro, k_col = (row[0:1, 16 * i:16 * i + 16] for i in range(3))
                inf_x = row[0:1, 48:49].to_broadcast([1, H])
                m05, p15 = half[0:1, 0, :], half[0:1, 1, :]
                mul, add = ALU.mult, ALU.add
                ops = [(W, fro, inf_x, mul), (V, W, inf_x, mul)]
                ops += [(NC, q_row, q_row, mul), (KK, k_col, k_col, mul), (NC, NC, KK, add), (NC, NC, m05, mul)]
                for it in range(3):
                    src = Y if it == 0 else S2
                    ops += [(W, src, src, mul), (W, W, V, mul), (W, W, m05, mul), (W, W, p15, add), (S2, src, W, mul)]
                ops += [(S2, S2, S2, add), (C, NC, S2, mul)]
                assert len(ops) == PCH
                after(pool, s["row"], 4 * j)
                after(pool, s["bc_ps"], j - 1)
                for n, (o, a, b_, op) in enumerate(ops):
                    if n > 0:
                        after(pool, s["pool"], PCH * (j - 1) + n)
                    if n == 6:
                        after(pool, s["seed"], 2 * j)
                    nc.gpsimd.tensor_tensor(out=o, in0=a, in1=b_, op=op).then_inc(s["pool"], 1)
            if not L.causal and P_:
                nothing = zero[:, 0:1].unsqueeze(2).to_broadcast([P, 2, T])
                after(pool, s["qk"], 2 * (j + 1))
                after(pool, s["scr_w"], 96 * j)
                for n, (o, a, b_, op) in enumerate(((part[:, :, 0, :], qk[:], nothing, ALU.add),
                                                    (rest[:], qk[:], part[:, :, 0, :], ALU.subtract),
                                                    (part[:, :, 1, :], rest[:], nothing, ALU.add),
                                                    (part[:, :, 2, :], rest[:], part[:, :, 1, :], ALU.subtract))):
                    if n > 0:
                        after(pool, s["split"], 4 * j + n)
                    nc.gpsimd.tensor_tensor(out=o, in0=a, in1=b_, op=op).then_inc(s["split"], 1)
            if not L.causal and isinstance(j, int):
                L.pool_hook(pool, j, H)
            if L.causal and T_:
                fixed(pool, 16 * bT + 1)
                for h in range(H):
                    after(pool, s["exp"], 16 * bT + h + 1)
                    if h < H - 1:
                        fixed(pool, 16 * bT + h + 2)
                    else:
                        nc.gpsimd.tensor_tensor(out=tick[:, 0:1], in0=tick[:, 1:2], in1=tick[:, 1:2], op=ALU.add)
                    d = pT[:, h % 8, 0:384].rearrange("p (a k) -> p a k", a=3)[:, 0:3:2, :]
                    nc.gpsimd.affine_select(out=d, in_=d, compare_op=ALU.is_ge, fill=0.0, base=0,
                                            pattern=[[0, 2], [1, P]], channel_multiplier=-1).then_inc(s["pT"], 1)
                    if L.pool_hook and isinstance(j, int):
                        L.pool_hook(pool, j, h + 1)

        def sp_step(sp, L, j, c, P_, V_, S_, T_, O_):
            s = L.s
            bS, bT = j - 2, j - 3

            def max_rows(b, u, r):
                ready, read, written = (fixed(sp, v) for v in (2 * b + u + 1, 32 * (2 * b + u), 16 * (2 * b + u + 1)))
                after(sp, s["m2"], ready)
                after(sp, s["mrow"], read)
                sp.dma_start(scr_m[u], mrow[:]).then_inc(s["mscr"], 16)
                after(sp, s["mscr"], written)
                for par in range(2):
                    sp.dma_start(qst[r][64 * par + ROWS:64 * par + ROWS + 2, 4 * u:4 * u + 4, :],
                                 scr_m[u, 4 * par:4 * par + 4].rearrange("t k q -> k t q")).then_inc(s["mrow"], 16)

            def beside(point):
                if L.sp_hook and isinstance(j, int):
                    L.sp_hook(sp, j, point)

            if T_:
                max_rows(bT, 1, (c - 3) % 3)
            beside(0)
            if not isinstance(j, int) or 0 <= j - 1 < B:
                b, r = j - 1, (c - 1) % 3
                ready, read, written, scored = (fixed(sp, v) for v in (4 * (b + 1), 64 * b, 96 * (b + 1), 16 * (b - 2)))
                after(sp, s["split"], ready)
                after(sp, s["stack"], read)
                q3 = part[:, 0, :, :]
                k3 = part[:, 1, :, :]
                sp.dma_start(scr_part[0, :, 0:3, :], q3).then_inc(s["scr_w"], 16)
                sp.dma_start(scr_part[0, :, 3:5, :], q3[:, 0:2, :]).then_inc(s["scr_w"], 16)
                sp.dma_start(scr_part[0, :, 5:6, :], q3[:, 0:1, :]).then_inc(s["scr_w"], 16)
                sp.dma_start(scr_part[1, :, 0:3:2, :], k3[:, 0:1, :].to_broadcast([P, 2, T])).then_inc(s["scr_w"], 16)
                sp.dma_start(scr_part[1, :, 1:4:2, :], k3[:, 0:2, :]).then_inc(s["scr_w"], 16)
                sp.dma_start(scr_part[1, :, 4:6, :], k3[:, 1:3, :]).then_inc(s["scr_w"], 16)
                after(sp, s["scr_w"], written)
                after(sp, s["ST"], scored)
                after(sp, s_mset, 2 * RING)
                for o, st in enumerate((qst, kst)):
                    for par in range(2):
                        sp.dma_start(st[r][64 * par:64 * par + ROWS, :, :],
                                     scr_part[o, 64 * par:64 * par + 64].rearrange("(t i) r q -> (i r) t q", t=8)
                                     ).then_inc(s["stack"], 16)
            beside(1)
            if S_:
                max_rows(bS, 0, (c - 2) % 3)
            beside(2)
            beside(3)

        def pipeline(step, eng, L):
            def flags(j):
                return [0 <= j < B] + [0 <= j - d < B for d in (2, 2, 3, 4)]

            for j in range(7):
                step(eng, L, j, j % 3, *flags(j))
            with eng.Fori(7, B - 2, 3) as j:
                for d in range(3):
                    step(eng, L, j + d, (7 + d) % 3, True, True, True, True, True)
            for j in range(B, B + 4):
                step(eng, L, j, j % 3, *flags(j))

        def dve_ln_stats(dve, lo, hi, done):
            for k in range(lo, hi):
                ins = nc.vector.bn_stats(bn6[:, k, :], x[:, k, :])
            link(ins)
            for k in range(lo, hi):
                ins = nc.vector.bn_aggr(mean_rstd[:, k, :], bn6[:, k, :])
            link(ins)
            dve_ln_root(lo, hi, done)

        def dve_ln_root(lo, hi, done):
            ve, y, a = (nwt[:, i, lo:hi] for i in range(3))
            link(nc.vector.tensor_scalar(ve, mean_rstd[:, lo:hi, 1], EPS, None, ALU.add))
            rsqrt(ve, y, a)
            nc.vector.tensor_copy(mean_rstd[:, lo:hi, 1], y).then_inc(done, 1)

        def rsqrt(v, y, a):
            link(nc.vector.tensor_scalar(a.bitcast(I32), v.bitcast(I32), 1, None, ALU.logical_shift_right))
            link(nc.vector.tensor_scalar(y.bitcast(I32), a.bitcast(I32), -1.0, RSQRT_MAGIC, ALU.mult, ALU.add))
            for _ in range(3):
                link(nc.vector.scalar_tensor_tensor(out=a, in0=y, scalar=-0.5, in1=y, op0=ALU.mult, op1=ALU.mult))
                link(nc.vector.tensor_tensor(out=a, in0=a, in1=v, op=ALU.mult))
                link(nc.vector.scalar_tensor_tensor(out=y, in0=a, scalar=1.5, in1=y, op0=ALU.add, op1=ALU.mult))

        def tiles_done(p, count):
            return 16 * ((count + 1 - p) // 2)

        def ffn_over(eng, l):
            eng.wait_ge(f_sem["y"], TILES * (l + 1))
            for i in range(2):
                eng.wait_ge(f_st[i], tiles_done(i, TILES * (l + 1)))

        def layer_over(eng, L):
            s = L.s
            for name, count in (("x1", 2 * B), ("y", 2 * B), ("exp", 16 * B), ("PV", 4 * B), ("oT", 2 * B),
                                ("onT", 2 * B), ("stack", 64 * B), ("mrow", 64 * B), ("v", B), ("split", 4 * B),
                                ("pT", 16 * B)):
                eng.wait_ge(s[name], count)

        logit_bank = [psM, psO[0]]
        count_bank = [psM, psO[1]]

        def dve_ln_at(dve, h, lo, done, times):
            if h < 8:
                for k in (lo + 2 * h, lo + 2 * h + 1):
                    ins = nc.vector.bn_stats(bn6[:, k, :], x[:, k, :])
                if h == 7:
                    link(ins)
            elif h < 10:
                for k in range(lo + 8 * (h - 8), lo + 8 * (h - 7)):
                    ins = nc.vector.bn_aggr(mean_rstd[:, k, :], bn6[:, k, :])
                link(ins)
            elif h == 10:
                dve_ln_root(lo, lo + GBLK, done)
                dve.wait_ge(done, times)

        def dve_tokens(dve, n, lo, hi):
            for k in range(lo, hi):
                nc.vector.tensor_scalar(xn[:, k, :], x[:, k, :], mean_rstd[:, k, 0:1], mean_rstd[:, k, 1:2],
                                        ALU.subtract, ALU.mult).then_inc(r_sem["xn"], 1)

        def pe_tokens(pe, n, i):
            g, r = n % G, r_sem
            pe.wait_ge(r["xn"], GBLK * n + 4 * i + 4)
            if i > 0:
                pe.wait_ge(r["T"], 4 * n + i)
            for m in range(4):
                last = nc.tensor.transpose(psM[:, m * P:(m + 1) * P],
                                           xn[:, g * GBLK + 4 * i + m, :], ident[:])
            last.then_inc(r["T_ps"], 1)

        def pe_logits(pe, n, i):
            g, r = n % G, r_sem
            pe.wait_ge(r["T"], 4 * n + (4 if g == 0 else i + 1))
            for m in range(4):
                k = 4 * i + m
                last = nc.tensor.matmul(logit_bank[g][:, E * k:E * k + E], xnT[i][:, m * P:(m + 1) * P], wr[:],
                                        start=True, stop=True, skip_group_check=True)
            last.then_inc(r["lg_ps"], 1)

        def pe_counts(pe, n):
            g, r = n % G, r_sem
            pe.wait_ge(r["pickb"], n + 1)
            rhs = pickb[:].rearrange("p k e -> p (k e)")
            ps = count_bank[g]
            nc.tensor.matmul(ps[:, 0:P], triu[:], rhs, start=True, stop=True, skip_group_check=True)
            nc.tensor.matmul(ps[:, P:2 * P], onesb[:], rhs, start=True, stop=True,
                             skip_group_check=True).then_inc(r["cnt_ps"], 1)

        def pe_route(pe, n):
            pe_tokens(pe, n, 3)
            pe_logits(pe, n, 3)
            pe_counts(pe, n)

        def act_tokens(act, n, i):
            r = r_sem
            act.wait_ge(r["T_ps"], 4 * n + i + 1)
            after(act, r["lg_ps"], 4 * (n - 1) + i + 1)
            nc.scalar.activation(xnT[i][:], psM[:], ACT.Copy).then_inc(r["T"], 1)

        def act_weights(act, n):
            r = r_sem
            act.wait_ge(r["d12"], n + 1)
            nc.scalar.activation(e1[:], v12[:, 2, :], ACT.Exp).then_inc(r["e12"], 1)

        def act_route(act, n):
            act_tokens(act, n, 3)
            act_weights(act, n)

        def dve_counts(dve, n):
            r = r_sem
            dve.wait_ge(r["cnt_ps"], n + 1)
            nc.vector.tensor_copy(counts[:], count_bank[n % G][:, 0:2 * P]).then_inc(r["cnt"], 1)
            dve.wait_ge(r["cnt"], n + 1)

        def dve_route(dve, n):
            for stage in (0, 1, 2):
                dve_route_part(dve, n, stage)
            dve_counts(dve, n)
            for stage in range(3, 8):
                dve_route_part(dve, n, stage)

        def dve_route_part(dve, n, stage):
            g = n % G
            r = r_sem
            w = wgt[g]
            shape = [P, GBLK, E]
            desc = cst[:, CST_DESC:CST_DESC + E].unsqueeze(1).to_broadcast(shape)

            def wide(a):
                return a.unsqueeze(2).to_broadcast(shape)

            if stage == 0:
                dve.wait_ge(r["lg_ps"], 4 * (n + 1))
                nc.vector.tensor_copy(lg[:].rearrange("p k e -> p (k e)"), logit_bank[g][:, 0:P]).then_inc(r["lg"], 1)
                dve.wait_ge(r["lg"], n + 1)
            if stage < 2:
                i = stage
                link(nc.vector.tensor_reduce(v12[:, i, :], lg[:], AX_X, ALU.max))
                link(nc.vector.tensor_tensor(out=ea[:], in0=lg[:], in1=wide(v12[:, i, :]), op=ALU.is_equal))
                link(nc.vector.tensor_tensor(out=ea[:], in0=ea[:], in1=desc, op=ALU.mult))
                link(nc.vector.tensor_reduce(slotf[:, 0, :], ea[:], AX_X, ALU.max))
                link(nc.vector.tensor_tensor(out=pick[i][:], in0=desc, in1=wide(slotf[:, 0, :]), op=ALU.is_equal))
            if stage == 0:
                link(nc.vector.scalar_tensor_tensor(out=lg[:], in0=pick[0][:], scalar=-1e38, in1=lg[:],
                                                    op0=ALU.mult, op1=ALU.add))
            if stage == 1:
                nc.vector.tensor_tensor(out=v12[:, 2, :], in0=v12[:, 1, :], in1=v12[:, 0, :],
                                        op=ALU.subtract).then_inc(r["d12"], 1)
                nc.vector.tensor_tensor(out=pickb[:], in0=pick[0][:], in1=pick[1][:],
                                        op=ALU.add).then_inc(r["pickb"], 1)
            if stage == 2:
                dve.wait_ge(r["e12"], n + 1)
                link(nc.vector.tensor_scalar(slotf[:, 0, :], e1[:], 1.0, None, ALU.add))
                link(nc.vector.reciprocal(slotf[:, 1, :], slotf[:, 0, :]))
                link(nc.vector.tensor_scalar(w[:, 0, :], slotf[:, 1, :], DEPTH_SCALE, None, ALU.mult))
                link(nc.vector.tensor_tensor(out=w[:, 1, :], in0=w[:, 0, :], in1=e1[:], op=ALU.mult))
            cnt = counts[:, P:2 * P].rearrange("p (k e) -> p k e", e=E)
            pre = counts[:, 0:P].rearrange("p (k e) -> p k e", e=E)
            a, b = ea, eb
            end = pc[:, 1, :]
            if stage == 3:
                link(nc.vector.tensor_copy(ea[:], cnt))
                for sh in (1, 2, 4, 8):
                    nc.vector.tensor_copy(b[:, 0:sh, :], a[:, 0:sh, :])
                    link(nc.vector.tensor_tensor(out=b[:, sh:, :], in0=a[:, sh:, :], in1=a[:, :GBLK - sh, :], op=ALU.add))
                    a, b = b, a
            if stage == 4:
                link(nc.vector.tensor_scalar(pc[:, 0, :], a[:, GBLK - 1, :], float(P - 1), None, ALU.add))
                link(nc.vector.tensor_copy(pci[:, 0, :], pc[:, 0, :]))
                link(nc.vector.tensor_scalar(pci[:, 1, :], pci[:, 0, :], 7, None, ALU.logical_shift_right))
                link(nc.vector.tensor_scalar(pci[:, 0, :], pci[:, 1, :], 7, None, ALU.logical_shift_left))
            if stage == 5:
                link(nc.vector.tensor_copy(pc[:, 0, :], pci[:, 0, :]))
                c, d = 0, 1
                for sh in (1, 2, 4):
                    nc.vector.tensor_copy(pc[:, d, 0:sh], pc[:, c, 0:sh])
                    link(nc.vector.tensor_tensor(out=pc[:, d, sh:], in0=pc[:, c, sh:], in1=pc[:, c, :E - sh], op=ALU.add))
                    c, d = d, (2 if d == 1 else 1)
                link(nc.vector.tensor_tensor(out=pc[:, 3, :], in0=end, in1=pc[:, 0, :], op=ALU.subtract))
            if stage == 6:
                link(nc.vector.tensor_tensor(out=b[:], in0=a[:], in1=cnt, op=ALU.subtract))
                link(nc.vector.tensor_tensor(out=a[:], in0=b[:], in1=pre, op=ALU.add))
                link(nc.vector.tensor_tensor(out=b[:], in0=a[:], in1=pc[:, 3, :].unsqueeze(1).to_broadcast(shape),
                                             op=ALU.add))
                for i in range(2):
                    link(nc.vector.tensor_tensor(out=a[:], in0=b[:], in1=pick[i][:], op=ALU.mult))
                    link(nc.vector.tensor_reduce(slotf[:, i, :], a[:], AX_X, ALU.add))
            if stage == 7:
                tile0 = cst[0:1, CST_TILE:CST_TILE + NT]
                link(nc.vector.tensor_tensor(out=cmpt[:], in0=end[0:1].unsqueeze(1).to_broadcast([1, NT, E]),
                                             in1=tile0.unsqueeze(2).to_broadcast([1, NT, E]), op=ALU.is_le))
                link(nc.vector.tensor_reduce(tef[:], cmpt[:], AX_X, ALU.add))
                link(nc.vector.tensor_scalar(tef[:], tef[:], float(E - 1), float(HID), ALU.min, ALU.mult))
                nc.vector.tensor_copy(te[:, g * NT:(g + 1) * NT], tef[:]).then_inc(r["slots"], 1)
                nc.vector.tensor_copy(slot[g][:], slotf[:]).then_inc(r["slots"], 1)

        def pool_scatter(pool, n, pairs):
            g = n % G
            if pairs[0] == 0:
                pool.wait_ge(r_sem["slots"], 2 * (n + 1))
            for pair in pairs:
                k, i = pair // 2, pair % 2
                nc.gpsimd.indirect_dma_start(
                    xg[g], bass.IndirectOffsetOnAxis(ap=slot[g][:, i, k:k + 1], axis=0),
                    xn[:, g * GBLK + k, :], None).then_inc(r_scat[g], 16)

        def pool_gather(pool, n, quarters):
            g = n % G
            if quarters[0] == 0:
                for i in range(2):
                    pool.wait_ge(f_st[i], tiles_done(i, NT * (n + 1)))
                if g == 1:
                    pool.wait_ge(r_scat[0], 16 * 2 * GBLK * (n // G + 1))
                    pool.wait_ge(r_scat[1], 16 * 2 * GBLK * (n // G + 1))
            for k in range(4 * quarters[0], 4 * quarters[-1] + 4):
                for i in range(2):
                    nc.gpsimd.indirect_dma_start(
                        gb[g][:, 2 * k + i, :], None, eo[g],
                        bass.IndirectOffsetOnAxis(ap=slot[g][:, i, k:k + 1], axis=0)).then_inc(r_gat[g][k // 4], 16)

        def dve_add_expert(n, k, i):
            blk = x[:, bass.ds(k, 1), :]
            w = wgt[0][:, i, bass.ds(k, 1)]
            nc.vector.scalar_tensor_tensor(out=blk, in0=gb[0][:, bass.ds(2 * k + i, 1), :], scalar=w,
                                           in1=blk, op0=ALU.mult, op1=ALU.add).then_inc(r_sem["x"], 1)

        def dve_combine_0(dve, l, k):
            n = 2 * l + 1
            dve_add_expert(n, k, 0)
            dve.wait_ge(r_sem["x"], 2 * GBLK * (n - 1) + 2 * k + 1)
            dve_add_expert(n, k, 1)

        def dve_combine_1(dve, n, q):
            dve.wait_ge(r_gat[1][q], 16 * 8 * (n // G + 1))
            for i in range(2):
                for k in range(4 * q, 4 * q + 4):
                    blk = x[:, GBLK + k, :]
                    nc.vector.scalar_tensor_tensor(out=blk, in0=gb[1][:, 2 * k + i, :], scalar=wgt[1][:, i, k:k + 1],
                                                   in1=blk, op0=ALU.mult, op1=ALU.add).then_inc(r_sem["x"], 1)
                dve.wait_ge(r_sem["x"], 2 * GBLK * n + 8 * q + 4 * (i + 1))

        def tile_loop(step, eng, l, second=None, window=None, between=None, last=None):
            start = TILES - 2 - GBLK
            for k in range(4):
                step(eng, l, k, k % 2)
            for lo, hi in ((4, NT - 3), (NT - 3, start), (start, TILES - 2)):
                if lo == NT - 3 and second is not None:
                    second()
                if lo == start and window is not None:
                    window()
                with eng.Fori(lo, hi - 3, 4) as k:
                    for d in range(4):
                        step(eng, l, k + d, d % 2)
                        if lo == start and between is not None:
                            between(eng, l, k + d - start)
            for k in range(TILES - 2, TILES + 2):
                step(eng, l, k, k % 2)
                if last is not None:
                    last(eng, l, k - TILES + 2)

        def live(k, d):
            return not isinstance(k, int) or 0 <= k + d < TILES

        def pe_tile(pe, l, k, p):
            f, n0 = f_sem, l * TILES

            def tokens(t, p):
                after(pe, f_ld[p], 8 * (n0 + t - p) + 16)
                after(pe, f["xT"], n0 + t)
                nc.tensor.transpose(psM[:, 0:P], xin[p][:], ident[:]).then_inc(f["T_ps"], 1)

            if isinstance(k, int) and k == 0:
                tokens(0, 0)
            if live(k, 0):
                e = pe.value_load(te[0:1, bass.ds(k, 1)], min_val=0, max_val=(E - 1) * HID)
                after(pe, f["xT"], n0 + k + 1)
                after(pe, f["silu"], n0 + k - 1)
                after(pe, f["h"], n0 + k - 1)
                nc.tensor.matmul(psS[p][:], xTt[p][:], wg[:, bass.ds(e, HID)], start=True, stop=True)
                nc.tensor.matmul(psT[p][:], xTt[p][:], wu[:, bass.ds(e, HID)],
                                 start=True, stop=True).then_inc(f["gu"], 1)
            if live(k, 1):
                tokens(k + 1, 1 - p)
            if live(k, -1):
                after(pe, f["h"], n0 + k)
                for half_, done in ((0, "hTa"), (1, "hTb")):
                    after(pe, f[done], n0 + k - 1)
                    for m in range(2):
                        hb = 2 * half_ + m
                        last = nc.tensor.transpose(psO[half_][:, m * P:(m + 1) * P],
                                                   hh[1 - p][:, hb * P:(hb + 1) * P], ident[:])
                    last.then_inc(f["hT_ps"], 1)
            if live(k, -2):
                e = pe.value_load(te[0:1, bass.ds(k - 2, 1)], min_val=0, max_val=(E - 1) * HID)
                after(pe, f["hTa"], n0 + k - 1)
                after(pe, f["hTb"], n0 + k - 1)
                after(pe, f["y"], n0 + k - 2)
                for hb in range(HB):
                    last = nc.tensor.matmul(psN[:, 0:P], hT[p][:, hb, :], wd[:, bass.ds(e + hb * P, P)],
                                            start=(hb == 0), stop=(hb == HB - 1))
                last.then_inc(f["y_ps"], 1)

        def act_tile(act, l, k, p):
            f, n0 = f_sem, l * TILES

            def tokens(t, p):
                after(act, f["T_ps"], n0 + t + 1)
                after(act, f["gu"], n0 + t - 1)
                nc.scalar.activation(xTt[p][:], psM[:, 0:P], ACT.Copy).then_inc(f["xT"], 1)

            if isinstance(k, int) and k == 0:
                tokens(0, 0)
            if live(k, 1):
                tokens(k + 1, 1 - p)
            if live(k, 0):
                after(act, f["gu"], n0 + k + 1)
                after(act, f["h"], n0 + k - 1)
                nc.scalar.activation(sg[p][:], psS[p][:], ACT.Silu).then_inc(f["silu"], 1)
            if live(k, -1):
                after(act, f["hT_ps"], 2 * (n0 + k) - 1)
                after(act, f["y_ps"], n0 + k - 2)
                nc.scalar.activation(hT[1 - p][:, 0:2, :], psO[0][:, 0:2 * P].rearrange("p (a c) -> p a c", a=2),
                                     ACT.Copy).then_inc(f["hTa"], 1)

        def dve_tile(dve, l, k, p):
            f, n0 = f_sem, l * TILES
            if live(k, -1):
                after(dve, f["hT_ps"], 2 * (n0 + k))
                after(dve, f["y_ps"], n0 + k - 2)
                nc.vector.tensor_copy(hT[1 - p][:, 2:4, :],
                                      psO[1][:, 0:2 * P].rearrange("p (a c) -> p a c", a=2)).then_inc(f["hTb"], 1)
            if live(k, 0):
                after(dve, f["silu"], n0 + k + 1)
                after(dve, f["hT_ps"], 2 * (n0 + k - 1))
                nc.vector.tensor_tensor(out=hh[p][:], in0=sg[p][:], in1=psT[p][:], op=ALU.mult).then_inc(f["h"], 1)
            if live(k, -2):
                after(dve, f["y_ps"], n0 + k - 1)
                after(dve, f_st[p], 8 * (n0 + k - 2 - p))
                nc.vector.tensor_copy(ysb[p][:], psN[:, 0:P]).then_inc(f["y"], 1)

        def sp_tile(sp, l, k, p, g_load, g_store):
            f, n0 = f_sem, l * TILES
            if isinstance(k, int) and k == 0:
                for t in range(2):
                    after(sp, f["T_ps"], n0)
                    sp.dma_start(xin[t][:], xg[0][t * P:(t + 1) * P, :]).then_inc(f_ld[t], 16)
            if live(k, 2):
                used, row0 = fixed(sp, n0 + k + 1), fixed(sp, (k + 2 - g_load * NT) * P)
                after(sp, f["T_ps"], used)
                sp.dma_start(xin[p][:], xg[g_load][bass.ds(row0, P), :]).then_inc(f_ld[p], 16)
            if live(k, -2):
                ready, row0 = fixed(sp, n0 + k - 1), fixed(sp, (k - 2 - g_store * NT) * P)
                after(sp, f["y"], ready)
                sp.dma_start(eo[g_store][bass.ds(row0, P), :], ysb[p][:]).then_inc(f_st[p], 16)

        block = ctx.enter_context(nc.Block())

        def load_layer(sp, L, weights, biases):
            for i, (w, b) in enumerate(zip(weights, biases)):
                done = L.s["w"] if i < 2 else L.s["w_vo"]
                sp.dma_start(L.w_in[:, i, :], w).then_inc(done, 16)
                sp.dma_start(L.b_in[0:1, i, :], b.rearrange("(a n) -> a n", a=1)).then_inc(done, 16)

        def sp_ffn(sp, l):
            def dispatched(g):
                sp.wait_ge(r_scat[g], 16 * 2 * GBLK * (l + 1))

            dispatched(0)
            if l > 0:
                for g in range(G):
                    for q in range(4):
                        sp.wait_ge(r_gat[g][q], 16 * 8 * l)
            for k in range(4):
                sp_tile(sp, l, k, k % 2, 0, 0)
            with sp.Fori(4, NT - 6, 4) as k:
                for d in range(4):
                    sp_tile(sp, l, k + d, d % 2, 0, 0)
            for k in range(NT - 3, NT + 5):
                if k == NT - 2:
                    dispatched(1)
                sp_tile(sp, l, k, k % 2, k + 2 >= NT, k - 2 >= NT)
            with sp.Fori(NT + 5, TILES - 5, 4) as k:
                for d in range(4):
                    sp_tile(sp, l, k + d, d % 2, 1, 1)
            for k in range(TILES - 2, TILES + 2):
                sp_tile(sp, l, k, k % 2, 1, 1)

        def pool_beside(l):
            def hook(pool, j, h):
                if l == 1 and j in (0, 2, 3, 4) and h == H:
                    q = max(j - 1, 0)
                    pool_gather(pool, 1, range(q, q + 1))
                if j == 18 and l == 0:
                    if h == 0:
                        pool.wait_ge(s_zfill, 16 * 8)
                    pool_scatter(pool, 0, range(h, h + 1))
                if j == 18 and l == 1 and h == 0:
                    pool_scatter(pool, 2, range(17))
            return hook

        def sp_beside(sp, j, point):
            experts = slice(2 * point, 2 * point + 2)
            if j in (3, 4):
                w, name = ((wg, "L0_ffn_Wg"), (wu, "L0_ffn_Wu"))[j - 3]
                sp.dma_start(w[:].rearrange("p (e h) -> p e h", e=E)[:, experts, :],
                             A[name].rearrange("e c h -> c e h")[:, experts, :]).then_inc(s_wffn, 16)
            if j == 5:
                for e in (2 * point, 2 * point + 1):
                    sp.dma_start(wd[:, e * HID:(e + 1) * HID].rearrange("p (k d) -> p k d", k=HB),
                                 A["L0_ffn_Wd"][e].rearrange("(k p) d -> p k d", p=P)).then_inc(s_wffn, 16)
            if j == 6:
                done = LB.s["w"] if point < 2 else LB.s["w_vo"]
                lo, hi = point * D, (point + 1) * D
                w = A["L0_attn_b_W_proj"] if point == 3 else A["L0_attn_b_W_qkv"][:, lo:hi]
                b = A["L0_attn_b_b_proj"] if point == 3 else A["L0_attn_b_b_qkv"][lo:hi]
                sp.dma_start(LB.w_in[:, point, :], w).then_inc(done, 16)
                sp.dma_start(LB.b_in[0:1, point, :], b.rearrange("(a n) -> a n", a=1)).then_inc(done, 16)
                if point == 0:
                    sp.dma_start(wr[:], A["L0_ffn_Wr"]).then_inc(s_wffn, 16)
            if j in (16, 17):
                sp.wait_ge(s_zero, 1)
                t0, t1 = (NT * point // 4, NT * (point + 1) // 4)
                sp.dma_start(xg[j - 16].rearrange("(t p) d -> p t d", p=P)[:, t0:t1, :],
                             zero[:].unsqueeze(1).to_broadcast([P, t1 - t0, D])).then_inc(s_zfill, 16)

        def pe_beside(l):
            L, n = (LA, LB)[l], 2 * l

            def hook(pe, j, h):
                if j == 1 and h == 15:
                    pe.wait_ge(L.s["w_vo"], 64)
                if j == 17 and 2 <= h < 6:
                    if h == 2:
                        pe.wait_ge(s_wffn, 16 * 17)
                        pe.wait_ge(s_half, 4)
                        pe.wait_ge(L.s["v"], B - 1)
                        if l == 1:
                            pe.wait_ge(L.s["bc"], 2 * B)
                    pe_tokens(pe, n, h - 2)
                if j == 17 and h == 7:
                    for i in range(4):
                        pe_logits(pe, n, i)
                if j == 17 and h == 8:
                    pe.wait_ge(r_sem["lg"], n + 1)
                if j == 17 and h == 11:
                    pe.wait_ge(L.s["m2"], 2 * B - 1)
                    pe_counts(pe, n)
                    pe.wait_ge(r_sem["cnt"], n + 1)
                if j == 19 and h in (0, 2, 4):
                    if h == 0:
                        pe.wait_ge(L.s["v"], B)
                    pe_tokens(pe, n + 1, h // 2)
                if j == 19 and h in (3, 6, 9):
                    if h == 3:
                        pe.wait_ge(L.s["oT"], 2 * B - 1)
                    pe_logits(pe, n + 1, h // 3 - 1)
                if l == 0 and j == 19 and h == 10:
                    pe.wait_ge(r_sem["slots"], 2)
                    pe_setup(pe, LB)
            return hook

        def act_beside(l):
            def hook(act, j, h):
                if j == 17 and 3 <= h < 7:
                    act_tokens(act, 2 * l, h - 3)
                if j == 17 and h == 11:
                    act_weights(act, 2 * l)
                if j == 19 and h in (1, 3, 5):
                    act_tokens(act, 2 * l + 1, h // 2)
                if l == 0 and j == 19 and h == 14:
                    act_setup(act, LB)
            return hook

        def dve_beside(l):
            n = 2 * l

            def hook(dve, j, h):
                if l == 0 and j == 1 and h == 15:
                    dve.wait_ge(s_xrest, 16)
                    dve_ln_stats(dve, 4, GBLK, s_lnA)
                    dve.wait_ge(s_lnA, 2)
                if l == 0 and j == 2:
                    dve_ln_at(dve, h, GBLK, s_lnA, 3)
                if l == 0 and j == 1 and h == 15:
                    dve.wait_ge(s_mset, 2 * RING)
                    nc.vector.memset(half[0:1, 0, :], -0.5).then_inc(s_half, 1)
                    nc.vector.memset(half[0:1, 1, :], 1.5).then_inc(s_half, 1)
                    dve.wait_ge(s_cst, 16)
                    nc.vector.memset(onesb[:], 1.0).then_inc(s_half, 1)
                    nc.vector.tensor_copy(triu[:], cst[:, CST_TRIU:CST_TRIU + P]).then_inc(s_half, 1)
                if l == 1 and (j, h) in ((3, 7), (4, 7), (5, 7), (6, 0)):
                    dve_combine_1(dve, 1, j - 3)
                if l == 1 and j == 6:
                    dve_ln_at(dve, h, GBLK, s_lnB, 2)
                if j == 16:
                    if h == 0:
                        dve.wait_ge((LA, LB)[l].s["x1"], GBLK)
                    dve_ln_at(dve, h, 0, s_ln[n], 1)
                    if 11 <= h < 15:
                        dve_tokens(dve, n, 4 * (h - 11), 4 * (h - 10))
                if j == 17 and h in (8, 9):
                    dve_route_part(dve, n, h - 8)
                if j == 17 and h == 11:
                    dve_counts(dve, n)
                if j == 17 and h == 12:
                    dve_route_part(dve, n, 2)
                if j == 17 and 13 <= h < 16:
                    dve_route_part(dve, n, h - 10)
                if j == 18 and h < 2:
                    dve_route_part(dve, n, h + 6)
                if j == 18 and h in (6, 8):
                    if h == 6:
                        dve.wait_ge((LA, LB)[l].s["x1"], NBLK - 4)
                        dve_ln_stats(dve, GBLK, NBLK - 4, s_ln[n + 1])
                        dve.wait_ge(s_ln[n + 1], 1)
                    else:
                        dve_tokens(dve, n + 1, GBLK, NBLK - 4)
                if l == 0 and j == 18 and h == 15:
                    dve_setup(dve, LB)
            return hook

        LA.sp_hook = sp_beside
        for l, L in enumerate((LA, LB)):
            L.pe_hook, L.act_hook, L.dve_hook, L.pool_hook = pe_beside(l), act_beside(l), dve_beside(l), pool_beside(l)

        def dve_ln_tail(dve, l, i):
            if i == 0:
                dve.wait_ge(r_sem["x"], 2 * GBLK * (2 * l + 1))
            if i < 3:
                for h in ((0, 1, 2, 3, 4), (5, 6, 7, 8), (9, 10))[i]:
                    dve_ln_at(dve, h, 0, s_lnB, 1)

        @block.sync
        def _(sp):
            sp.dma_start(x[:, 0:4, :], x_dram[:, 0:4, :]).then_inc(s_xin, 16)
            load_layer(sp, LA, [A["L0_attn_a_w" + c] for c in "qkvo"], [A["L0_attn_a_b" + c] for c in "qkvo"])
            sp.dma_start(x[:, 4:, :], x_dram[:, 4:, :]).then_inc(s_xrest, 16)
            sp.dma_start(cst[:], A["const"]).then_inc(s_cst, 16)
            pipeline(sp_step, sp, LA)
            sp_ffn(sp, 0)
            pipeline(sp_step, sp, LB)
            sp_ffn(sp, 1)
            sp.wait_ge(r_sem["x"], 2 * GBLK * 3)
            sp.dma_start(out_dram[:, 0:GBLK, :], x[:, 0:GBLK, :]).then_inc(s_out, 16)
            for q in range(4):
                lo = GBLK + 4 * q
                sp.wait_ge(r_sem["x"], 2 * GBLK * 3 + 8 * (q + 1))
                sp.dma_start(out_dram[:, lo:lo + 4, :], x[:, lo:lo + 4, :]).then_inc(s_out, 16)
            sp.wait_ge(s_out, 16 * 5)

        @block.gpsimd
        def _(pool):
            nc.gpsimd.memset(ident[:], 0.0).then_inc(s_const, 1)
            nc.gpsimd.memset(trib[:], 0.0).then_inc(s_const, 1)
            nc.gpsimd.memset(tick[:], 0.0).then_inc(s_const, 1)
            pool.wait_ge(s_const, 3)
            nc.gpsimd.affine_select(out=ident[:], in_=ident[:], compare_op=ALU.not_equal, fill=1.0, base=0,
                                    pattern=[[-1, P]], channel_multiplier=1).then_inc(s_const, 1)
            nc.gpsimd.affine_select(out=trib[:], in_=trib[:], compare_op=ALU.is_ge, fill=NEG, base=0,
                                    pattern=[[-1, P]], channel_multiplier=1).then_inc(s_const, 1)
            for r in range(RING):
                if r == 0:
                    nc.gpsimd.memset(zero[:], 0.0).then_inc(s_zero, 1)
                ins = nc.gpsimd.memset(kst[r][:], -1.0)
            for r in range(RING):
                nc.gpsimd.memset(vp[r][:], 0.0).then_inc(s_mset, 1)
            pool.wait_ge(s_mset, RING)
            for r in range(RING):
                nc.gpsimd.memset(vp[r][:, :, :, HD:HD + 1], 1.0).then_inc(s_mset, 1)
            pipeline(pool_step, pool, LA)
            pool_scatter(pool, 0, range(17, 2 * GBLK))
            pool_scatter(pool, 1, range(2 * GBLK))
            pool_gather(pool, 0, range(4))
            pool.wait_ge(s_half, 2)
            pipeline(pool_step, pool, LB)
            pool_scatter(pool, 2, range(17, 2 * GBLK))
            pool_scatter(pool, 3, range(2 * GBLK))
            pool_gather(pool, 2, range(4))
            pool_gather(pool, 3, range(4))

        @block.scalar
        def _(act):
            act_setup(act, LA)
            pipeline(act_step, act, LA)
            for l in range(2):
                layer_over(act, (LA, LB)[l])
                act_route(act, 2 * l + 1)
                tile_loop(act_tile, act, l)
                if l == 0:
                    ffn_over(act, 0)
                    act.wait_ge(r_sem["x"], 2 * GBLK)
                    pipeline(act_step, act, LB)

        @block.vector
        def _(dve):
            nc.vector.memset(ones_row[:], 1.0).then_inc(s_const_dve, 1)
            dve.wait_ge(s_xin, 16)
            dve_ln_stats(dve, 0, 4, s_lnA)
            dve.wait_ge(s_lnA, 1)
            dve.wait_ge(s_const, 5)
            nc.vector.tensor_copy(identb[:], ident[:]).then_inc(s_const_dve, 1)
            dve_setup(dve, LA)
            pipeline(dve_step, dve, LA)
            for l in range(2):
                layer_over(dve, (LA, LB)[l])
                n = 2 * l + 1
                dve_ln_stats(dve, NBLK - 4, NBLK, s_ln[n])
                dve.wait_ge(s_ln[n], 2)
                dve_tokens(dve, n, NBLK - 4, NBLK)
                dve_route(dve, n)

                def gathered():
                    for q in range(4):
                        dve.wait_ge(r_gat[0][q], 16 * 8 * (l + 1))

                tile_loop(dve_tile, dve, l, window=gathered, between=dve_combine_0,
                          last=dve_ln_tail if l == 0 else None)
                if l == 0:
                    pipeline(dve_step, dve, LB)
            for q in range(4):
                dve_combine_1(dve, 3, q)

        @block.tensor
        def _(pe):
            pe.wait_ge(s_const, 5)
            pe_setup(pe, LA)
            pipeline(pe_step, pe, LA)
            for l in range(2):
                layer_over(pe, (LA, LB)[l])
                pe.wait_ge(r_sem["slots"], 4 * l + 2)
                pe.wait_ge(LB.s["bcol"], 1)
                pe_route(pe, 2 * l + 1)
                tile_loop(pe_tile, pe, l, second=lambda: pe.wait_ge(r_sem["slots"], 4 * l + 4))
                if l == 0:
                    ffn_over(pe, 0)
                    pipeline(pe_step, pe, LB)


def constants():
    import numpy as np
    c = np.zeros((P, CST_COLS), np.float32)
    c[:, CST_DESC:CST_DESC + E] = E - np.arange(E)
    c[:, CST_TILE:CST_TILE + NT] = P * np.arange(NT)
    p = np.arange(P)
    c[:, CST_HEAD:CST_HEAD + P] = p[:, None] // HD == p[None, :] // HD
    c[:, CST_TRIU:CST_TRIU + P] = p[:, None] < p[None, :]
    return c


_INS = ['L0_attn_a_x', 'L0_attn_a_wq', 'L0_attn_a_bq', 'L0_attn_a_wk', 'L0_attn_a_bk', 'L0_attn_a_wv',
        'L0_attn_a_bv', 'L0_attn_a_wo', 'L0_attn_a_bo', 'L0_attn_b_W_qkv', 'L0_attn_b_b_qkv',
        'L0_attn_b_W_proj', 'L0_attn_b_b_proj', 'L0_ffn_Wr', 'L0_ffn_Wg', 'L0_ffn_Wu', 'L0_ffn_Wd']
_OUTS = [((16, 256, 128), 'float32')]


def kernel(**inputs):
    import numpy as _np
    import concourse.bacc as _bacc
    from concourse import mybir as _mybir
    from concourse.bass_utils import run_bass_kernel_spmd as _run

    nc = _bacc.Bacc("TRN2", target_bir_lowering=False, num_devices=1)
    arrays, args = {}, {}
    for name in _INS:
        a = _np.ascontiguousarray(inputs[name])
        arrays[f"in_{name}"] = a
        args[name] = nc.dram_tensor(f"in_{name}", a.shape, _mybir.dt.from_np(a.dtype), kind="ExternalInput").ap()
    arrays["in_const"] = constants()
    args["const"] = nc.dram_tensor("in_const", (P, CST_COLS), F32, kind="ExternalInput").ap()
    shape, dtype = _OUTS[0]
    out = nc.dram_tensor("out_0", shape, _mybir.dt.from_np(_np.dtype(dtype)), kind="ExternalOutput").ap()
    build(nc, args, out)
    r = _run(nc, [arrays], core_ids=[0])
    return r.results[0]["out_0"]
```
